# Optimizing a Trainium2 kernel written in Bass

```python
import numpy as np
import jax
import jax.numpy as jnp

def _softmax(x, axis=-1):
    return jax.nn.softmax(x, axis=axis)

def _gelu(x):
    return jax.nn.gelu(x, approximate=True)

def _silu(x):
    return jax.nn.silu(x)

def _sigmoid(x):
    return jax.nn.sigmoid(x)

def _layernorm(x, axis=-1, eps=1e-05):
    m = jnp.mean(x, axis=axis, keepdims=True)
    v = jnp.var(x, axis=axis, keepdims=True)
    return (x - m) / jnp.sqrt(v + eps)

def _scatter_add(tgt, idx, src, axis=0):
    return tgt.at[idx].add(src)

def _segment_sum(src, seg, n):
    return jax.ops.segment_sum(src, seg, n)
kernel_name = 'mk_prb_d2_jaxref_r8_45b87c'

def setup_inputs(seed: int=0):
    np.random.seed(seed)
    _w = jnp.asarray

    def _L0_attn_setup():
        import math
        import jax, jax.numpy as jnp
        import numpy as np
        D_MODEL = 128
        HEADS = 16
        DH = D_MODEL // HEADS
        MAX_REL = 128
        LN_EPS = 1e-05

        def _layernorm(x, gamma, beta):
            mu = jnp.mean(x, axis=-1, keepdims=True)
            var = jnp.mean(jnp.square(x - mu), axis=-1, keepdims=True)
            return (x - mu) * jax.lax.rsqrt(var + LN_EPS) * gamma + beta
        key = jax.random.key(seed)
        ks = jax.random.split(key, 6)
        B, T = (4, 256)
        scale = 1.0 / math.sqrt(D_MODEL)
        x = jax.random.normal(ks[0], (B, T, D_MODEL), dtype=jnp.float32)
        Wq = jax.random.normal(ks[1], (D_MODEL, D_MODEL), dtype=jnp.float32) * scale
        Wk = jax.random.normal(ks[2], (D_MODEL, D_MODEL), dtype=jnp.float32) * scale
        Wv = jax.random.normal(ks[3], (D_MODEL, D_MODEL), dtype=jnp.float32) * scale
        Wo = jax.random.normal(ks[4], (D_MODEL, D_MODEL), dtype=jnp.float32) * scale
        rel = jnp.tile(jnp.linspace(0.0, -2.0, MAX_REL + 1, dtype=jnp.float32)[None, :], (HEADS, 1))
        ln_gamma = jnp.ones((D_MODEL,), dtype=jnp.float32)
        ln_beta = jnp.zeros((D_MODEL,), dtype=jnp.float32)
        return {'x': x, 'Wq': Wq, 'Wk': Wk, 'Wv': Wv, 'Wo': Wo, 'rel': rel, 'ln_gamma': ln_gamma, 'ln_beta': ln_beta}
    _L0_attn_in = _L0_attn_setup()

    def _L0_ffn_setup():
        import jax, jax.numpy as jnp
        import numpy as np
        D_MODEL = 128
        N_HEADS = 16
        HEAD_DIM = D_MODEL // N_HEADS
        KV_LATENT = 64
        N_EXPERTS = 4
        D_HIDDEN = 4 * D_MODEL
        B, T = (2, 128)

        def rmsnorm(x, w, eps=1e-06):
            return w * (x * jax.lax.rsqrt(jnp.mean(x * x, axis=-1, keepdims=True) + eps))

        def layernorm(x, g, b, eps=1e-05):
            mu = jnp.mean(x, axis=-1, keepdims=True)
            var = jnp.mean((x - mu) ** 2, axis=-1, keepdims=True)
            return (x - mu) * jax.lax.rsqrt(var + eps) * g + b

        def apply_rope(x):
            t, d = (x.shape[2], x.shape[3])
            half = d // 2
            pos = jnp.arange(t, dtype=x.dtype)[:, None]
            inv_freq = 1.0 / 10000.0 ** (jnp.arange(half, dtype=x.dtype) / half)
            ang = pos * inv_freq[None, :]
            sin, cos = (jnp.sin(ang), jnp.cos(ang))
            x1, x2 = (x[..., :half], x[..., half:])
            return jnp.concatenate([x1 * cos - x2 * sin, x1 * sin + x2 * cos], axis=-1)

        def mla_attention(x, Wq, Wdkv, Wuk, Wuv, Wo, ln_g, ln_b):
            b, t, _ = x.shape
            q = (x @ Wq.T).reshape(b, t, N_HEADS, HEAD_DIM).transpose(0, 2, 1, 3)
            latent = layernorm(x @ Wdkv.T, ln_g, ln_b)
            k = (latent @ Wuk.T).reshape(b, t, N_HEADS, HEAD_DIM).transpose(0, 2, 1, 3)
            v = (latent @ Wuv.T).reshape(b, t, N_HEADS, HEAD_DIM).transpose(0, 2, 1, 3)
            q = apply_rope(q)
            k = apply_rope(k)
            scores = jnp.einsum('bhqd,bhkd->bhqk', q, k) / np.sqrt(HEAD_DIM)
            causal = jnp.tril(jnp.ones((t, t), dtype=bool))
            scores = jnp.where(causal, scores, -jnp.inf)
            attn = jax.nn.softmax(scores, axis=-1)
            out = jnp.einsum('bhqk,bhkd->bhqd', attn, v).transpose(0, 2, 1, 3).reshape(b, t, D_MODEL)
            return out @ Wo.T

        def moe(x, gate_w, gate_b, W1, b1, W2, b2):
            logits = x @ gate_w.T + gate_b
            top = jnp.argmax(logits, axis=-1)
            onehot = jax.nn.one_hot(top, N_EXPERTS, dtype=x.dtype)
            h = jax.nn.relu(jnp.einsum('btd,ehd->bteh', x, W1) + b1)
            y = jnp.einsum('bteh,edh->bted', h, W2) + b2
            return jnp.einsum('bted,bte->btd', y, onehot)
        key = jax.random.key(seed)
        ks = jax.random.split(key, 16)
        s = lambda fan_in: 1.0 / np.sqrt(fan_in)
        return {'x': jax.random.normal(ks[0], (B, T, D_MODEL), jnp.float32), 'norm1_w': jnp.ones((D_MODEL,), jnp.float32), 'norm2_w': jnp.ones((D_MODEL,), jnp.float32), 'Wq': jax.random.normal(ks[1], (D_MODEL, D_MODEL), jnp.float32) * s(D_MODEL), 'Wdkv': jax.random.normal(ks[2], (KV_LATENT, D_MODEL), jnp.float32) * s(D_MODEL), 'Wuk': jax.random.normal(ks[3], (D_MODEL, KV_LATENT), jnp.float32) * s(KV_LATENT), 'Wuv': jax.random.normal(ks[4], (D_MODEL, KV_LATENT), jnp.float32) * s(KV_LATENT), 'Wo': jax.random.normal(ks[5], (D_MODEL, D_MODEL), jnp.float32) * s(D_MODEL), 'ln_g': jnp.ones((KV_LATENT,), jnp.float32), 'ln_b': jnp.zeros((KV_LATENT,), jnp.float32), 'gate_w': jax.random.normal(ks[6], (N_EXPERTS, D_MODEL), jnp.float32) * s(D_MODEL), 'gate_b': jnp.zeros((N_EXPERTS,), jnp.float32), 'W1': jax.random.normal(ks[7], (N_EXPERTS, D_HIDDEN, D_MODEL), jnp.float32) * s(D_MODEL), 'b1': jnp.zeros((N_EXPERTS, D_HIDDEN), jnp.float32), 'W2': jax.random.normal(ks[8], (N_EXPERTS, D_MODEL, D_HIDDEN), jnp.float32) * s(D_HIDDEN), 'b2': jnp.zeros((N_EXPERTS, D_MODEL), jnp.float32)}
    _L0_ffn_in = _L0_ffn_setup()

    def _L1_attn_setup():
        import jax, jax.numpy as jnp
        import numpy as np
        EPS = 1e-06
        N_HEADS = 16

        def _project_static(x):
            sp = jnp.clip(x[..., 1:], -8.0, 8.0)
            x0 = jnp.sqrt(1.0 + jnp.sum(sp * sp, axis=-1, keepdims=True) + EPS)
            return jnp.concatenate([x0, sp], axis=-1)

        def _inner_static(x, y):
            return -x[..., 0] * y[..., 0] + jnp.sum(x[..., 1:] * y[..., 1:], axis=-1)

        def _log_map_approx(x, y):
            y = _project_static(y)
            xy = _inner_static(x, y)
            xy = jnp.minimum(xy, -(1.0 + EPS))[..., None]
            d = jnp.maximum(jnp.arccosh(jnp.maximum(-xy, 1.0 + EPS)), 0.001)
            dirv = y + xy * x
            dn = jnp.sqrt(jnp.maximum(_inner_static(dirv, dirv), EPS))[..., None]
            return d * dirv / (dn + EPS)

        def _dynamic_metric(x, mu, W1, b1, W2, b2):
            d = x.shape[-1]
            eta = jnp.ones((d,), x.dtype).at[0].set(-1.0)
            v = x - mu
            h = jnp.tanh(jnp.tanh(v @ W1.T + b1) @ W2.T + b2) * 0.1
            g = eta + h
            return jnp.concatenate([-jnp.abs(g[..., :1]), jnp.abs(g[..., 1:])], axis=-1)
        key = jax.random.key(seed)
        ks = jax.random.split(key, 9)
        B, T, d = (2, 256, 128)
        s = 0.02
        return {'x': jax.random.normal(ks[0], (B, T, d), jnp.float32), 'W1': jax.random.normal(ks[1], (2 * d, d), jnp.float32) * s, 'b1': jax.random.normal(ks[2], (2 * d,), jnp.float32) * s, 'W2': jax.random.normal(ks[3], (d, 2 * d), jnp.float32) * s, 'b2': jax.random.normal(ks[4], (d,), jnp.float32) * s, 'Wq': jax.random.normal(ks[5], (d, d), jnp.float32) * s, 'Wk': jax.random.normal(ks[6], (d, d), jnp.float32) * s, 'Wv': jax.random.normal(ks[7], (d, d), jnp.float32) * s, 'Wo': jax.random.normal(ks[8], (d, d), jnp.float32) * s}
    _L1_attn_in = _L1_attn_setup()

    def _L1_ffn_setup():
        import jax, jax.numpy as jnp
        import numpy as np
        E = 32
        H = 128
        I = 64
        G = 8
        TKG = 4
        TOPK = 8
        NSH = 2
        SCALE = 2.5
        key = jax.random.key(seed)
        ks = jax.random.split(key, 10)
        s = 0.02
        return {'hidden_states': jax.random.normal(ks[0], (2, 128, H), jnp.float32), 'gate_w': jax.random.normal(ks[1], (E, H), jnp.float32) * s, 'gate_bias': jax.random.normal(ks[2], (E,), jnp.float32) * s, 'w_gate': jax.random.normal(ks[3], (E, I, H), jnp.float32) * s, 'w_up': jax.random.normal(ks[4], (E, I, H), jnp.float32) * s, 'w_down': jax.random.normal(ks[5], (E, H, I), jnp.float32) * s, 'sh_gate': jax.random.normal(ks[6], (I * NSH, H), jnp.float32) * s, 'sh_up': jax.random.normal(ks[7], (I * NSH, H), jnp.float32) * s, 'sh_down': jax.random.normal(ks[8], (H, I * NSH), jnp.float32) * s}
    _L1_ffn_in = _L1_ffn_setup()
    _d = {'L0_attn_x': _L0_attn_in['x'], 'L0_attn_Wq': _L0_attn_in['Wq'], 'L0_attn_Wk': _L0_attn_in['Wk'], 'L0_attn_Wv': _L0_attn_in['Wv'], 'L0_attn_Wo': _L0_attn_in['Wo'], 'L0_attn_rel': _L0_attn_in['rel'], 'L0_attn_ln_gamma': _L0_attn_in['ln_gamma'], 'L0_attn_ln_beta': _L0_attn_in['ln_beta'], 'L0_ffn_norm1_w': _L0_ffn_in['norm1_w'], 'L0_ffn_norm2_w': _L0_ffn_in['norm2_w'], 'L0_ffn_Wq': _L0_ffn_in['Wq'], 'L0_ffn_Wdkv': _L0_ffn_in['Wdkv'], 'L0_ffn_Wuk': _L0_ffn_in['Wuk'], 'L0_ffn_Wuv': _L0_ffn_in['Wuv'], 'L0_ffn_Wo': _L0_ffn_in['Wo'], 'L0_ffn_ln_g': _L0_ffn_in['ln_g'], 'L0_ffn_ln_b': _L0_ffn_in['ln_b'], 'L0_ffn_gate_w': _L0_ffn_in['gate_w'], 'L0_ffn_gate_b': _L0_ffn_in['gate_b'], 'L0_ffn_W1': _L0_ffn_in['W1'], 'L0_ffn_b1': _L0_ffn_in['b1'], 'L0_ffn_W2': _L0_ffn_in['W2'], 'L0_ffn_b2': _L0_ffn_in['b2'], 'L1_attn_W1': _L1_attn_in['W1'], 'L1_attn_b1': _L1_attn_in['b1'], 'L1_attn_W2': _L1_attn_in['W2'], 'L1_attn_b2': _L1_attn_in['b2'], 'L1_attn_Wq': _L1_attn_in['Wq'], 'L1_attn_Wk': _L1_attn_in['Wk'], 'L1_attn_Wv': _L1_attn_in['Wv'], 'L1_attn_Wo': _L1_attn_in['Wo'], 'L1_ffn_gate_w': _L1_ffn_in['gate_w'], 'L1_ffn_gate_bias': _L1_ffn_in['gate_bias'], 'L1_ffn_w_gate': _L1_ffn_in['w_gate'], 'L1_ffn_w_up': _L1_ffn_in['w_up'], 'L1_ffn_w_down': _L1_ffn_in['w_down'], 'L1_ffn_sh_gate': _L1_ffn_in['sh_gate'], 'L1_ffn_sh_up': _L1_ffn_in['sh_up'], 'L1_ffn_sh_down': _L1_ffn_in['sh_down']}
    _x0 = _d['L0_attn_x']
    _d['L0_attn_x'] = jax.random.normal(jax.random.fold_in(jax.random.key(seed), 1), (16, 512, 128), dtype=_x0.dtype)
    del _x0
    return _d

def reference(L0_attn_x, L0_attn_Wq, L0_attn_Wk, L0_attn_Wv, L0_attn_Wo, L0_attn_rel, L0_attn_ln_gamma, L0_attn_ln_beta, L0_ffn_norm1_w, L0_ffn_norm2_w, L0_ffn_Wq, L0_ffn_Wdkv, L0_ffn_Wuk, L0_ffn_Wuv, L0_ffn_Wo, L0_ffn_ln_g, L0_ffn_ln_b, L0_ffn_gate_w, L0_ffn_gate_b, L0_ffn_W1, L0_ffn_b1, L0_ffn_W2, L0_ffn_b2, L1_attn_W1, L1_attn_b1, L1_attn_W2, L1_attn_b2, L1_attn_Wq, L1_attn_Wk, L1_attn_Wv, L1_attn_Wo, L1_ffn_gate_w, L1_ffn_gate_bias, L1_ffn_w_gate, L1_ffn_w_up, L1_ffn_w_down, L1_ffn_sh_gate, L1_ffn_sh_up, L1_ffn_sh_down):

    def _L0_attn_ref(x, Wq, Wk, Wv, Wo, rel, ln_gamma, ln_beta):
        import math
        import jax, jax.numpy as jnp
        import numpy as np
        D_MODEL = 128
        HEADS = 16
        DH = D_MODEL // HEADS
        MAX_REL = 128
        LN_EPS = 1e-05

        def _layernorm(x, gamma, beta):
            mu = jnp.mean(x, axis=-1, keepdims=True)
            var = jnp.mean(jnp.square(x - mu), axis=-1, keepdims=True)
            return (x - mu) * jax.lax.rsqrt(var + LN_EPS) * gamma + beta
        B, T, D = x.shape
        x0 = x
        xn = _layernorm(x, ln_gamma, ln_beta)

        def proj(W):
            return (xn @ W.T).reshape(B, T, HEADS, DH).transpose(0, 2, 1, 3)
        q = proj(Wq) / math.sqrt(DH)
        k = proj(Wk)
        v = proj(Wv)
        scores = jnp.einsum('bhid,bhjd->bhij', q, k)
        i = jnp.arange(T)
        dist = jnp.clip(i[:, None] - i[None, :], 0, MAX_REL)
        bias = rel[:, dist]
        scores = scores + bias[None]
        causal = i[:, None] >= i[None, :]
        scores = jnp.where(causal[None, None], scores, -jnp.inf)
        attn = jax.nn.softmax(scores, axis=-1)
        y = jnp.einsum('bhij,bhjd->bhid', attn, v)
        y = y.transpose(0, 2, 1, 3).reshape(B, T, D)
        y = y @ Wo.T
        return x0 + y

    def _L0_ffn_ref(x, norm1_w, norm2_w, Wq, Wdkv, Wuk, Wuv, Wo, ln_g, ln_b, gate_w, gate_b, W1, b1, W2, b2):
        import jax, jax.numpy as jnp
        import numpy as np
        D_MODEL = 128
        N_HEADS = 16
        HEAD_DIM = D_MODEL // N_HEADS
        KV_LATENT = 64
        N_EXPERTS = 4
        D_HIDDEN = 4 * D_MODEL
        B, T = (2, 128)

        def rmsnorm(x, w, eps=1e-06):
            return w * (x * jax.lax.rsqrt(jnp.mean(x * x, axis=-1, keepdims=True) + eps))

        def layernorm(x, g, b, eps=1e-05):
            mu = jnp.mean(x, axis=-1, keepdims=True)
            var = jnp.mean((x - mu) ** 2, axis=-1, keepdims=True)
            return (x - mu) * jax.lax.rsqrt(var + eps) * g + b

        def apply_rope(x):
            t, d = (x.shape[2], x.shape[3])
            half = d // 2
            pos = jnp.arange(t, dtype=x.dtype)[:, None]
            inv_freq = 1.0 / 10000.0 ** (jnp.arange(half, dtype=x.dtype) / half)
            ang = pos * inv_freq[None, :]
            sin, cos = (jnp.sin(ang), jnp.cos(ang))
            x1, x2 = (x[..., :half], x[..., half:])
            return jnp.concatenate([x1 * cos - x2 * sin, x1 * sin + x2 * cos], axis=-1)

        def mla_attention(x, Wq, Wdkv, Wuk, Wuv, Wo, ln_g, ln_b):
            b, t, _ = x.shape
            q = (x @ Wq.T).reshape(b, t, N_HEADS, HEAD_DIM).transpose(0, 2, 1, 3)
            latent = layernorm(x @ Wdkv.T, ln_g, ln_b)
            k = (latent @ Wuk.T).reshape(b, t, N_HEADS, HEAD_DIM).transpose(0, 2, 1, 3)
            v = (latent @ Wuv.T).reshape(b, t, N_HEADS, HEAD_DIM).transpose(0, 2, 1, 3)
            q = apply_rope(q)
            k = apply_rope(k)
            scores = jnp.einsum('bhqd,bhkd->bhqk', q, k) / np.sqrt(HEAD_DIM)
            causal = jnp.tril(jnp.ones((t, t), dtype=bool))
            scores = jnp.where(causal, scores, -jnp.inf)
            attn = jax.nn.softmax(scores, axis=-1)
            out = jnp.einsum('bhqk,bhkd->bhqd', attn, v).transpose(0, 2, 1, 3).reshape(b, t, D_MODEL)
            return out @ Wo.T

        def moe(x, gate_w, gate_b, W1, b1, W2, b2):
            logits = x @ gate_w.T + gate_b
            top = jnp.argmax(logits, axis=-1)
            onehot = jax.nn.one_hot(top, N_EXPERTS, dtype=x.dtype)
            h = jax.nn.relu(jnp.einsum('btd,ehd->bteh', x, W1) + b1)
            y = jnp.einsum('bteh,edh->bted', h, W2) + b2
            return jnp.einsum('bted,bte->btd', y, onehot)
        x = x + mla_attention(rmsnorm(x, norm1_w), Wq, Wdkv, Wuk, Wuv, Wo, ln_g, ln_b)
        x = x + moe(rmsnorm(x, norm2_w), gate_w, gate_b, W1, b1, W2, b2)
        return x

    def _L1_attn_ref(x, W1, b1, W2, b2, Wq, Wk, Wv, Wo):
        import jax, jax.numpy as jnp
        import numpy as np
        EPS = 1e-06
        N_HEADS = 16

        def _project_static(x):
            sp = jnp.clip(x[..., 1:], -8.0, 8.0)
            x0 = jnp.sqrt(1.0 + jnp.sum(sp * sp, axis=-1, keepdims=True) + EPS)
            return jnp.concatenate([x0, sp], axis=-1)

        def _inner_static(x, y):
            return -x[..., 0] * y[..., 0] + jnp.sum(x[..., 1:] * y[..., 1:], axis=-1)

        def _log_map_approx(x, y):
            y = _project_static(y)
            xy = _inner_static(x, y)
            xy = jnp.minimum(xy, -(1.0 + EPS))[..., None]
            d = jnp.maximum(jnp.arccosh(jnp.maximum(-xy, 1.0 + EPS)), 0.001)
            dirv = y + xy * x
            dn = jnp.sqrt(jnp.maximum(_inner_static(dirv, dirv), EPS))[..., None]
            return d * dirv / (dn + EPS)

        def _dynamic_metric(x, mu, W1, b1, W2, b2):
            d = x.shape[-1]
            eta = jnp.ones((d,), x.dtype).at[0].set(-1.0)
            v = x - mu
            h = jnp.tanh(jnp.tanh(v @ W1.T + b1) @ W2.T + b2) * 0.1
            g = eta + h
            return jnp.concatenate([-jnp.abs(g[..., :1]), jnp.abs(g[..., 1:])], axis=-1)
        B, T, d = x.shape
        h, dh = (N_HEADS, d // N_HEADS)
        mu = jnp.zeros((d,), x.dtype).at[0].set(1.0)
        mu = jnp.broadcast_to(mu, (B, T, d))
        v = _log_map_approx(mu, x)
        q = (v @ Wq.T).reshape(B, T, h, dh).transpose(0, 2, 1, 3)
        k = (v @ Wk.T).reshape(B, T, h, dh).transpose(0, 2, 1, 3)
        vv = (v @ Wv.T).reshape(B, T, h, dh).transpose(0, 2, 1, 3)
        g_x = _dynamic_metric(x, mu, W1, b1, W2, b2)
        gh = g_x.reshape(B, T, h, dh).transpose(0, 2, 1, 3)
        sc = jnp.einsum('bhqd,bhkd->bhqk', q * gh, k) / jnp.sqrt(jnp.asarray(dh, x.dtype))
        at = jax.nn.softmax(sc, axis=-1)
        out = jnp.einsum('bhqk,bhkd->bhqd', at, vv).transpose(0, 2, 1, 3).reshape(B, T, d)
        out = out @ Wo.T
        return _project_static(_project_static(mu) + out * 0.1)

    def _L1_ffn_ref(hidden_states, gate_w, gate_bias, w_gate, w_up, w_down, sh_gate, sh_up, sh_down):
        import jax, jax.numpy as jnp
        import numpy as np
        E = 32
        H = 128
        I = 64
        G = 8
        TKG = 4
        TOPK = 8
        NSH = 2
        SCALE = 2.5
        B, S, Hd = hidden_states.shape
        h = hidden_states.reshape(-1, Hd)
        logits = h.astype(jnp.float32) @ gate_w.T
        scores = jax.nn.sigmoid(logits)
        sc = scores + gate_bias
        grp = sc.reshape(-1, G, E // G)
        group_scores = jax.lax.top_k(grp, 2)[0].sum(-1)
        gidx = jax.lax.top_k(group_scores, TKG)[1]
        gmask = jnp.sum(jax.nn.one_hot(gidx, G, dtype=sc.dtype), axis=1)
        smask = jnp.repeat(gmask, E // G, axis=1)
        masked = jnp.where(smask > 0, sc, jnp.zeros_like(sc))
        tki = jax.lax.top_k(masked, TOPK)[1]
        tkw = jnp.take_along_axis(scores, tki, axis=1)
        tkw = tkw / (tkw.sum(-1, keepdims=True) + 1e-20)
        tkw = tkw * SCALE
        combine = (jax.nn.one_hot(tki, E, dtype=tkw.dtype) * tkw[..., None]).sum(1)
        g = jax.nn.silu(jnp.einsum('th,eih->tei', h, w_gate))
        u = jnp.einsum('th,eih->tei', h, w_up)
        routed = jnp.einsum('tei,ehi->th', g * u * combine[:, :, None], w_down)
        sg = jax.nn.silu(h @ sh_gate.T)
        shared = sg * (h @ sh_up.T) @ sh_down.T
        return (routed + shared).reshape(B, S, Hd)
    x = L0_attn_x
    xn = _layernorm(x, axis=-1)
    x = x + _L0_attn_ref(xn, L0_attn_Wq, L0_attn_Wk, L0_attn_Wv, L0_attn_Wo, L0_attn_rel, L0_attn_ln_gamma, L0_attn_ln_beta) + _L0_ffn_ref(xn, L0_ffn_norm1_w, L0_ffn_norm2_w, L0_ffn_Wq, L0_ffn_Wdkv, L0_ffn_Wuk, L0_ffn_Wuv, L0_ffn_Wo, L0_ffn_ln_g, L0_ffn_ln_b, L0_ffn_gate_w, L0_ffn_gate_b, L0_ffn_W1, L0_ffn_b1, L0_ffn_W2, L0_ffn_b2)
    xn = _layernorm(x, axis=-1)
    x = x + _L1_attn_ref(xn, L1_attn_W1, L1_attn_b1, L1_attn_W2, L1_attn_b2, L1_attn_Wq, L1_attn_Wk, L1_attn_Wv, L1_attn_Wo) + _L1_ffn_ref(xn, L1_ffn_gate_w, L1_ffn_gate_bias, L1_ffn_w_gate, L1_ffn_w_up, L1_ffn_w_down, L1_ffn_sh_gate, L1_ffn_sh_up, L1_ffn_sh_down)
    return x

_drawn_inputs = setup_inputs


def setup_inputs(seed=0):
    import zlib

    import numpy as np

    out = dict(_drawn_inputs(seed))
    spreads = {'L0_attn_ln_gamma': (1.0, 0.6),
     'L0_attn_ln_beta': (0.0, 0.1),
     'L0_ffn_norm1_w': (1.0, 0.2),
     'L0_ffn_norm2_w': (1.0, 0.2),
     'L0_ffn_ln_g': (1.0, 0.2),
     'L0_ffn_ln_b': (0.0, 0.1),
     'L0_ffn_gate_b': (0.0, 0.1),
     'L0_ffn_b1': (0.0, 0.36),
     'L0_ffn_b2': (0.0, 0.1)}
    factors = {'L1_attn_W1': 64.0,
     'L1_attn_b1': 64.0,
     'L1_attn_W2': 64.0,
     'L1_attn_b2': 64.0,
     'L1_attn_Wq': 64.0,
     'L1_attn_Wk': 64.0,
     'L1_attn_Wv': 64.0,
     'L1_attn_Wo': 64.0,
     'L1_ffn_gate_w': 8.0,
     'L1_ffn_gate_bias': 8.0,
     'L1_ffn_w_gate': 8.0,
     'L1_ffn_w_up': 8.0,
     'L1_ffn_w_down': 8.0,
     'L1_ffn_sh_gate': 8.0,
     'L1_ffn_sh_up': 8.0,
     'L1_ffn_sh_down': 8.0}
    for name, (base, spread) in spreads.items():
        noise = np.random.default_rng([zlib.crc32(name.encode()), seed]).standard_normal(out[name].shape)
        drawn = base * np.exp(spread * noise) if base else spread * noise
        out[name] = jnp.asarray(drawn.astype(out[name].dtype))
    for name, factor in factors.items():
        out[name] = (out[name] * factor).astype(out[name].dtype)
    return out
```

```python
import concourse.bass as bass
from concourse import mybir
from contextlib import ExitStack
import numpy as np

F32 = mybir.dt.float32
BF16 = mybir.dt.bfloat16
ALU = mybir.AluOpType
ACT = mybir.ActivationFunctionType
AX = mybir.AxisListType

T, D, H, DH = 512, 128, 16, 8
TT = T // 128
HID0, E0 = 2048, 4
E1, TOPK, GROUPS, TOPG = 32, 8, 8, 4
HT = HID0 // 128
MASKED = -1e30
CONSTANTS = [-0.5, 0.5, 1e-5, 1e-6, 1.0, -1.0, 1.0 / D]
RSQ8 = float(1.0 / np.sqrt(8.0))

UNITS = [(a, half) for a in range(3) for half in range(2)]
CAUSAL_STEPS = [[(0, 0)], [(1, 0), (3, 384)], [(2, 0)]]
FULL_STEPS = [[(k, 0)] for k in range(4)]


def steps_of(a):
    return FULL_STEPS if a == 2 else CAUSAL_STEPS


def first_query(a, kt):
    return 0 if a == 2 else 128 * kt


def step_width(a, s):
    return sum(T - first_query(a, kt) for kt, _ in steps_of(a)[s])


def max_items(u):
    return [("mx", u, hl, qt) for hl in range(8) for qt in range(TT)]


def exp_items(u):
    s_n = len(steps_of(UNITS[u][0]))
    out = []
    for n in range(2 * s_n):
        out += [("st", u, n // s_n, pair, n % s_n) for pair in range(2)]
        if n >= 2 and (n - 1) % s_n == 0:
            out.append(("fin", u, (n - 2) // s_n))
        if n >= 1:
            out.append(("pv", u, (n - 1) // s_n, (n - 1) % s_n))
    return out + [("pv", u, 1, s_n - 1), ("fin", u, 1)]


def merged(exps, maxes, lead):
    out, m = list(exps[:lead]), 0
    rest = exps[lead:]
    for n, item in enumerate(rest):
        out.append(item)
        upto = (n + 1) * len(maxes) // len(rest)
        out += maxes[m:upto]
        m = upto
    return out


SEGMENTS = [
    max_items(0),
    max_items(1)[:6] + [("mrow", 0)] + merged(exp_items(0), max_items(1)[6:], 0),
    [("mrow", 1)] + merged(exp_items(1), max_items(2), 4),
    [("woT", 0), ("wo", 0), ("mrow", 2)] + merged(exp_items(2), max_items(3), 2),
    [("mrow", 3)] + exp_items(3) + [("woT", 1), ("wo", 1)],
    max_items(4),
    max_items(5)[:6] + [("mrow", 4)] + merged(exp_items(4), max_items(5)[6:], 0),
    [("mrow", 5)] + exp_items(5) + [("woT", 2), ("wo", 2)],
]


def uses_of(kinds, segments):
    return [i for k in segments for i in SEGMENTS[k] if i[0] in kinds]


RING = (["zT", "qk0", "v0", "q1", "k1", "v1"] + uses_of(["st"], range(5))
        + [("moe0", n) for n in range(HT // 2)] + ["hT", "hid", "met", "qk2", "v2"]
        + uses_of(["st"], range(5, 8)) + [("moe1", n) for n in range(HT + 1)])
ROWMAX = uses_of(["mx"], range(8)) + [("comb", n) for n in range(HT)]
SMALL = (["latT"] + uses_of(["fin", "mrow", "woT", "wo"], range(5)) + ["z2T", "gate0", "ohT", "y0"]
         + uses_of(["fin", "mrow", "woT", "wo"], range(5, 8)) + ["gate1", "combT", "y1"])
PVS = (uses_of(["pv"], range(5)), uses_of(["pv"], range(5, 8)))
PV = [("quad", u, g) for u in range(4) for g in range(2)] + ["down0"] \
    + [("quad", u, g) for u in (4, 5) for g in range(2)] + ["down1"]
PROBS = (uses_of(["st"], range(5)) + [("moe0", n) for n in range(HT // 2)]
         + uses_of(["st"], range(5, 8)) + [("moe1", n) for n in range(HT + 1)])

RI, MI, SI, PI, QI = ({k: n for n, k in enumerate(x)} for x in (RING, ROWMAX, SMALL, PV, PROBS))

PER = dict(
    ring_full=len(RING), ring_free0=2 * ((len(RING) + 1) // 2), ring_free1=2 * (len(RING) // 2),
    max_full=len(ROWMAX), max_free0=(len(ROWMAX) + 1) // 2, max_free1=len(ROWMAX) // 2,
    small_full=len(SMALL), small_free=len(SMALL), pv_full=len(PV), pv_free=len(PV),
    probs_used=len(PROBS), x_in=16, out_done=16, stats=3, rstd=4, xn=2, za=1, zb=1,
    hi=6, parts=6, scr_w=3 * 6 * 16, stk0=3 * 14 * 16, stk1=3 * 14 * 16, nmax0=3 * 64, nmax1=3 * 64,
    nmax_parts=6, roped=2, acc=2, ssq=2, z2=1, onehot=1, squares=1, vrow=1,
    logm=2, lns=1, metric=1, x0=1, comb=1, comb_hi=1, combS=1, silu=HT + 1, dve=55, pool=35,
)

PRIMED = ("ring_full", "ring_free0", "ring_free1", "max_free0", "max_free1", "small_free", "pv_free",
          "probs_used")


def layers_kernel(nc, batches, x, out, w0, w1, w1k, w2, m0_up, m0_down, m0_b2, m0_gate, m1_gate_w,
                  m1_up_w, m1_down_w, m1_shared, m1_router, cols, rows, rel_t, rel_s, mask_t, mask_s,
                  causal_t, causal_s, rope_cos, rope_sin, eye, eye_b, pick0, pick1, ones2, zeros2, per):
    counted = {}
    scr = nc.dram_tensor("scratch_parts", (3, 2, H, 3, DH, T), BF16, kind="Internal").ap()
    ctx = ExitStack()
    with ctx:
        def sb(name, shape, dt=F32):
            return ctx.enter_context(nc.sbuf_tensor(name, shape, dt))

        W0 = sb("W0", [128, 4, 128])
        W1 = sb("W1", [128, 448])
        W1k = sb("W1k", [64, 3, 128])
        W2 = sb("W2", [128, 8, 128])
        up0 = sb("up0", [128, HT, 128])
        down0 = sb("down0", [128, HT, 128])
        b2row = sb("b2row", [128, 128])
        gate0 = sb("gate0", [128, E0])
        gw1 = sb("gw1", [128, HT, 128])
        uw1 = sb("uw1", [128, HT, 128])
        dw1 = sb("dw1", [128, HT, 128])
        shared = sb("shared", [128, 3, 128])
        router = sb("router", [128, E1])
        col = sb("col", [128, cols.shape[1]])
        rowc = sb("rowc", [128, rows.shape[1]])
        cosT = sb("cosT", [128, T])
        sinT = sb("sinT", [128, T])
        ident = sb("ident", [128, 128])
        identb = sb("identb", [128, 128], BF16)
        causT = sb("causT", [128, 128], BF16)
        causS = sb("causS", [128, 128], BF16)
        sel0 = sb("sel0", [128, E0, 128], BF16)
        sel1 = sb("sel1", [128, HT, 128], BF16)
        biasT = sb("biasT", [128, 3, H, 256], BF16)
        biasS = sb("biasS", [128, 2, H, 256], BF16)
        qst = sb("qst", [128, 2, 8, T], BF16)
        kst = sb("kst", [128, 2, 4, T], BF16)
        q3 = sb("q3", [128, 3, T], BF16)
        k3 = sb("k3", [128, 3, T], BF16)
        va = sb("va", [128, TT, H, 32])
        vb = sb("vb", [128, TT, H, 32])
        probs = sb("probs", [128, 4, 2, T])
        wk = [sb(f"wk{n}", [128, T]) for n in range(6)]
        h1 = sb("h1", [128, 2, T])
        xt, xn, acc = sb("xt", [128, TT, 128]), sb("xn", [128, TT, 128]), sb("acc", [128, TT, 128])
        za, zb = sb("za", [128, TT, 128]), sb("zb", [128, TT, 128])
        otok, oT, oq = sb("otok", [128, TT, 128]), sb("oT", [128, T]), sb("oq", [128, T])
        x2 = sb("x2", [128, TT, 128])
        ohT = sb("ohT", [128, T])
        penT = sb("penT", [128, T], BF16)
        combS = sb("combS", [128, T], BF16)
        lat = sb("lat", [128, TT, 64])
        zaT, zbT, rq, rk, t1, t2 = (w[:] for w in wk)
        qf, kf = h1[:, 0, :], h1[:, 1, :]
        bst = sb("bst", [128, TT, 6])
        mv = sb("mv", [128, TT, 2])
        st = sb("st", [128, 16, TT])
        const = sb("const", [128, len(CONSTANTS), TT])
        nmax = sb("nmax", [128, 2, TT, 8])
        nmp = sb("nmp", [128, 2, TT, 2, 8], BF16)
        nmrow = sb("nmrow", [16, T], BF16)
        spare = sb("spare", [128, 2])
        rcp = sb("rcp", [128, TT, 4])
        g0 = sb("g0", [128, 3, TT, E0])
        gm = sb("gm", [128, 2, TT])
        lg = oq[:].rearrange("p (n t e) -> p n t e", n=4, t=TT)
        gs = oT[:, 0:320].rearrange("p (n t g) -> p n t g", n=10, t=TT)
        top = oT[:, 320:352].rearrange("p (t g) -> p t g", t=TT)
        gg = otok[:].rearrange("p t (n g) -> p (t n) g", n=16).rearrange("p (n t g) h -> p n t g h", n=2, t=TT)

        PS = ctx.enter_context(nc.psum_tensor("PS", [128, 8, T], F32))
        PVB, SMB = 4, 7
        SM = PS[:, SMB, :]
        SM_rows = SM.rearrange("p (t c) -> p t c", t=TT)
        PVT = PS[:, PVB, :]

        sem = {n: ctx.enter_context(nc.semaphore(n)) for n in PER}
        loads = ctx.enter_context(nc.semaphore("loads"))
        built = ctx.enter_context(nc.semaphore("built"))
        rel_in = ctx.enter_context(nc.semaphore("rel_in"))
        bias = ctx.enter_context(nc.semaphore("bias"))
        block = ctx.enter_context(nc.Block())

        gamma, beta, norm1, norm2, ln_g, ln_b, b2m, eta, mu0 = (col[:, n:n + 1] for n in range(9))
        b1m = [col[:, 9 + n:10 + n] for n in range(2)]
        rel_far = [col[:, 11 + n:12 + n] for n in range(H)]
        b1e = [col[:, 27 + n:28 + n] for n in range(HT)]
        gate_b, tie_w = rowc[:, 0:E0], rowc[:, E0:2 * E0]
        gate_bias = rowc[:, 8:8 + E1]
        earlier = rowc[:, 40:40 + GROUPS * GROUPS].rearrange("p (a b) -> p a b", a=GROUPS)
        LOADS = [(W0, w0), (W1, w1), (W1k, w1k), (W2, w2), (up0, m0_up), (down0, m0_down),
                 (gate0, m0_gate), (gw1, m1_gate_w), (uw1, m1_up_w), (dw1, m1_down_w), (shared, m1_shared),
                 (router, m1_router), (col, cols), (rowc, rows), (cosT, rope_cos), (sinT, rope_sin),
                 (ident, eye), (identb, eye_b), (causT, causal_t), (causS, causal_s), (sel0, pick0),
                 (sel1, pick1)]
        N_LOADS = 16 * (len(LOADS) + 9)

        def rows_of(t, n):
            return t[:, n * 128:(n + 1) * 128]

        def bank(res, key):
            return {"ring": lambda: 2 * (RI[key] % 2), "max": lambda: 5 + MI[key] % 2}[res]()

        def stack_ready(u):
            return f"stk{u % 2}", (u // 2 + 1) * 14 * 16

        def nmax_ready(u):
            return f"nmax{u % 2}", (u // 2 + 1) * 64

        def unfused(engine):
            n = 0 if engine is nc.vector else 1
            engine.tensor_tensor(spare[:, n:n + 1], const[:, 0, 0:1], const[:, 0, 0:1], ALU.mult)

        def stack_freed(u):
            return RI[("st", u - 2, 1, 1, len(steps_of(UNITS[u - 2][0])) - 1)] + 1 if u >= 2 else 0

        @block.sync
        def _(sp):
            for t, d in LOADS:
                sp.dma_start(t[:], d).then_inc(loads, 16)
            sp.wait_ge(built, 4)
            sp.dma_start(b2row[0:E0, :], m0_b2).then_inc(loads, 16)
            for s in range(2):
                for g in range(2):
                    sp.dma_start(kst[64 * g + 48:64 * g + 50, s], ones2).then_inc(loads, 16)
            for s in range(2):
                for g in range(2):
                    sp.dma_start(qst[64 * g + 48:64 * g + 50, s, g::2], zeros2).then_inc(loads, 16)
            tab = probs[:].rearrange("p a b t -> p (a b t)")
            sp.dma_start(tab, rel_t).then_inc(rel_in, 16)
            sp.dma_start(h1[:, 0, 0:256], mask_t).then_inc(rel_in, 16)
            sp.dma_start(h1[:, 1, 0:256], mask_s).then_inc(rel_in, 16)
            sp.wait_ge(bias, H + 5)
            sp.dma_start(tab, rel_s).then_inc(rel_in, 16)

            with sp.Fori(0, batches) as it:
                def wait(name, n):
                    sp.wait_ge(sem[name], it * per[name] + n + (name in PRIMED))

                def store_parts(a):
                    wait("parts", 2 * a + 2)
                    for n, t in enumerate((q3, k3)):
                        for r in range(3):
                            sp.dma_start(scr[a, n, :, r], t[:, r, :]).then_inc(sem["scr_w"], 16)

                def load_stack(u):
                    a, hf = UNITS[u]
                    s = u % 2
                    name = sem[f"stk{s}"]
                    wait("ring_full", stack_freed(u))
                    for g in range(2):
                        sp.dma_start(qst[64 * g + 48:64 * g + 50, s, g::2], zeros2).then_inc(name, 16)
                    wait("scr_w", 96 * (a + 1))
                    for n, t in enumerate((qst, kst)):
                        src = scr[a, n, 8 * hf:8 * hf + 8].rearrange("(p g) r d t -> g (r d) p t", g=2)
                        for g in range(2):
                            dst = t[:, s, g::2] if n == 0 else t[:, s]
                            r0 = 64 * g
                            second, third = ((0, 16), (0, 8)) if n == 0 else ((8, 24), (16, 24))
                            sp.dma_start(dst[r0:r0 + 24], src[g]).then_inc(name, 16)
                            sp.dma_start(dst[r0 + 24:r0 + 40], src[g, second[0]:second[1]]).then_inc(name, 16)
                            sp.dma_start(dst[r0 + 40:r0 + 48], src[g, third[0]:third[1]]).then_inc(name, 16)

                def load_nmax(u):
                    s = u % 2
                    wait("small_free", SI[("mrow", u)] + 1)
                    for g in range(2):
                        for part in range(2):
                            sp.dma_start(qst[64 * g + 48 + part:64 * g + 49 + part, s, g::2],
                                         nmrow[8 * part + g:8 * part + 8:2, :]).then_inc(sem[f"nmax{s}"], 16)

                store_parts(0)
                load_stack(0)
                load_stack(1)
                store_parts(1)
                load_nmax(0)
                load_stack(2)
                load_nmax(1)
                load_stack(3)
                load_nmax(2)
                load_nmax(3)
                store_parts(2)
                load_stack(4)
                load_stack(5)
                load_nmax(4)
                load_nmax(5)
            sp.wait_ge(sem["scr_w"], batches * per["scr_w"])

        @block.tensor
        def _(pe):
            pe.wait_ge(loads, N_LOADS)
            pe.wait_ge(bias, 2 * H + 8)
            pe.wait_ge(built, 6)

            with pe.Fori(0, batches) as it:
                def wait(name, n):
                    pe.wait_ge(sem[name], it * per[name] + n + (name in PRIMED))

                def claim_ring(key):
                    n = RI[key]
                    wait(f"ring_free{n % 2}", 2 * (n // 2))
                    return 2 * (n % 2)

                def claim_max(key):
                    n = MI[key]
                    wait(f"max_free{n % 2}", n // 2)
                    return 5 + n % 2

                def claim_small(key):
                    wait("small_free", SI[key])

                def drained(key):
                    n = RI[key]
                    wait(f"ring_free{n % 2}", 2 * (n // 2) + 2)

                def transposes(dst, src, n=TT, width=128):
                    for t in range(n):
                        mm = nc.tensor.transpose(dst[0:width, t * 128:(t + 1) * 128], src[:, t, :], ident[:])
                    return mm

                def by_rows(dst, lhs, rhs, width=128, k=128):
                    for t in range(TT):
                        mm = nc.tensor.matmul(dst[:, t * width:(t + 1) * width], rows_of(lhs, t)[0:k], rhs,
                                              start=True, stop=True)
                    return mm

                b = claim_ring("zT")
                wait("za", 1)
                transposes(PS[:, b, :], za)
                wait("zb", 1)
                transposes(PS[:, b + 1, :], zb).then_inc(sem["ring_full"], 1)
                drained("zT")
                b = claim_ring("qk0")
                nc.tensor.matmul(PS[:, b, :], W0[:, 0, :], zaT, start=True, stop=True)
                nc.tensor.matmul(PS[:, b + 1, :], W0[:, 1, :], zaT, start=True, stop=True)\
                    .then_inc(sem["ring_full"], 1)
                b = claim_ring("v0")
                by_rows(PS[:, b + 1, :], zbT, W1[:, 256:320], width=64)
                by_rows(PS[:, b, :], zaT, W0[:, 2, :]).then_inc(sem["ring_full"], 1)
                b = claim_ring("q1")
                nc.tensor.matmul(PS[:, b, :], W1[:, 0:128], zbT, start=True, stop=True)
                nc.tensor.matmul(PS[:, b + 1, :], W1[:, 128:256], zbT, start=True, stop=True)\
                    .then_inc(sem["ring_full"], 1)
                claim_small("latT")
                drained("v0")
                for t in range(TT):
                    mm = nc.tensor.matmul(SM[0:64, t * 128:(t + 1) * 128], lat[:, t, :], ident[:], start=True, stop=True)
                mm.then_inc(sem["small_full"], 1)
                wait("small_free", SI["latT"] + 1)
                latT = rk
                b = claim_ring("k1")
                nc.tensor.matmul(PS[:, b, :], W1k[:, 0, :], latT[0:64], start=True, stop=True)
                nc.tensor.matmul(PS[:, b + 1, :], W1k[:, 1, :], latT[0:64], start=True, stop=True)\
                    .then_inc(sem["ring_full"], 1)
                b = claim_ring("v1")
                by_rows(PS[:, b, :], latT, W1k[:, 2, :], k=64).then_inc(sem["ring_full"], 1)

                def row_max(u, hl, qt):
                    a, hf = UNITS[u]
                    h, s = 8 * hf + hl, u % 2
                    b = claim_max(("mx", u, hl, qt))
                    keys = T if a == 2 else 128 * (qt + 1)
                    mm = nc.tensor.matmul(PS[:, b, 0:keys], qst[:, s, hl, qt * 128:(qt + 1) * 128],
                                          kst[:, s, hl // 2, 0:keys], start=True, stop=(a == 2))
                    if a == 0:
                        w = min(256, keys)
                        for part in range(2):
                            mm = nc.tensor.matmul(PS[:, b, keys - w:keys], identb[:], biasS[:, part, h, 256 - w:256],
                                                  start=False, stop=(part == 1))
                    elif a == 1:
                        mm = nc.tensor.matmul(PS[:, b, keys - 128:keys], identb[:], causS[:], start=False, stop=True)
                    mm.then_inc(sem["max_full"], 1)

                def scores_t(u, g, pair, s):
                    a, hf = UNITS[u]
                    b = claim_ring(("st", u, g, pair, s))
                    for i in range(2):
                        hl = 4 * g + 2 * pair + i
                        for kt, c in steps_of(a)[s]:
                            q0 = first_query(a, kt)
                            n = T - q0
                            mm = nc.tensor.matmul(PS[:, b + i, c:c + n], kst[:, u % 2, 2 * g + pair, kt * 128:(kt + 1) * 128],
                                                  qst[:, u % 2, hl, q0:T], start=True, stop=(a == 2))
                            if a == 0:
                                w = min(256, n)
                                for part in range(3):
                                    mm = nc.tensor.matmul(PS[:, b + i, c:c + w], identb[:],
                                                          biasT[:, part, 8 * hf + hl, 0:w],
                                                          start=False, stop=(part == 2))
                            elif a == 1:
                                mm = nc.tensor.matmul(PS[:, b + i, c:c + 128], identb[:], causT[:],
                                                      start=False, stop=True)
                    mm.then_inc(sem["ring_full"], 1)

                def values(u, g, s):
                    a, hf = UNITS[u]
                    v = vb if a == 1 else va
                    if s == 0:
                        wait("pv_free", PI[("quad", u, g)])
                    drained(("st", u, g, 0, s))
                    drained(("st", u, g, 1, s))
                    last = steps_of(a)[-1][-1][0]
                    for kt, c in steps_of(a)[s]:
                        q0 = first_query(a, kt)
                        n = T - q0
                        for j in range(4):
                            slot = QI[("st", u, g, j // 2, s)] % 4
                            mm = nc.tensor.matmul(PVT[32 * j:32 * j + 32, q0:T], v[:, kt, 8 * hf + 4 * g + j, :],
                                                  probs[:, slot, j % 2, c:c + n], start=(kt == 0),
                                                  stop=(kt == last), tile_position=(0, 32 * j))
                    mm.then_inc(sem["probs_used"], 2)

                def attend(items):
                    for item in items:
                        kind, u = item[0], item[1]
                        if kind == "mx":
                            if item[2:] == (0, 0):
                                wait(*stack_ready(u))
                            row_max(*item[1:])
                        elif kind == "mrow":
                            claim_small(item)
                            wait("nmax_parts", u + 1)
                            for t in range(TT):
                                mm = nc.tensor.transpose(
                                    PS[0:16, SMB, :].bitcast(BF16)[:, t * 128:(t + 1) * 128],
                                    nmp[:, u % 2, t].rearrange("p a h -> p (a h)"), identb[:])
                            mm.then_inc(sem["small_full"], 1)
                        elif kind == "st":
                            if item[2:] == (0, 0, 0):
                                wait(*nmax_ready(u))
                            scores_t(*item[1:])
                        elif kind == "pv":
                            values(*item[1:])
                        elif kind == "fin":
                            wait("pv_free", PI[("quad", u, item[2])] + 1)
                            claim_small(item)
                            for t in range(TT):
                                mm = nc.tensor.transpose(SM[:, t * 128:(t + 1) * 128], rows_of(oq, t), ident[:])
                            mm.then_inc(sem["small_full"], 1)
                        elif kind == "woT":
                            claim_small(item)
                            transposes(SM, otok).then_inc(sem["small_full"], 1)
                        elif kind == "wo":
                            claim_small(item)
                            wo = (W0[:, 3, :], W1[:, 320:448], W2[:, 3, :])[u]
                            by_rows(SM, oT, wo).then_inc(sem["small_full"], 1)

                for seg in range(5):
                    attend(SEGMENTS[seg])

                claim_small("z2T")
                wait("z2", 1)
                transposes(SM, za).then_inc(sem["small_full"], 1)
                claim_small("gate0")
                z2T = zaT
                by_rows(SM, z2T, gate0[:], width=E0).then_inc(sem["small_full"], 1)
                claim_small("ohT")
                wait("onehot", 1)
                for t in range(TT):
                    mm = nc.tensor.transpose(SM[0:E0, t * 128:(t + 1) * 128], g0[:, 2, t, :], ident[:])
                mm.then_inc(sem["small_full"], 1)
                wait("small_free", SI["ohT"] + 1)

                def down0_tiles(n):
                    drained(("moe0", n))
                    slot = QI[("moe0", n)] % 4
                    for i in range(2):
                        mm = nc.tensor.matmul(PVT, down0[:, 2 * n + i, :], probs[:, slot, i, :],
                                              start=False, stop=(2 * n + i == HT - 1))
                    mm.then_inc(sem["probs_used"], 1)

                wait("pv_free", PI["down0"])
                nc.tensor.matmul(PVT, b2row[:], ohT[:], start=True, stop=False)
                for n in range(HT // 2):
                    b = claim_ring(("moe0", n))
                    for i in range(2):
                        tile = 2 * n + i
                        nc.tensor.matmul(PS[:, b + i, :], sel0[:, tile // TT, :], penT[:], start=True, stop=False)
                        mm = nc.tensor.matmul(PS[:, b + i, :], up0[:, tile, :], z2T, start=False, stop=True)
                    mm.then_inc(sem["ring_full"], 1)
                    if n >= 1:
                        down0_tiles(n - 1)
                down0_tiles(HT // 2 - 1)
                wait("pv_free", PI["down0"] + 1)
                claim_small("y0")
                for t in range(TT):
                    mm = nc.tensor.transpose(SM[:, t * 128:(t + 1) * 128], rows_of(t2, t), ident[:])
                mm.then_inc(sem["small_full"], 1)

                b = claim_ring("hT")
                wait("xn", 2)
                transposes(PS[:, b, :], xn)
                wait("vrow", 1)
                transposes(PS[:, b + 1, :], zb).then_inc(sem["ring_full"], 1)
                drained("hT")
                hT, vT, hmT = zaT, zbT, t1
                b = claim_ring("hid")
                for i in range(2):
                    mm = nc.tensor.matmul(PS[:, b + i, :], W2[:, 4 + i, :], hmT, start=True, stop=True)
                mm.then_inc(sem["ring_full"], 1)
                drained("hid")
                b = claim_ring("met")
                for i in range(2):
                    mm = nc.tensor.matmul(PS[:, b, :], W2[:, 6 + i, :], h1[:, i, :], start=(i == 0), stop=(i == 1))
                mm.then_inc(sem["ring_full"], 1)
                b = claim_ring("qk2")
                nc.tensor.matmul(PS[:, b, :], W2[:, 0, :], vT, start=True, stop=True)
                nc.tensor.matmul(PS[:, b + 1, :], W2[:, 1, :], vT, start=True, stop=True)\
                    .then_inc(sem["ring_full"], 1)
                b = claim_ring("v2")
                by_rows(PS[:, b, :], vT, W2[:, 2, :]).then_inc(sem["ring_full"], 1)

                for seg in range(5, 8):
                    attend(SEGMENTS[seg])

                claim_small("gate1")
                by_rows(SM, hT, router[:], width=E1).then_inc(sem["small_full"], 1)
                claim_small("combT")
                wait("comb", 1)
                for t in range(TT):
                    mm = nc.tensor.transpose(SM[0:E1, t * 128:(t + 1) * 128], lg[:, 3, t, :], ident[:])
                mm.then_inc(sem["small_full"], 1)
                wait("combS", 1)

                def down1_tile(n):
                    drained(("moe1", n)) if n == HT else wait(f"max_free{MI[('comb', n)] % 2}",
                                                              MI[("comb", n)] // 2 + 1)
                    lhs = shared[:, 2, :] if n == HT else dw1[:, n, :]
                    nc.tensor.matmul(PVT, lhs, probs[:, QI[("moe1", n)] % 4, 0, :], start=(n == 0), stop=(n == HT))\
                        .then_inc(sem["probs_used"], 1)

                wait("pv_free", PI["down1"])
                for n in range(HT + 1):
                    b = claim_ring(("moe1", n))
                    gw, uw = (shared[:, 0, :], shared[:, 1, :]) if n == HT else (gw1[:, n, :], uw1[:, n, :])
                    nc.tensor.matmul(PS[:, b, :], gw, hT, start=True, stop=True)
                    nc.tensor.matmul(PS[:, b + 1, :], uw, hT, start=True, stop=True).then_inc(sem["ring_full"], 1)
                    if n < HT:
                        b = claim_max(("comb", n))
                        nc.tensor.matmul(PS[:, b, :], sel1[:, n, :], combS[:], start=True, stop=True)\
                            .then_inc(sem["max_full"], 1)
                    if n >= 1:
                        down1_tile(n - 1)
                down1_tile(HT)
                wait("pv_free", PI["down1"] + 1)
                claim_small("y1")
                for t in range(TT):
                    mm = nc.tensor.transpose(SM[:, t * 128:(t + 1) * 128], rows_of(t2, t), ident[:])
                mm.then_inc(sem["small_full"], 1)

        @block.scalar
        def _(act):
            act.wait_ge(loads, N_LOADS)
            act.wait_ge(built, 6)
            tab = probs[:].rearrange("p a b t -> p (a b t)").rearrange("p (h c) -> p h c", h=H)
            act.wait_ge(bias, H)
            act.activation(biasT[:, 0], tab, ACT.Copy).then_inc(bias, 1)
            act.wait_ge(bias, 2 * H + 5)
            act.activation(biasS[:, 0], tab, ACT.Copy).then_inc(bias, 1)

            act.dma_start(xt[:], x[0].rearrange("(t p) c -> p t c", p=128)).then_inc(sem["x_in"], 16)

            with act.Fori(0, batches) as it:
                def wait(name, n):
                    act.wait_ge(sem[name], it * per[name] + n + (name in PRIMED))

                def full(key):
                    wait("ring_full", RI[key] + 1)
                    return 2 * (RI[key] % 2), sem[f"ring_free{RI[key] % 2}"]

                def small(key):
                    wait("small_full", SI[key] + 1)

                def by_token(dst, src, scale):
                    for t in range(TT):
                        last = act.activation(dst[:, t, :], src[:, t, :], ACT.Copy, scale=scale[:, t:t + 1])
                    return last

                def v_columns(v):
                    return v[:].rearrange("p t h c -> p (t h) c")[:, :, 0:DH]

                def v_source(b):
                    return PS[:, b, :].rearrange("p (n d) -> p n d", d=DH)

                wait("rstd", 1)
                wait("xn", 1)
                by_token(za, xn, st[:, 4, :]).then_inc(sem["za"], 1)
                b, free = full("zT")
                act.activation(zaT, PS[:, b, :], ACT.Identity, scale=gamma, bias=beta).then_inc(free, 1)
                act.activation(zbT, PS[:, b + 1, :], ACT.Copy, scale=norm1).then_inc(free, 1)
                b, _ = full("qk0")
                act.activation(q3[:, 0, :], PS[:, b, :], ACT.Copy, scale=RSQ8).then_inc(sem["hi"], 1)
                act.activation(k3[:, 2, :], PS[:, b + 1, :], ACT.Copy).then_inc(sem["hi"], 1)
                b, free = full("v0")
                act.activation(v_columns(va), v_source(b), ACT.Copy).then_inc(free, 1)
                small("latT")
                wait("parts", 2)
                act.activation(rk[0:64], SM[0:64], ACT.Identity, scale=ln_g[0:64], bias=ln_b[0:64])\
                    .then_inc(sem["small_free"], 1)
                wait("scr_w", 96)
                wait("roped", 1)
                act.activation(q3[:, 0, :], qf, ACT.Copy).then_inc(sem["hi"], 1)
                b, free = full("v1")
                act.activation(v_columns(vb), v_source(b), ACT.Copy).then_inc(free, 2)
                wait("roped", 2)
                act.activation(k3[:, 2, :], kf, ACT.Copy).then_inc(sem["hi"], 1)

                def attend(items):
                    for item in items:
                        kind, u = item[0], item[1]
                        if kind == "mrow":
                            small(item)
                            if u >= 1:
                                wait(*nmax_ready(u - 1))
                            act.activation(nmrow[:], PS[0:16, SMB, :].bitcast(BF16)[:, 0:T], ACT.Copy)\
                                .then_inc(sem["small_free"], 1)
                        elif kind == "st":
                            a = UNITS[u][0]
                            n, w = QI[item], step_width(a, item[4])
                            wait("probs_used", max(n - 3, 0))
                            b, free = full(item)
                            act.activation(probs[:, n % 4, :, 0:w], PS[:, b:b + 2, 0:w], ACT.Exp,
                                           scale=1.0 if a == 0 else RSQ8).then_inc(free, 2)
                        elif kind == "pv" and item[3] == len(steps_of(UNITS[u][0])) - 1:
                            q = PI[("quad", u, item[2])]
                            if q >= 1 and ("quad", u, item[2]) != ("quad", 0, 0):
                                prev = PV[q - 1] if PV[q - 1] != "down0" else PV[q - 2]
                                wait("small_full", SI[("fin",) + prev[1:]] + 1)
                            wait("probs_used", QI[("st", u, item[2], 1, item[3])] + 1)
                            act.activation(oq[:], PVT, ACT.Copy).then_inc(sem["pv_free"], 1)
                        elif kind == "woT":
                            small(item)
                            act.activation(oT[:], SM, ACT.Copy).then_inc(sem["small_free"], 1)

                for seg in range(5):
                    attend(SEGMENTS[seg])

                wait("acc", 2)
                act.dma_start(xt[:], x[it + 1].rearrange("(t p) c -> p t c", p=128)).then_inc(sem["x_in"], 16)
                wait("small_free", SI[("wo", 1)] + 1)
                for t in range(TT):
                    last = act.activation(za[:, t, :], x2[:, t, :], ACT.Square, accum_out=st[:, 6, t:t + 1])
                last.then_inc(sem["ssq"], 1)
                wait("rstd", 3)
                by_token(za, x2, st[:, 7, :]).then_inc(sem["z2"], 1)
                small("z2T")
                act.activation(zaT, SM, ACT.Copy, scale=norm2).then_inc(sem["small_free"], 1)
                for n in range(0, HT // 2, 2):
                    m = QI[("moe0", n)]
                    wait("probs_used", m - 3)
                    b, free = full(("moe0", n))
                    for i in range(2):
                        act.activation(probs[:, m % 4, i, :], PS[:, b + i, :], ACT.Relu, bias=b1e[2 * n + i])\
                            .then_inc(free, 1)
                wait("probs_used", QI[("moe0", HT // 2 - 1)] + 1)
                act.activation(t2, PVT, ACT.Copy).then_inc(sem["pv_free"], 1)

                wait("logm", 1)
                act.activation(st[:, 10, :], st[:, 9, :], ACT.Ln).then_inc(sem["lns"], 1)
                b, free = full("hT")
                act.activation(zaT, PS[:, b, :], ACT.Copy).then_inc(free, 1)
                act.activation(t1, PS[:, b, :], ACT.Identity, bias=mu0)
                act.activation(zbT, PS[:, b + 1, :], ACT.Copy).then_inc(free, 1)
                b, free = full("hid")
                for i in range(2):
                    act.activation(h1[:, i, :], PS[:, b + i, :], ACT.Tanh, bias=b1m[i]).then_inc(free, 1)
                b, free = full("met")
                act.activation(t1, PS[:, b, :], ACT.Tanh, bias=b2m).then_inc(free, 2)
                b, _ = full("qk2")
                wait("scr_w", 192)
                act.activation(k3[:, 2, :], PS[:, b + 1, :], ACT.Copy).then_inc(sem["hi"], 1)
                wait("metric", 1)
                act.activation(q3[:, 0, :], qf, ACT.Copy).then_inc(sem["hi"], 1)
                b, free = full("v2")
                act.activation(v_columns(va), v_source(b), ACT.Copy).then_inc(free, 2)

                for seg in range(5, 8):
                    attend(SEGMENTS[seg])

                wait("small_free", SI[("wo", 2)] + 1)
                for t in range(TT):
                    last = act.activation(zb[:, t, 1:], za[:, t, 1:], ACT.Square, accum_out=st[:, 6, t:t + 1])
                last.then_inc(sem["ssq"], 1)
                small("gate1")
                act.activation(lg[:, 0].rearrange("p t e -> p (t e)"), SM[:, 0:TT * E1], ACT.Exp, scale=-1.0)\
                    .then_inc(sem["small_free"], 1)
                small("combT")
                act.activation(combS[0:E1], SM[0:E1], ACT.Copy).then_inc(sem["comb_hi"], 1)
                for n in range(HT + 1):
                    b, _ = full(("moe1", n))
                    if n >= 2:
                        c = MI[("comb", n - 2)]
                        wait(f"max_free{c % 2}", c // 2 + 1)
                    act.activation((rq, rk)[n % 2], PS[:, b, :], ACT.Silu).then_inc(sem["silu"], 1)
                wait("probs_used", QI[("moe1", HT)] + 1)
                act.activation(t2, PVT, ACT.Copy).then_inc(sem["pv_free"], 1)
                wait("small_free", SI["y1"] + 1)
                act.dma_start(out[it].rearrange("(t p) c -> p t c", p=128), acc[:]).then_inc(sem["out_done"], 16)
            act.wait_ge(sem["out_done"], batches * 16)
            act.wait_ge(sem["x_in"], batches * 16 + 16)

        @block.vector
        def _(dve):
            count = [0]
            tab = probs[:].rearrange("p a b t -> p (a b t)").rearrange("p (h c) -> p h c", h=H)
            dve.wait_ge(loads, N_LOADS)
            for n, (parts, mask) in enumerate(((biasT, h1[:, 0, 0:256]), (biasS, h1[:, 1, 0:256]))):
                dve.wait_ge(rel_in, 48 + 16 * n)
                base = n * (H + 5)
                for h in range(H):
                    dve.scalar_tensor_tensor(tab[:, h, :], tab[:, h, :], rel_far[h], mask,
                                             ALU.subtract, ALU.add).then_inc(bias, 1)
                dve.wait_ge(bias, base + H + 1)
                dve.tensor_tensor(tab, tab, parts[:, 0], ALU.subtract).then_inc(bias, 1)
                dve.wait_ge(bias, base + H + 2)
                if n == 0:
                    dve.tensor_copy(parts[:, 1], tab).then_inc(bias, 1)
                    dve.wait_ge(bias, base + H + 3)
                    dve.tensor_tensor(parts[:, 2], tab, parts[:, 1], ALU.subtract).then_inc(bias, 2)
                    dve.wait_ge(bias, base + H + 5)
                else:
                    dve.tensor_copy(parts[:, 1], tab).then_inc(bias, 1)
                    dve.wait_ge(bias, base + H + 3)

            with dve.Fori(0, batches) as it:
                def wait(name, n):
                    dve.wait_ge(sem[name], it * per[name] + n + (name in PRIMED))

                def step(instruction):
                    count[0] += 1
                    instruction.then_inc(sem["dve"], 1)
                    wait("dve", count[0])

                def full(key):
                    wait("ring_full", RI[key] + 1)
                    return 2 * (RI[key] % 2), sem[f"ring_free{RI[key] % 2}"]

                def small(key):
                    wait("small_full", SI[key] + 1)

                def statistics(src, width=128):
                    for t in range(TT):
                        last = dve.bn_stats(bst[:, t, :], src[:, t, 0:width])
                    step(last)
                    unfused(nc.vector)
                    for t in range(TT):
                        last = dve.bn_aggr(mv[:, t, :], bst[:, t, :])
                    last.then_inc(sem["stats"], 1)

                def normalise(dst, src, rstd):
                    for t in range(TT):
                        last = dve.tensor_scalar(dst[:, t, :], src[:, t, :], mv[:, t, 0:1], rstd[:, t:t + 1],
                                                 ALU.subtract, ALU.mult)
                    return last

                wait("x_in", 16)
                statistics(xt)
                wait("rstd", 1)
                normalise(xn, xt, st[:, 0, :]).then_inc(sem["xn"], 1)
                b, free = full("qk0")
                wait("hi", 1)
                dve.scalar_tensor_tensor(rq, PS[:, b, :], RSQ8, q3[:, 0, :], ALU.mult, ALU.subtract)\
                    .then_inc(free, 1)
                wait("hi", 2)
                dve.tensor_tensor(rk, PS[:, b + 1, :], k3[:, 2, :], ALU.subtract).then_inc(free, 1)
                b, free = full("v0")
                latent = PS[:, b + 1, 0:TT * 64].rearrange("p (t c) -> p t c", t=TT)
                statistics(latent, 64)
                wait("rstd", 2)
                normalise(lat, latent, st[:, 5, :]).then_inc(free, 1)
                for key, dst in (("q1", qf), ("k1", kf)):
                    b, free = full(key)
                    if key == "k1":
                        wait("roped", 1)
                    dve.tensor_tensor(t1, PS[:, b, :], cosT[:], ALU.mult).then_inc(free, 1)
                    dve.tensor_tensor(t2, PS[:, b + 1, :], sinT[:], ALU.mult).then_inc(free, 1)

                def attend(items):
                    for item in items:
                        kind, u = item[0], item[1]
                        if kind == "mx":
                            _, _, hl, qt = item
                            a, n = UNITS[u][0], MI[item]
                            keys = T if a == 2 else 128 * (qt + 1)
                            wait("max_full", n + 1)
                            dve.tensor_reduce(nmax[:, u % 2, qt, hl:hl + 1], PS[:, 5 + n % 2, 0:keys], AX.X,
                                              ALU.max, negate=True).then_inc(sem[f"max_free{n % 2}"], 1)
                            if (hl, qt) == (7, TT - 1):
                                wait(f"max_free{n % 2}", n // 2 + 1)
                                wait(f"max_free{(n - 1) % 2}", (n - 1) // 2 + 1)
                                step(dve.tensor_copy(nmp[:, u % 2, :, 0], nmax[:, u % 2]))
                                dve.tensor_tensor(nmp[:, u % 2, :, 1], nmax[:, u % 2], nmp[:, u % 2, :, 0],
                                                  ALU.subtract).then_inc(sem["nmax_parts"], 1)
                        elif kind == "fin":
                            small(item)
                            ps = SM.rearrange("p (t j c) -> p t j c", t=TT, j=4)
                            step(dve.reciprocal(rcp[:].unsqueeze(3), ps[:, :, :, DH:DH + 1]))
                            c0 = 64 * UNITS[u][1] + 32 * item[2]
                            dve.tensor_tensor(otok[:, :, c0:c0 + 32].rearrange("p t (j d) -> p t j d", d=DH),
                                              ps[:, :, :, 0:DH], rcp[:].unsqueeze(3).broadcast_to((128, TT, 4, DH)),
                                              ALU.mult).then_inc(sem["small_free"], 1)
                        elif kind == "wo":
                            small(item)
                            if u == 0:
                                wait("acc", 1)
                                dve.tensor_tensor(acc[:], acc[:], SM_rows, ALU.add).then_inc(sem["small_free"], 1)
                            elif u == 1:
                                dve.tensor_tensor(x2[:], xn[:], SM_rows, ALU.add).then_inc(sem["small_free"], 1)
                            else:
                                step(dve.tensor_scalar(za[:], SM_rows, 0.1, 8.0, ALU.mult, ALU.min))
                                dve.tensor_scalar(za[:], za[:], -8.0, None, ALU.max).then_inc(sem["small_free"], 1)

                for seg in range(5):
                    attend(SEGMENTS[seg])

                small("gate0")
                lg0 = SM[:, 0:TT * E0].rearrange("p (t e) -> p t e", t=TT)
                dve.tensor_tensor(g0[:, 0], lg0, gate_b.unsqueeze(1).broadcast_to((128, TT, E0)), ALU.add)\
                    .then_inc(sem["small_free"], 1)
                wait("small_free", SI["gate0"] + 1)
                step(dve.tensor_reduce(gm[:, 0], g0[:, 0], AX.X, ALU.max))
                step(dve.tensor_tensor(g0[:, 1], g0[:, 0], gm[:, 0].unsqueeze(2).broadcast_to((128, TT, E0)),
                                       ALU.is_equal))
                step(dve.tensor_tensor(g0[:, 0], g0[:, 1], tie_w.unsqueeze(1).broadcast_to((128, TT, E0)), ALU.mult))
                step(dve.tensor_reduce(gm[:, 1], g0[:, 0], AX.X, ALU.max))
                dve.tensor_tensor(g0[:, 2], g0[:, 0], gm[:, 1].unsqueeze(2).broadcast_to((128, TT, E0)),
                                  ALU.is_equal).then_inc(sem["onehot"], 1)
                small("ohT")
                step(dve.tensor_copy(ohT[0:E0], SM[0:E0]))
                dve.tensor_scalar(penT[0:E0], SM[0:E0], -MASKED, MASKED, ALU.mult, ALU.add)\
                    .then_inc(sem["small_free"], 1)
                for n in range(1, HT // 2, 2):
                    m = QI[("moe0", n)]
                    wait("probs_used", m - 3)
                    b, free = full(("moe0", n))
                    for i in range(2):
                        dve.tensor_scalar(probs[:, m % 4, i, :], PS[:, b + i, :], b1e[2 * n + i], 0.0,
                                          ALU.add, ALU.max).then_inc(free, 1)
                small("y0")
                wait("acc", 2)
                dve.tensor_tensor(acc[:], acc[:], SM_rows, ALU.add).then_inc(sem["small_free"], 1)

                wait("small_free", SI["y0"] + 1)
                statistics(acc)
                wait("rstd", 4)
                normalise(xn, acc, st[:, 0, :]).then_inc(sem["xn"], 1)
                wait("xn", 2)
                step(dve.tensor_scalar(zb[:], xn[:], 8.0, -8.0, ALU.min, ALU.max))
                for t in range(TT):
                    last = dve.tensor_tensor_reduce(out=x2[:, t, 1:], in0=zb[:, t, 1:], in1=zb[:, t, 1:], scale=1.0,
                                                    scalar=0.0, op0=ALU.mult, op1=ALU.add,
                                                    accum_out=st[:, 8, t:t + 1])
                last.then_inc(sem["squares"], 1)
                wait("logm", 2)
                step(dve.reciprocal(st[:, 12, :], st[:, 12, :]))
                step(dve.tensor_tensor(st[:, 13, :], st[:, 11, :], st[:, 12, :], ALU.mult))
                for t in range(TT):
                    last = dve.tensor_scalar(zb[:, t, :], zb[:, t, :], st[:, 13, t:t + 1], None, ALU.mult)
                step(last)
                dve.tensor_tensor(zb[:, :, 0:1], st[:, 13, :].unsqueeze(2), st[:, 14, :].unsqueeze(2), ALU.mult)\
                    .then_inc(sem["vrow"], 1)
                met = RI["met"]
                wait(f"ring_free{met % 2}", 2 * (met // 2) + 2)
                step(dve.tensor_scalar(t1, t1, 0.1, eta, ALU.mult, ALU.add))
                b, free = full("qk2")
                dve.tensor_tensor(qf, PS[:, b, :], t1, ALU.mult).then_inc(sem["metric"], 1)
                wait("hi", 5)
                dve.tensor_tensor(rk, PS[:, b + 1, :], k3[:, 2, :], ALU.subtract).then_inc(free, 2)

                for seg in range(5, 8):
                    attend(SEGMENTS[seg])
                wait("x0", 1)
                dve.tensor_tensor(acc[:, :, 1:], acc[:, :, 1:], za[:, :, 1:], ALU.add)
                step(dve.tensor_tensor(acc[:, :, 0:1], acc[:, :, 0:1], st[:, 9, :].unsqueeze(2), ALU.add))

                wait("small_free", SI["gate1"] + 1)
                step(dve.tensor_scalar(lg[:, 0], lg[:, 0], 1.0, None, ALU.add))
                step(dve.reciprocal(lg[:, 0], lg[:, 0]))
                step(dve.tensor_tensor(lg[:, 1], lg[:, 0], gate_bias.unsqueeze(1).broadcast_to((128, TT, E1)),
                                       ALU.add))
                four = lg[:, 1].rearrange("p t (g e) -> p t g e", e=E1 // GROUPS)
                for n, (i, op) in enumerate(((0, ALU.max), (0, ALU.min), (2, ALU.max), (2, ALU.min))):
                    last = dve.tensor_tensor(gs[:, n].unsqueeze(3), four[:, :, :, i:i + 1], four[:, :, :, i + 1:i + 2], op)
                step(last)
                dve.tensor_tensor(gs[:, 4], gs[:, 0], gs[:, 2], ALU.max)
                dve.tensor_tensor(gs[:, 5], gs[:, 0], gs[:, 2], ALU.min)
                step(dve.tensor_tensor(gs[:, 6], gs[:, 1], gs[:, 3], ALU.max))
                step(dve.tensor_tensor(gs[:, 7], gs[:, 5], gs[:, 6], ALU.max))
                step(dve.tensor_tensor(gs[:, 8], gs[:, 4], gs[:, 7], ALU.add))
                mine = gs[:, 8].unsqueeze(3).broadcast_to((128, TT, GROUPS, GROUPS))
                other = gs[:, 8].unsqueeze(2).broadcast_to((128, TT, GROUPS, GROUPS))
                early = earlier.unsqueeze(1).broadcast_to((128, TT, GROUPS, GROUPS))
                dve.tensor_tensor(gg[:, 0], other, mine, ALU.is_gt)
                step(dve.tensor_tensor(gg[:, 1], other, mine, ALU.is_equal))
                step(dve.tensor_tensor(gg[:, 1], gg[:, 1], early, ALU.mult))
                step(dve.tensor_tensor(gg[:, 0], gg[:, 0], gg[:, 1], ALU.add))
                step(dve.tensor_reduce(gs[:, 9], gg[:, 0], AX.X, ALU.add))
                step(dve.tensor_scalar(gs[:, 9], gs[:, 9], float(TOPG), None, ALU.is_lt))
                step(dve.tensor_tensor(lg[:, 2].rearrange("p t (g e) -> p t g e", e=E1 // GROUPS), four,
                                       gs[:, 9].unsqueeze(3).broadcast_to((128, TT, GROUPS, E1 // GROUPS)), ALU.mult))
                unfused(nc.vector)
                for t in range(TT):
                    last = dve.max(top[:, t, :], lg[:, 2, t, :])
                step(last)
                unfused(nc.vector)
                for t in range(TT):
                    last = dve.match_replace(lg[:, 1, t, :], top[:, t, :], lg[:, 2, t, :], MASKED)
                step(last)
                step(dve.tensor_scalar(lg[:, 2], lg[:, 1], MASKED, None, ALU.is_equal))
                step(dve.tensor_tensor(lg[:, 2], lg[:, 2], lg[:, 0], ALU.mult))
                step(dve.tensor_reduce(gm[:, 0], lg[:, 2], AX.X, ALU.add))
                step(dve.tensor_scalar(gm[:, 0], gm[:, 0], 1e-20, None, ALU.add))
                step(dve.reciprocal(gm[:, 1], gm[:, 0]))
                step(dve.tensor_tensor(lg[:, 2], lg[:, 2], gm[:, 1].unsqueeze(2).broadcast_to((128, TT, E1)), ALU.mult))
                dve.tensor_scalar(lg[:, 3], lg[:, 2], 2.5, None, ALU.mult).then_inc(sem["comb"], 1)
                wait("comb_hi", 1)
                dve.tensor_tensor(rq[0:E1], SM[0:E1], combS[0:E1], ALU.subtract).then_inc(sem["small_free"], 1)
                wait("small_free", SI["combT"] + 1)
                dve.tensor_copy(combS[32:64], rq[0:E1])
                step(dve.tensor_copy(k3[0:E1, 0, :], rq[0:E1]))
                dve.tensor_tensor(combS[64:96], rq[0:E1], k3[0:E1, 0, :], ALU.subtract).then_inc(sem["combS"], 1)
                for n in range(HT + 1):
                    m = QI[("moe1", n)]
                    s = (rq, rk)[n % 2]
                    wait("silu", n + 1)
                    b, free = full(("moe1", n))
                    if n < HT:
                        dve.tensor_tensor(s, s, PS[:, b + 1, :], ALU.mult).then_inc(free, 2)
                        r = RI[("moe1", n)]
                        wait(f"ring_free{r % 2}", 2 * (r // 2) + 2)
                        c = MI[("comb", n)]
                        wait("max_full", c + 1)
                        wait("probs_used", m - 3)
                        dve.tensor_tensor(probs[:, m % 4, 0, :], s, PS[:, 5 + c % 2, :], ALU.mult)\
                            .then_inc(sem[f"max_free{c % 2}"], 1)
                    else:
                        wait("probs_used", m - 3)
                        dve.tensor_tensor(probs[:, m % 4, 0, :], s, PS[:, b + 1, :], ALU.mult).then_inc(free, 2)
                small("y1")
                dve.tensor_tensor(acc[:], acc[:], SM_rows, ALU.add).then_inc(sem["small_free"], 1)
            counted["dve"] = count[0]

        @block.gpsimd
        def _(pool):
            count = [0]
            pool.memset(qst[:], 0.0).then_inc(built, 1)
            pool.memset(kst[:], 0.0).then_inc(built, 1)
            pool.memset(b2row[:], 0.0).then_inc(built, 1)
            for n, c in enumerate(CONSTANTS):
                last = pool.memset(const[:, n, :], c)
            last.then_inc(built, 1)
            for t in (va, vb):
                pool.memset(t[:], 0.0)
            pool.memset(ohT[:], 0.0)
            pool.memset(penT[:], 0.0)
            pool.memset(combS[:], 0.0)
            pool.memset(st[:], 0.0).then_inc(built, 1)
            pool.wait_ge(built, 5)
            for t in (va, vb):
                last = pool.memset(t[:].rearrange("p t h c -> p (t h) c")[:, :, DH:DH + 1], 1.0)
            last.then_inc(built, 1)
            pool.wait_ge(built, 6)
            for name in PRIMED:
                pool.sem_inc(sem[name], 1)

            with pool.Fori(0, batches) as it:
                def wait(name, n):
                    pool.wait_ge(sem[name], it * per[name] + n + (name in PRIMED))

                def step(instruction):
                    count[0] += 1
                    instruction.then_inc(sem["pool"], 1)
                    wait("pool", count[0])

                def with_constant(dst, src, op, c):
                    return pool.tensor_tensor(dst, src, const[:, CONSTANTS.index(c), :], op)

                def add(dst, src, c):
                    return with_constant(dst, src, ALU.add, c)

                def at_least(dst, src, c):
                    unfused(nc.gpsimd)
                    return pool.tensor_scalar(dst, src, c, None, ALU.max)

                def power(dst, src, c):
                    return with_constant(dst, src, ALU.pow, c)

                def parts(dst, mid, lo, rest):
                    unfused(nc.gpsimd)
                    step(pool.tensor_copy(dst[:, mid, :], rest))
                    pool.tensor_tensor(dst[:, lo, :], rest, dst[:, mid, :], ALU.subtract)\
                        .then_inc(sem["parts"], 1)

                S = [st[:, n, :] for n in range(16)]
                wait("stats", 1)
                step(add(S[1], mv[:, :, 1], 1e-5))
                step(power(S[0], S[1], -0.5))
                step(pool.tensor_tensor(S[2], S[0], S[0], ALU.mult))
                step(pool.tensor_tensor(S[3], S[2], mv[:, :, 1], ALU.mult))
                step(add(S[4], S[3], 1e-5))
                step(power(S[4], S[4], -0.5))
                step(add(S[2], S[3], 1e-6))
                power(S[2], S[2], -0.5).then_inc(sem["rstd"], 1)
                wait("rstd", 1)
                wait("xn", 1)
                unfused(nc.gpsimd)
                for t in range(TT):
                    last = pool.tensor_scalar(zb[:, t, :], xn[:, t, :], S[2][:, t:t + 1], None, ALU.mult)
                last.then_inc(sem["zb"], 1)
                pool.tensor_tensor(acc[:], xt[:], xn[:], ALU.add).then_inc(sem["acc"], 1)
                qk0 = RI["qk0"]
                wait(f"ring_free{qk0 % 2}", 2 * (qk0 // 2) + 2)
                parts(q3, 1, 2, rq)
                parts(k3, 1, 0, rk)
                wait("stats", 2)
                step(add(S[5], mv[:, :, 1], 1e-5))
                power(S[5], S[5], -0.5).then_inc(sem["rstd"], 1)
                for n, (key, full, first, p3, mid, lo) in enumerate((("q1", qf, 0, q3, 1, 2), ("k1", kf, 2, k3, 1, 0))):
                    r = RI[key]
                    wait(f"ring_free{r % 2}", 2 * (r // 2) + 2)
                    pool.tensor_tensor(full, t1, t2, ALU.add).then_inc(sem["roped"], 1)
                for n, (full, first, p3, mid, lo) in enumerate(((qf, 0, q3, 1, 2), (kf, 2, k3, 1, 0))):
                    wait("hi", 3 + n)
                    step(pool.tensor_tensor(full, full, p3[:, first, :], ALU.subtract))
                    parts(p3, mid, lo, full)
                wait("small_free", SI[("wo", 1)] + 1)
                pool.tensor_tensor(acc[:], acc[:], x2[:], ALU.add).then_inc(sem["acc"], 1)
                wait("ssq", 1)
                step(with_constant(S[7], S[6], ALU.mult, 1.0 / D))
                step(add(S[7], S[7], 1e-6))
                power(S[7], S[7], -0.5).then_inc(sem["rstd"], 1)
                wait("stats", 3)
                step(add(S[5], mv[:, :, 1], 1e-5))
                power(S[0], S[5], -0.5).then_inc(sem["rstd"], 1)
                wait("squares", 1)
                step(add(S[9], S[8], 1.0))
                step(add(S[9], S[9], 1e-6))
                step(power(S[9], S[9], 0.5))
                step(at_least(S[10], S[9], 1.0 + 1e-6))
                step(pool.tensor_tensor(S[14], S[9], S[10], ALU.subtract))
                add(S[11], S[10], -1.0)
                step(add(S[12], S[10], 1.0))
                step(pool.tensor_tensor(S[11], S[11], S[12], ALU.mult))
                step(power(S[11], S[11], 0.5))
                pool.tensor_tensor(S[9], S[11], S[10], ALU.add).then_inc(sem["logm"], 1)
                step(pool.tensor_tensor(S[12], S[14], S[14], ALU.mult))
                step(pool.tensor_tensor(S[12], S[8], S[12], ALU.subtract))
                step(at_least(S[12], S[12], 1e-6))
                step(power(S[12], S[12], 0.5))
                step(add(S[12], S[12], 1e-6))
                wait("lns", 1)
                at_least(S[11], S[10], 1e-3).then_inc(sem["logm"], 1)
                r = RI["qk2"]
                wait(f"ring_free{r % 2}", 2 * (r // 2) + 2)
                parts(k3, 1, 0, rk)
                wait("hi", 6)
                step(pool.tensor_tensor(qf, qf, q3[:, 0, :], ALU.subtract))
                parts(q3, 1, 2, qf)
                wait("ssq", 2)
                step(add(S[9], S[6], 1.0))
                step(add(S[9], S[9], 1e-6))
                power(S[9], S[9], 0.5).then_inc(sem["x0"], 1)
                wait("out_done", 16)
            counted["pool"] = count[0]
    return counted


def _host(x):
    f, bf = np.float32, mybir.dt.np(BF16)
    con = np.ascontiguousarray
    i = {k: np.asarray(v) for k, v in x.items()}
    t = lambda w: w.T
    swap = np.array([h * DH + (d + DH // 2) % DH for h in range(H) for d in range(DH)])
    pad = lambda v, n=128: np.concatenate([v, np.zeros(n - v.shape[0], f)])
    mq = t(i["L0_ffn_Wq"])
    uk = t(i["L0_ffn_Wuk"])
    stack = lambda *w: con(np.stack(w, 1))
    tiles = lambda w: con(w.reshape(-1, 128, w.shape[-1]).transpose(1, 0, 2))
    w2 = t(i["L1_attn_W2"])
    w1 = t(i["L1_attn_W1"])
    rel = i["L0_attn_rel"]
    p = np.arange(128)[:, None]
    c = np.arange(256)[None, :]
    far = rel.shape[1] - 1
    eta = np.ones(D, f)
    eta[0] = -1
    mu = np.zeros(D, f)
    mu[0] = -1
    cols = [i["L0_attn_ln_gamma"], i["L0_attn_ln_beta"], i["L0_ffn_norm1_w"], i["L0_ffn_norm2_w"],
            pad(i["L0_ffn_ln_g"]), pad(i["L0_ffn_ln_b"]), i["L1_attn_b2"], eta, mu,
            i["L1_attn_b1"][:128], i["L1_attn_b1"][128:]]
    cols += [np.broadcast_to(rel[h, far], (128,)) for h in range(H)]
    cols += list(i["L0_ffn_b1"].reshape(HT, 128))
    tri = (np.arange(GROUPS)[None, :] < np.arange(GROUPS)[:, None]).astype(f).ravel()
    rows = np.concatenate([i["L0_ffn_gate_b"], np.arange(E0, 0, -1).astype(f), i["L1_ffn_gate_bias"], tri])
    half = DH // 2
    freq = (f(1.0) / f(10000.0) ** (np.arange(half, dtype=f) / f(half))).astype(f)
    ang = np.arange(T, dtype=f)[None, :] * freq[:, None]
    cos, sin = np.cos(ang).astype(f), np.sin(ang).astype(f)
    pick0 = np.zeros((128, E0, 128), f)
    for e in range(E0):
        pick0[e, e] = 1
    pick1 = np.zeros((128, HT, 128), f)
    for n in range(HT):
        for part in range(3):
            pick1[32 * part + 2 * n, n, :64] = 1
            pick1[32 * part + 2 * n + 1, n, 64:] = 1
    sq = np.arange(128)
    return dict(
        x=con(np.concatenate([i["L0_attn_x"], np.zeros((1, T, D), f)])),
        w0=stack(*(t(i["L0_attn_" + n]) for n in ("Wq", "Wk", "Wv", "Wo"))),
        w1=con(np.concatenate([mq, mq[:, swap], t(i["L0_ffn_Wdkv"]), t(i["L0_ffn_Wo"])], 1)),
        w1k=stack(uk, uk[:, swap], t(i["L0_ffn_Wuv"])),
        w2=stack(*(t(i["L1_attn_" + n]) for n in ("Wq", "Wk", "Wv", "Wo")), w1[:, :128], w1[:, 128:],
                 w2[:128], w2[128:]),
        m0_up=con(t(i["L0_ffn_W1"].reshape(HID0, D)).reshape(D, HT, 128)),
        m0_down=tiles(i["L0_ffn_W2"].transpose(0, 2, 1).reshape(HID0, D)),
        m0_b2=con(i["L0_ffn_b2"]), m0_gate=con(t(i["L0_ffn_gate_w"])),
        m1_gate_w=con(t(i["L1_ffn_w_gate"].reshape(HID0, D)).reshape(D, HT, 128)),
        m1_up_w=con(t(i["L1_ffn_w_up"].reshape(HID0, D)).reshape(D, HT, 128)),
        m1_down_w=tiles(i["L1_ffn_w_down"].transpose(0, 2, 1).reshape(HID0, D)),
        m1_shared=stack(*(t(i["L1_ffn_" + n]) for n in ("sh_gate", "sh_up", "sh_down"))),
        m1_router=con(t(i["L1_ffn_gate_w"])),
        cols=con(np.stack(cols, 1)), rows=con(np.broadcast_to(rows, (128, rows.shape[0]))),
        rel_t=con(rel[:, np.clip(c - p, 0, far)].transpose(1, 0, 2).reshape(128, -1)),
        rel_s=con(rel[:, np.clip(128 + p - c, 0, far)].transpose(1, 0, 2).reshape(128, -1)),
        mask_t=np.where(c < p, MASKED, 0).astype(f), mask_s=np.where(c > 128 + p, MASKED, 0).astype(f),
        causal_t=np.where(sq[None] < sq[:, None], MASKED, 0).astype(bf),
        causal_s=np.where(sq[None] > sq[:, None], MASKED, 0).astype(bf),
        rope_cos=con(np.tile(np.concatenate([cos, cos]), (H, 1))),
        rope_sin=con(np.tile(np.concatenate([-sin, sin]), (H, 1))),
        eye=np.eye(128, dtype=f), eye_b=np.eye(128).astype(bf), pick0=pick0.astype(bf), pick1=pick1.astype(bf),
        ones2=np.ones((2, 4, T), bf), zeros2=np.zeros((2, 4, T), bf),
    )


def kernel(**inputs):
    from concourse import bacc as _bacc
    from concourse.bass_utils import run_bass_kernel_spmd as _run

    nc = _bacc.Bacc("TRN2", target_bir_lowering=False, num_devices=1)
    arrays = _host(inputs)
    b = arrays["x"].shape[0] - 1
    args = {n: nc.dram_tensor(f"in_{n}", a.shape, mybir.dt.from_np(a.dtype), kind="ExternalInput").ap()
            for n, a in arrays.items()}
    out = nc.dram_tensor("out_0", (b, T, D), F32, kind="ExternalOutput").ap()
    layers_kernel(nc, b, out=out, per=PER, **args)
    r = _run(nc, [{f"in_{n}": a for n, a in arrays.items()}], core_ids=[0])
    return r.results[0]["out_0"]
```

```python
import concourse.bass as bass
from concourse import mybir
from contextlib import ExitStack
import numpy as np

F32 = mybir.dt.float32
BF16 = mybir.dt.bfloat16
ALU = mybir.AluOpType
ACT = mybir.ActivationFunctionType
AX = mybir.AxisListType

T, D, H, DH = 512, 128, 16, 8
TT = T // 128
HID0, E0 = 2048, 4
E1, TOPK, GROUPS, TOPG = 32, 8, 8, 4
HT = HID0 // 128
MASKED = -1e30
CONSTANTS = [-0.5, 0.5, 1e-5, 1e-6, 1.0, -1.0, 1.0 / D]
RSQ8 = float(1.0 / np.sqrt(8.0))

UNITS = [(0, 0), (1, 0), (1, 1), (0, 1), (2, 0), (2, 1)]
CAUSAL_STEPS = [[(0, 0)], [(1, 0), (3, 384)], [(2, 0)]]
FULL_STEPS = [[(k, 0)] for k in range(4)]


def steps_of(a):
    return FULL_STEPS if a == 2 else CAUSAL_STEPS


def first_query(a, kt):
    return 0 if a == 2 else 128 * kt


def step_width(a, s):
    return sum(T - first_query(a, kt) for kt, _ in steps_of(a)[s])


def max_items(u):
    return [("mx", u, hl, qt) for hl in range(8) for qt in range(TT)]


def exp_items(u):
    s_n = len(steps_of(UNITS[u][0]))
    out = []
    for n in range(2 * s_n):
        out += [("st", u, n // s_n, pair, n % s_n) for pair in range(2)]
        if n >= 2 and (n - 1) % s_n == 0:
            out.append(("fin", u, (n - 2) // s_n))
        if n >= 1:
            out.append(("pv", u, (n - 1) // s_n, (n - 1) % s_n))
    return out + [("pv", u, 1, s_n - 1), ("fin", u, 1)]


def merged(exps, maxes, lead=0, tail=0):
    end = len(exps) - tail
    out, m = list(exps[:lead]), 0
    for n, item in enumerate(exps[lead:end]):
        out.append(item)
        upto = (n + 1) * len(maxes) // (end - lead)
        out += maxes[m:upto]
        m = upto
    return out, list(exps[end:])


def beside(u, maxes, lead, tail):
    out, rest = merged(exp_items(u), maxes, lead, tail)
    return out + [("mrow", (u + 1) % 6)] + rest


def experts0(lo, hi):
    chunks = [[("moe0", lo)]] + [[("moe0", n), ("down0", n - 1)] for n in range(lo + 1, hi)]
    return chunks + [[("down0", hi - 1)]]


def with_experts(exps, first, last):
    before, beside_pv, behind = experts0(0, first), experts0(first, last), experts0(last, HT // 2)
    out = sum(before[:-1], []) + exps[:2] + before[-1]
    for item in exps[2:]:
        out.append(item)
        if item[0] == "pv" and beside_pv:
            out += beside_pv.pop(0)
    return out + sum(behind, [])


def experts1(n, maxes):
    return [("moe1", n)] + maxes[:2] + [("down1", n - 1 if n else HT)] + maxes[2:] + [("comb", n)]


def later(items, *moves):
    out = list(items)
    for item, by in moves:
        n = out.index(item)
        out.insert(n + by, out.pop(n))
    return out


def spread(items, others, first, every):
    out, rest = [], list(others)
    for n, item in enumerate(items):
        out.append(item)
        if n >= first and (n - first) % every == 0 and rest:
            out.append(rest.pop(0))
    return out + rest


TAIL = 8
MX0, MX3, MX4 = max_items(0), max_items(3), max_items(4)
NORM = [("ln", 0), ("xn", 0)]
PROJECT = [("zT", 0), ("qk0", 0), ("v0", 0), ("latln", 0), ("q1", 0), ("latn", 0), ("q1hi", 0), ("latT", 0),
           ("k1", 0), ("k1hi", 0)]
CHOICE = (MX3[16:18] + [("woT", 1)] + MX3[18:20] + [("wo", 1)] + MX3[20:26] + [("z2T", 0)] + MX3[26:28]
          + [("gate0", 0)] + MX3[28:31] + [("ohT", 0)] + MX3[31:] + [("mrow", 3)])
EARLY1, MX4_A_TILE = 5, 3
EXPERTS1 = [("moe1", HT), ("combT", 0)]
for n in range(HT):
    EXPERTS1 += [NORM[0]] if n == HT - 5 else []
    EXPERTS1 += [NORM[1]] if n == HT - 2 else []
    EXPERTS1 += experts1(n, MX4[max(0, MX4_A_TILE * (n - EARLY1)):max(0, MX4_A_TILE * (n - EARLY1 + 1))])
EXPERTS1 += [("mrow", 4), ("down1", HT - 1), ("y1", 0)]
OPENING = NORM + PROJECT + MX0 + [("mrow", 0)]
LAYER0 = (spread(beside(0, max_items(1), 8, TAIL), [("v1", 0)], 1, 1) + beside(1, max_items(2), 5, TAIL)
          + sum(merged(exp_items(2), MX3[:16], 5), []) + CHOICE + with_experts(exp_items(3), 3, 6))
LAYER0 += [("wo", 0), ("y0", 0)]
LAYER0 = later(LAYER0, (("mrow", 1), 2), (("fin", 0, 1), 2), (("mrow", 2), 2), (("fin", 1, 1), 2), (("mrow", 3), 1),
               (("fin", 3, 1), 1))
LAYER0.insert(LAYER0.index(("fin", 1, 0)), ("x", 0))
LAYER0.insert(LAYER0.index(("down0", HT // 2 - 2)), ("woT", 0))
LAYER1 = (EXPERTS1 + spread(beside(4, max_items(5), 0, TAIL), PROJECT, 0, 5)
          + beside(5, MX0, 8, TAIL) + [("woT", 2), ("wo", 2)])
LAYER1 = later(LAYER1, (("mrow", 5), 2), (("fin", 4, 1), 2), (("mrow", 0), 2))
PROJECTED = ["hT", "hid", "met", "vT", "qk2", "v2"]
SMALLS = ["fin", "mrow", "woT", "wo", "z2T", "gate0", "ohT", "y0", "combT", "y1", "latT"]


def of(kinds, items):
    return [i for i in items if i[0] in kinds]


class Uses:

    def __init__(self, ring, maxima, small, pv, tiles, **others):
        self.ring, self.maxima, self.small, self.pv, self.tiles = (
            {k: n for n, k in enumerate(x)} for x in (ring, maxima, small, pv, tiles))
        self.pv_order = pv
        self.raised = dict(
            ring_full=len(ring), ring_free0=2 * ((len(ring) + 1) // 2), ring_free1=2 * (len(ring) // 2),
            max_full=len(maxima), max_free0=(len(maxima) + 1) // 2, max_free1=len(maxima) // 2,
            small_full=len(small), small_free=len(small), pv_free=len(pv), probs_used=len(tiles), **others)


RINGS = ["zT", "qk0", "v0", "q1", "k1", "v1", "st", "moe0", "moe1"]
BEFORE = Uses(
    of(RINGS, OPENING), of(["mx"], OPENING), of(SMALLS, OPENING), [], [],
    x_in=16, out_done=0, stats=2, rstd=2, xn=1, za=1, zb=1, lat=1, hi=4, parts=4, scr_w=2 * 6 * 16,
    stk0=14 * 16, stk1=0, nmax0=64, nmax1=0, nmax_parts=1, roped=2, acc=0, ssq=0, z2=0, onehot=0, squares=0,
    vrow=0, logm=0, lns=0, metric=0, x0=0, comb=0, comb_hi=0, combS=0, silu=0, dve=3, pool=14)
TURN = Uses(
    of(RINGS, LAYER0) + PROJECTED + of(RINGS, LAYER1),
    of(["mx"], LAYER0) + ["acc0"] + of(["mx", "comb"], LAYER1),
    of(SMALLS, LAYER0) + ["gate1"] + of(SMALLS, LAYER1),
    [("quad", u, g) for u in range(4) for g in range(2)] + ["acc1"] + [("quad", u, g) for u in (4, 5) for g in range(2)],
    of(["st", "moe0", "moe1"], LAYER0 + LAYER1),
    x_in=16, out_done=16, stats=3, rstd=4, xn=2, za=1, zb=1, lat=1, hi=6, parts=6, scr_w=3 * 6 * 16,
    stk0=3 * 14 * 16, stk1=3 * 14 * 16, nmax0=3 * 64, nmax1=3 * 64, nmax_parts=6, roped=2, acc=2, ssq=2, z2=1,
    onehot=1, squares=1, vrow=1, logm=2, lns=1, metric=1, x0=2, comb=1, comb_hi=1, combS=1, silu=HT + 1,
    dve=54, pool=35)
BEFORE.first = dict(stats=0, rstd=0, xn=0, hi=0, parts=0, scr_w=0)
TURN.first = dict(stats=1, rstd=2, xn=1, hi=2, parts=2, scr_w=96)
BEFORE.nth, BEFORE.nth_stack = {0: 1}, {0: 1}
TURN.nth = {1: 1, 2: 2, 3: 3, 4: 4, 5: 5, 0: 6}
TURN.nth_stack = {2: 1, 4: 2, 0: 3, 1: 1, 3: 2, 5: 3}

PRIMED = ("ring_full", "ring_free0", "ring_free1", "max_free0", "max_free1", "small_free", "pv_free",
          "probs_used")


def layers_kernel(nc, batches, x, out, w0, w1, w1k, w2, m0_up, m0_down, m0_b2, m0_gate, m1_gate_w,
                  m1_up_w, m1_down_w, m1_shared, m1_router, cols, rows, rel_t, rel_s, mask_t, mask_s,
                  causal_t, causal_s, rope_cos, rope_sin, eye, eye_b, pick0, pick1, ones2, zeros2, before, per):
    counted, counted_before = {}, {}
    scr = nc.dram_tensor("scratch_parts", (3, 2, H, 3, DH, T), BF16, kind="Internal").ap()
    ctx = ExitStack()
    with ctx:
        def sb(name, shape, dt=F32):
            return ctx.enter_context(nc.sbuf_tensor(name, shape, dt))

        W0 = sb("W0", [128, 4, 128])
        W1 = sb("W1", [128, 448])
        W1k = sb("W1k", [64, 3, 128])
        W2 = sb("W2", [128, 8, 128])
        up0 = sb("up0", [128, HT, 128])
        down0 = sb("down0", [128, HT, 128])
        b2row = sb("b2row", [128, 128])
        gate0 = sb("gate0", [128, E0])
        gw1 = sb("gw1", [128, HT, 128])
        uw1 = sb("uw1", [128, HT, 128])
        dw1 = sb("dw1", [128, HT, 128])
        shared = sb("shared", [128, 3, 128])
        router = sb("router", [128, E1])
        col = sb("col", [128, cols.shape[1]])
        rowc = sb("rowc", [128, rows.shape[1]])
        cosT = sb("cosT", [128, T])
        sinT = sb("sinT", [128, T])
        ident = sb("ident", [128, 128])
        identb = sb("identb", [128, 128], BF16)
        causT = sb("causT", [128, 128], BF16)
        causS = sb("causS", [128, 128], BF16)
        sel0 = sb("sel0", [128, E0, 128], BF16)
        sel1 = sb("sel1", [128, HT, 128], BF16)
        biasT = sb("biasT", [128, 3, H, 256], BF16)
        biasS = sb("biasS", [128, 2, H, 256], BF16)
        qst = sb("qst", [128, 2, 8, T], BF16)
        kst = sb("kst", [128, 2, 4, T], BF16)
        q3 = sb("q3", [128, 3, T], BF16)
        k3 = sb("k3", [128, 3, T], BF16)
        va = sb("va", [128, TT, H, 32])
        vb = sb("vb", [128, TT, H, 32])
        probs = sb("probs", [128, 4, 2, T])
        wk = [sb(f"wk{n}", [128, T]) for n in range(6)]
        h1 = sb("h1", [128, 2, T])
        xt, xn, acc = sb("xt", [128, TT, 128]), sb("xn", [128, TT, 128]), sb("acc", [128, TT, 128])
        za, zb = sb("za", [128, TT, 128]), sb("zb", [128, TT, 128])
        otok, oT, oq = sb("otok", [128, TT, 128]), sb("oT", [128, T]), sb("oq", [128, T])
        x2 = sb("x2", [128, TT, 128])
        ohT = sb("ohT", [128, T])
        penT = sb("penT", [128, T], BF16)
        combS = sb("combS", [128, T], BF16)
        lat = sb("lat", [128, TT, 64])
        zaT, zbT, rq, rk, t1, t2 = (w[:] for w in wk)
        qf, kf = h1[:, 0, :], h1[:, 1, :]
        bst = sb("bst", [128, TT, 6])
        mv = sb("mv", [128, TT, 2])
        st = sb("st", [128, 16, TT])
        const = sb("const", [128, len(CONSTANTS), TT])
        nmax = sb("nmax", [128, 2, TT, 8])
        nmp = sb("nmp", [128, 2, TT, 2, 8], BF16)
        nmrow = sb("nmrow", [16, T], BF16)
        spare = sb("spare", [128, 2])
        rcp = sb("rcp", [128, TT, 4])
        g0 = sb("g0", [128, 3, TT, E0])
        gm = sb("gm", [128, 2, TT])
        lg = oq[:].rearrange("p (n t e) -> p n t e", n=4, t=TT)
        gs = oT[:, 0:320].rearrange("p (n t g) -> p n t g", n=10, t=TT)
        top = oT[:, 320:352].rearrange("p (t g) -> p t g", t=TT)
        gg = otok[:].rearrange("p t (n g) -> p (t n) g", n=16).rearrange("p (n t g) h -> p n t g h", n=2, t=TT)

        PS = ctx.enter_context(nc.psum_tensor("PS", [128, 8, T], F32))
        PVB, SMB = 4, 7
        SM = PS[:, SMB, :]
        SM_rows = SM.rearrange("p (t c) -> p t c", t=TT)
        PVT = PS[:, PVB, :]
        ACC0 = PS[:, 5 + TURN.maxima["acc0"] % 2, :]
        z2T, hT, vT, hmT, latT = zaT, zaT, zbT, t1, rk

        sem = {n: ctx.enter_context(nc.semaphore(n)) for n in per}
        loads = ctx.enter_context(nc.semaphore("loads"))
        built = ctx.enter_context(nc.semaphore("built"))
        rel_in = ctx.enter_context(nc.semaphore("rel_in"))
        bias = ctx.enter_context(nc.semaphore("bias"))
        block = ctx.enter_context(nc.Block())

        gamma, beta, norm1, norm2, ln_g, ln_b, b2m, eta, mu0 = (col[:, n:n + 1] for n in range(9))
        b1m = [col[:, 9 + n:10 + n] for n in range(2)]
        rel_far = [col[:, 11 + n:12 + n] for n in range(H)]
        b1e = [col[:, 27 + n:28 + n] for n in range(HT)]
        gate_b, tie_w = rowc[:, 0:E0], rowc[:, E0:2 * E0]
        gate_bias = rowc[:, 8:8 + E1]
        earlier = rowc[:, 40:40 + GROUPS * GROUPS].rearrange("p (a b) -> p a b", a=GROUPS)
        LOADS = [(W0, w0), (W1, w1), (W1k, w1k), (W2, w2), (up0, m0_up), (down0, m0_down),
                 (gate0, m0_gate), (gw1, m1_gate_w), (uw1, m1_up_w), (dw1, m1_down_w), (shared, m1_shared),
                 (router, m1_router), (col, cols), (rowc, rows), (cosT, rope_cos), (sinT, rope_sin),
                 (ident, eye), (identb, eye_b), (causT, causal_t), (causS, causal_s), (sel0, pick0),
                 (sel1, pick1)]
        N_LOADS = 16 * (len(LOADS) + 9)

        def token_outputs(a):
            return zb if a == 0 else otok

        def rows_of(t, n):
            return t[:, n * 128:(n + 1) * 128]

        def at(it, name, n):
            n += name in PRIMED
            return n if it is None else it * per[name] + (before[name] + n)

        def stack_ready(it, now, u):
            name = f"stk{u % 2}"
            return sem[name], at(it, name, now.nth_stack[u] * 14 * 16)

        def nmax_ready(it, n, slot):
            name = f"nmax{slot}"
            return sem[name], at(it, name, 64 * n)

        def silu_place(n):
            return 0 if n == HT else n + 1

        def unfused(engine):
            n = 0 if engine is nc.vector else 1
            engine.tensor_tensor(spare[:, n:n + 1], const[:, 0, 0:1], const[:, 0, 0:1], ALU.mult)

        def stack_freed(now, u):
            if u == 1 or now is BEFORE:
                return 0
            had = 4 if u == 0 else u - 2
            return now.ring[("st", had, 1, 1, len(steps_of(UNITS[had][0])) - 1)] + 1

        @block.sync
        def _(sp):
            for t, d in LOADS:
                sp.dma_start(t[:], d).then_inc(loads, 16)
            sp.wait_ge(built, 4)
            sp.dma_start(b2row[0:E0, :], m0_b2).then_inc(loads, 16)
            for s in range(2):
                for g in range(2):
                    sp.dma_start(kst[64 * g + 48:64 * g + 50, s], ones2).then_inc(loads, 16)
            for s in range(2):
                for g in range(2):
                    sp.dma_start(qst[64 * g + 48:64 * g + 50, s, g::2], zeros2).then_inc(loads, 16)
            tab = probs[:].rearrange("p a b t -> p (a b t)")
            sp.dma_start(tab, rel_t).then_inc(rel_in, 16)
            sp.dma_start(h1[:, 0, 0:256], mask_t).then_inc(rel_in, 16)
            sp.dma_start(h1[:, 1, 0:256], mask_s).then_inc(rel_in, 16)
            sp.wait_ge(bias, H + 5)
            sp.dma_start(tab, rel_s).then_inc(rel_in, 16)

            now, it = BEFORE, None

            def store_parts(a):
                n = 2 if a == 2 else now.first["parts"] + 2 * a + 2
                sp.wait_ge(sem["parts"], at(it, "parts", n))
                for n, t in enumerate((q3, k3)):
                    for r in range(3):
                        sp.dma_start(scr[a, n, :, r], t[:, r, :]).then_inc(sem["scr_w"], 16)

            def load_stack(u):
                a, hf = UNITS[u]
                s = u % 2
                name = sem[f"stk{s}"]
                sp.wait_ge(sem["ring_full"], at(it, "ring_full", stack_freed(now, u)))
                for g in range(2):
                    sp.dma_start(qst[64 * g + 48:64 * g + 50, s, g::2], zeros2).then_inc(name, 16)
                stored = {4: 96, 5: 96, 0: now.first["scr_w"] + 96}.get(u, 0)
                sp.wait_ge(sem["scr_w"], at(it, "scr_w", stored))
                for n, t in enumerate((qst, kst)):
                    src = scr[a, n, 8 * hf:8 * hf + 8].rearrange("(p g) r d t -> g (r d) p t", g=2)
                    for g in range(2):
                        dst = t[:, s, g::2] if n == 0 else t[:, s]
                        r0 = 64 * g
                        second, third = ((0, 16), (0, 8)) if n == 0 else ((8, 24), (16, 24))
                        sp.dma_start(dst[r0:r0 + 24], src[g]).then_inc(name, 16)
                        sp.dma_start(dst[r0 + 24:r0 + 40], src[g, second[0]:second[1]]).then_inc(name, 16)
                        sp.dma_start(dst[r0 + 40:r0 + 48], src[g, third[0]:third[1]]).then_inc(name, 16)

            def load_nmax(u):
                s = u % 2
                sp.wait_ge(sem["small_free"], at(it, "small_free", now.small[("mrow", u)] + 1))
                for g in range(2):
                    for part in range(2):
                        sp.dma_start(qst[64 * g + 48 + part:64 * g + 49 + part, s, g::2],
                                     nmrow[8 * part + g:8 * part + 8:2, :]).then_inc(sem[f"nmax{s}"], 16)

            store_parts(0)
            load_stack(0)
            store_parts(1)
            load_nmax(0)
            with sp.Fori(0, batches) as it:
                now = TURN
                load_stack(1)
                load_nmax(1)
                load_stack(2)
                load_nmax(2)
                load_stack(3)
                load_nmax(3)
                store_parts(2)
                load_stack(4)
                load_stack(5)
                load_nmax(4)
                store_parts(0)
                load_nmax(5)
                load_stack(0)
                store_parts(1)
                load_nmax(0)
            sp.wait_ge(sem["nmax0"], before["nmax0"] + batches * per["nmax0"])
            sp.wait_ge(sem["scr_w"], before["scr_w"] + batches * per["scr_w"])

        @block.tensor
        def _(pe):
            pe.wait_ge(loads, N_LOADS)
            pe.wait_ge(bias, 2 * H + 8)
            pe.wait_ge(built, 6)

            now, it = BEFORE, None

            def claim_ring(key):
                n = now.ring[key]
                pe.wait_ge(sem[f"ring_free{n % 2}"], at(it, f"ring_free{n % 2}", 2 * (n // 2)))
                return 2 * (n % 2)

            def claim_max(key):
                n = now.maxima[key]
                pe.wait_ge(sem[f"max_free{n % 2}"], at(it, f"max_free{n % 2}", n // 2))
                return 5 + n % 2

            def claim_small(key):
                pe.wait_ge(sem["small_free"], at(it, "small_free", now.small[key]))

            def drained(*keys):
                for slot in range(2):
                    last = max((now.ring[key] for key in keys if now.ring[key] % 2 == slot), default=None)
                    if last is not None:
                        pe.wait_ge(sem[f"ring_free{slot}"], at(it, f"ring_free{slot}", 2 * (last // 2) + 2))

            def transposes(dst, src, n=TT, width=128):
                for t in range(n):
                    mm = nc.tensor.transpose(dst[0:width, t * 128:(t + 1) * 128], src[:, t, :], ident[:])
                return mm

            def by_rows(dst, lhs, rhs, width=128, k=128):
                for t in range(TT):
                    mm = nc.tensor.matmul(dst[:, t * width:(t + 1) * width], rows_of(lhs, t)[0:k], rhs,
                                          start=True, stop=True)
                return mm

            def row_max(u, hl, qt):
                a, hf = UNITS[u]
                h, s = 8 * hf + hl, u % 2
                b = claim_max(("mx", u, hl, qt))
                keys = T if a == 2 else 128 * (qt + 1)
                mm = nc.tensor.matmul(PS[:, b, 0:keys], qst[:, s, hl, qt * 128:(qt + 1) * 128],
                                      kst[:, s, hl // 2, 0:keys], start=True, stop=(a == 2))
                if a == 0:
                    w = min(256, keys)
                    for part in range(2):
                        mm = nc.tensor.matmul(PS[:, b, keys - w:keys], identb[:], biasS[:, part, h, 256 - w:256],
                                              start=False, stop=(part == 1))
                elif a == 1:
                    mm = nc.tensor.matmul(PS[:, b, keys - 128:keys], identb[:], causS[:], start=False, stop=True)
                mm.then_inc(sem["max_full"], 1)

            def scores_t(u, g, pair, s):
                a, hf = UNITS[u]
                b = claim_ring(("st", u, g, pair, s))
                for i in range(2):
                    hl = 4 * g + 2 * pair + i
                    for kt, c in steps_of(a)[s]:
                        q0 = first_query(a, kt)
                        n = T - q0
                        mm = nc.tensor.matmul(PS[:, b + i, c:c + n], kst[:, u % 2, 2 * g + pair, kt * 128:(kt + 1) * 128],
                                              qst[:, u % 2, hl, q0:T], start=True, stop=(a == 2))
                        if a == 0:
                            w = min(256, n)
                            for part in range(3):
                                mm = nc.tensor.matmul(PS[:, b + i, c:c + w], identb[:],
                                                      biasT[:, part, 8 * hf + hl, 0:w],
                                                      start=False, stop=(part == 2))
                        elif a == 1:
                            mm = nc.tensor.matmul(PS[:, b + i, c:c + 128], identb[:], causT[:],
                                                  start=False, stop=True)
                mm.then_inc(sem["ring_full"], 1)

            def values(u, g, s):
                a, hf = UNITS[u]
                v = va if a == 0 else vb
                if s == 0:
                    pe.wait_ge(sem["pv_free"], at(it, "pv_free", now.pv[("quad", u, g)]))
                drained(("st", u, g, 0, s), ("st", u, g, 1, s))
                last = steps_of(a)[-1][-1][0]
                for kt, c in steps_of(a)[s]:
                    q0 = first_query(a, kt)
                    n = T - q0
                    for j in range(4):
                        slot = now.tiles[("st", u, g, j // 2, s)] % 4
                        mm = nc.tensor.matmul(PVT[32 * j:32 * j + 32, q0:T], v[:, kt, 8 * hf + 4 * g + j, :],
                                              probs[:, slot, j % 2, c:c + n], start=(kt == 0),
                                              stop=(kt == last), tile_position=(0, 32 * j))
                mm.then_inc(sem["probs_used"], 2)

            def attend(items):
                for item in items:
                    kind, u = item[0], item[1]
                    if kind == "zT":
                        b = claim_ring(item)
                        pe.wait_ge(sem["za"], at(it, "za", 1))
                        transposes(PS[:, b, :], za)
                        pe.wait_ge(sem["zb"], at(it, "zb", 1))
                        transposes(PS[:, b + 1, :], zb).then_inc(sem["ring_full"], 1)
                    elif kind == "qk0":
                        b = claim_ring(item)
                        if (now.ring[item] - now.ring[("zT", 0)]) % 2:
                            drained(("zT", 0))
                        nc.tensor.matmul(PS[:, b, :], W0[:, 0, :], zaT, start=True, stop=True)
                        nc.tensor.matmul(PS[:, b + 1, :], W0[:, 1, :], zaT, start=True, stop=True)\
                            .then_inc(sem["ring_full"], 1)
                    elif kind == "v0":
                        b = claim_ring(item)
                        by_rows(PS[:, b + 1, :], zbT, W1[:, 256:320], width=64)
                        by_rows(PS[:, b, :], zaT, W0[:, 2, :]).then_inc(sem["ring_full"], 1)
                    elif kind == "q1":
                        b = claim_ring(item)
                        nc.tensor.matmul(PS[:, b, :], W1[:, 0:128], zbT, start=True, stop=True)
                        nc.tensor.matmul(PS[:, b + 1, :], W1[:, 128:256], zbT, start=True, stop=True)\
                            .then_inc(sem["ring_full"], 1)
                    elif kind == "latT":
                        claim_small(item)
                        pe.wait_ge(sem["lat"], at(it, "lat", 1))
                        for t in range(TT):
                            mm = nc.tensor.matmul(SM[0:64, t * 128:(t + 1) * 128], lat[:, t, :], ident[:],
                                                  start=True, stop=True)
                        mm.then_inc(sem["small_full"], 1)
                    elif kind == "k1":
                        pe.wait_ge(sem["small_free"], at(it, "small_free", now.small[("latT", 0)] + 1))
                        b = claim_ring(item)
                        nc.tensor.matmul(PS[:, b, :], W1k[:, 0, :], latT[0:64], start=True, stop=True)
                        nc.tensor.matmul(PS[:, b + 1, :], W1k[:, 1, :], latT[0:64], start=True, stop=True)\
                            .then_inc(sem["ring_full"], 1)
                    elif kind == "v1":
                        b = claim_ring(item)
                        by_rows(PS[:, b, :], latT, W1k[:, 2, :], k=64).then_inc(sem["ring_full"], 1)
                    elif kind == "mx":
                        if item[2:] == (0, 0):
                            pe.wait_ge(*stack_ready(it, now, u))
                        row_max(*item[1:])
                    elif kind == "mrow":
                        claim_small(item)
                        pe.wait_ge(sem["nmax_parts"], at(it, "nmax_parts", now.nth[u]))
                        for t in range(TT):
                            mm = nc.tensor.transpose(
                                PS[0:16, SMB, :].bitcast(BF16)[:, t * 128:(t + 1) * 128],
                                nmp[:, u % 2, t].rearrange("p a h -> p (a h)"), identb[:])
                        mm.then_inc(sem["small_full"], 1)
                    elif kind == "st":
                        if item[2:] == (0, 0, 0):
                            pe.wait_ge(*nmax_ready(it, now.nth_stack[u] if u else 0, u % 2))
                        scores_t(*item[1:])
                    elif kind == "pv":
                        values(*item[1:])
                    elif kind == "fin":
                        pe.wait_ge(sem["pv_free"], at(it, "pv_free", now.pv[("quad", u, item[2])] + 1))
                        claim_small(item)
                        for t in range(TT):
                            mm = nc.tensor.transpose(SM[:, t * 128:(t + 1) * 128], rows_of(oq, t), ident[:])
                        mm.then_inc(sem["small_full"], 1)
                    elif kind == "woT":
                        claim_small(item)
                        transposes(SM, token_outputs(u)).then_inc(sem["small_full"], 1)
                    elif kind == "wo":
                        claim_small(item)
                        wo = (W0[:, 3, :], W1[:, 320:448], W2[:, 3, :])[u]
                        by_rows(SM, oT, wo).then_inc(sem["small_full"], 1)
                    elif kind == "z2T":
                        claim_small(item)
                        pe.wait_ge(sem["z2"], at(it, "z2", 1))
                        transposes(SM, za).then_inc(sem["small_full"], 1)
                    elif kind == "gate0":
                        claim_small(item)
                        by_rows(SM, z2T, gate0[:], width=E0).then_inc(sem["small_full"], 1)
                    elif kind == "ohT":
                        claim_small(item)
                        pe.wait_ge(sem["onehot"], at(it, "onehot", 1))
                        for t in range(TT):
                            mm = nc.tensor.transpose(SM[0:E0, t * 128:(t + 1) * 128], g0[:, 2, t, :], ident[:])
                        mm.then_inc(sem["small_full"], 1)
                    elif kind == "moe0":
                        n = item[1]
                        if n == 0:
                            claim_max("acc0")
                            pe.wait_ge(sem["small_free"], at(it, "small_free", now.small[("ohT", 0)] + 1))
                            nc.tensor.matmul(ACC0, b2row[:], ohT[:], start=True, stop=False)\
                                .then_inc(sem["max_full"], 1)
                        b = claim_ring(item)
                        for i in range(2):
                            tile = 2 * n + i
                            nc.tensor.matmul(PS[:, b + i, :], sel0[:, tile // TT, :], penT[:], start=True, stop=False)
                            mm = nc.tensor.matmul(PS[:, b + i, :], up0[:, tile, :], z2T, start=False, stop=True)
                        mm.then_inc(sem["ring_full"], 1)
                    elif kind == "down0":
                        n = item[1]
                        drained(("moe0", n))
                        slot = now.tiles[("moe0", n)] % 4
                        for i in range(2):
                            mm = nc.tensor.matmul(ACC0, down0[:, 2 * n + i, :], probs[:, slot, i, :],
                                                  start=False, stop=(2 * n + i == HT - 1))
                        mm.then_inc(sem["probs_used"], 1)
                    elif kind in ("y0", "y1"):
                        if kind == "y0":
                            c = now.maxima["acc0"]
                            pe.wait_ge(sem[f"max_free{c % 2}"], at(it, f"max_free{c % 2}", c // 2 + 1))
                        else:
                            pe.wait_ge(sem["pv_free"], at(it, "pv_free", now.pv["acc1"] + 1))
                        claim_small(item)
                        for t in range(TT):
                            mm = nc.tensor.transpose(SM[:, t * 128:(t + 1) * 128], rows_of(t2, t), ident[:])
                        mm.then_inc(sem["small_full"], 1)
                    elif kind == "combT":
                        claim_small(item)
                        pe.wait_ge(sem["comb"], at(it, "comb", 1))
                        for t in range(TT):
                            mm = nc.tensor.transpose(SM[0:E1, t * 128:(t + 1) * 128], lg[:, 3, t, :], ident[:])
                        mm.then_inc(sem["small_full"], 1)
                    elif kind == "moe1":
                        n = item[1]
                        b = claim_ring(item)
                        gw, uw = (shared[:, 0, :], shared[:, 1, :]) if n == HT else (gw1[:, n, :], uw1[:, n, :])
                        nc.tensor.matmul(PS[:, b, :], gw, hT, start=True, stop=True)
                        nc.tensor.matmul(PS[:, b + 1, :], uw, hT, start=True, stop=True).then_inc(sem["ring_full"], 1)
                    elif kind == "comb":
                        if item[1] == 0:
                            pe.wait_ge(sem["combS"], at(it, "combS", 1))
                        b = claim_max(item)
                        nc.tensor.matmul(PS[:, b, :], sel1[:, item[1], :], combS[:], start=True, stop=True)\
                            .then_inc(sem["max_full"], 1)
                    elif kind == "down1":
                        n = item[1]
                        if n == HT:
                            drained(("moe1", n))
                            pe.wait_ge(sem["pv_free"], at(it, "pv_free", now.pv["acc1"]))
                        else:
                            c = now.maxima[("comb", n)]
                            pe.wait_ge(sem[f"max_free{c % 2}"], at(it, f"max_free{c % 2}", c // 2 + 1))
                        lhs = shared[:, 2, :] if n == HT else dw1[:, n, :]
                        nc.tensor.matmul(PVT, lhs, probs[:, now.tiles[("moe1", n)] % 4, 0, :], start=(n == HT),
                                         stop=(n == HT - 1))\
                            .then_inc(sem["probs_used"], 1)

            attend(OPENING)
            with pe.Fori(0, batches) as it:
                now = TURN
                attend(LAYER0)

                b = claim_ring("hT")
                pe.wait_ge(sem["xn"], at(it, "xn", 1))
                transposes(PS[:, b, :], xn).then_inc(sem["ring_full"], 1)
                drained("hT")
                claim_small("gate1")
                by_rows(SM, hT, router[:], width=E1).then_inc(sem["small_full"], 1)
                b = claim_ring("hid")
                for i in range(2):
                    mm = nc.tensor.matmul(PS[:, b + i, :], W2[:, 4 + i, :], hmT, start=True, stop=True)
                mm.then_inc(sem["ring_full"], 1)
                drained("hid")
                b = claim_ring("met")
                for i in range(2):
                    mm = nc.tensor.matmul(PS[:, b, :], W2[:, 6 + i, :], h1[:, i, :], start=(i == 0), stop=(i == 1))
                mm.then_inc(sem["ring_full"], 1)
                b = claim_ring("vT")
                pe.wait_ge(sem["vrow"], at(it, "vrow", 1))
                transposes(PS[:, b, :], zb).then_inc(sem["ring_full"], 1)
                drained("vT")
                b = claim_ring("qk2")
                nc.tensor.matmul(PS[:, b, :], W2[:, 0, :], vT, start=True, stop=True)
                nc.tensor.matmul(PS[:, b + 1, :], W2[:, 1, :], vT, start=True, stop=True)\
                    .then_inc(sem["ring_full"], 1)
                b = claim_ring("v2")
                by_rows(PS[:, b, :], vT, W2[:, 2, :]).then_inc(sem["ring_full"], 1)

                attend(LAYER1)

        @block.scalar
        def _(act):
            act.wait_ge(loads, N_LOADS)
            act.wait_ge(built, 6)
            tab = probs[:].rearrange("p a b t -> p (a b t)").rearrange("p (h c) -> p h c", h=H)
            act.wait_ge(bias, H)
            act.activation(biasT[:, 0], tab, ACT.Copy).then_inc(bias, 1)
            act.wait_ge(bias, 2 * H + 5)
            act.activation(biasS[:, 0], tab, ACT.Copy).then_inc(bias, 1)

            act.dma_start(xt[:], x[0].rearrange("(t p) c -> p t c", p=128)).then_inc(sem["x_in"], 16)

            now, it = BEFORE, None

            def full(key):
                act.wait_ge(sem["ring_full"], at(it, "ring_full", now.ring[key] + 1))
                return 2 * (now.ring[key] % 2), sem[f"ring_free{now.ring[key] % 2}"]

            def small(key):
                act.wait_ge(sem["small_full"], at(it, "small_full", now.small[key] + 1))

            def by_token(dst, src, scale):
                for t in range(TT):
                    last = act.activation(dst[:, t, :], src[:, t, :], ACT.Copy, scale=scale[:, t:t + 1])
                return last

            def v_columns(v):
                return v[:].rearrange("p t h c -> p (t h) c")[:, :, 0:DH]

            def v_source(b):
                return PS[:, b, :].rearrange("p (n d) -> p n d", d=DH)

            def attend(items):
                for item in items:
                    kind, u = item[0], item[1]
                    if kind == "xn":
                        act.wait_ge(sem["rstd"], at(it, "rstd", now.first["rstd"] + 1))
                        act.wait_ge(sem["xn"], at(it, "xn", now.first["xn"] + 1))
                        by_token(za, xn, st[:, 4, :]).then_inc(sem["za"], 1)
                    elif kind == "zT":
                        b, free = full(item)
                        act.activation(zaT, PS[:, b, :], ACT.Identity, scale=gamma, bias=beta).then_inc(free, 1)
                        act.activation(zbT, PS[:, b + 1, :], ACT.Copy, scale=norm1).then_inc(free, 1)
                    elif kind == "qk0":
                        b, _ = full(item)
                        if now is TURN:
                            act.wait_ge(sem["scr_w"], at(it, "scr_w", now.first["scr_w"]))
                        act.activation(q3[:, 0, :], PS[:, b, :], ACT.Copy, scale=RSQ8).then_inc(sem["hi"], 1)
                        act.activation(k3[:, 2, :], PS[:, b + 1, :], ACT.Copy).then_inc(sem["hi"], 1)
                    elif kind == "v0":
                        b, free = full(item)
                        act.activation(lat[:].rearrange("p t c -> p (t c)"), PS[:, b + 1, 0:TT * 64], ACT.Copy)\
                            .then_inc(free, 1)
                        act.activation(v_columns(va), v_source(b), ACT.Copy).then_inc(free, 1)
                    elif kind == "latT":
                        small(item)
                        act.wait_ge(sem["parts"], at(it, "parts", now.first["parts"] + 2))
                        act.activation(latT[0:64], SM[0:64], ACT.Identity, scale=ln_g[0:64], bias=ln_b[0:64])\
                            .then_inc(sem["small_free"], 1)
                    elif kind == "q1hi":
                        act.wait_ge(sem["scr_w"], at(it, "scr_w", now.first["scr_w"] + 96))
                        act.wait_ge(sem["roped"], at(it, "roped", 1))
                        act.activation(q3[:, 0, :], qf, ACT.Copy).then_inc(sem["hi"], 1)
                    elif kind == "k1hi":
                        act.wait_ge(sem["roped"], at(it, "roped", 2))
                        act.activation(k3[:, 2, :], kf, ACT.Copy).then_inc(sem["hi"], 1)
                    elif kind == "x":
                        act.wait_ge(sem["acc"], at(it, "acc", 1))
                        act.dma_start(xt[:], x[it + 1].rearrange("(t p) c -> p t c", p=128)).then_inc(sem["x_in"], 16)
                    elif kind == "v1":
                        b, free = full(item)
                        act.activation(v_columns(vb), v_source(b), ACT.Copy).then_inc(free, 2)
                    elif kind == "mrow":
                        small(item)
                        if u == 1:
                            act.wait_ge(*nmax_ready(it, 0, 0))
                        elif now is TURN:
                            had = (u - 1) % 6
                            act.wait_ge(*nmax_ready(it, now.nth_stack[had], had % 2))
                        act.activation(nmrow[:], PS[0:16, SMB, :].bitcast(BF16)[:, 0:T], ACT.Copy)\
                            .then_inc(sem["small_free"], 1)
                    elif kind == "st":
                        a = UNITS[u][0]
                        n, w = now.tiles[item], step_width(a, item[4])
                        act.wait_ge(sem["probs_used"], at(it, "probs_used", max(n - 3, 0)))
                        b, free = full(item)
                        act.activation(probs[:, n % 4, :, 0:w], PS[:, b:b + 2, 0:w], ACT.Exp,
                                       scale=1.0 if a == 0 else RSQ8).then_inc(free, 2)
                    elif kind == "pv" and item[3] == len(steps_of(UNITS[u][0])) - 1:
                        q = now.pv[("quad", u, item[2])]
                        if q >= 1 and now.pv_order[q - 1] != "acc1":
                            act.wait_ge(sem["small_full"], at(it, "small_full", now.small[("fin",) + now.pv_order[q - 1][1:]] + 1))
                        act.wait_ge(sem["probs_used"], at(it, "probs_used", now.tiles[("st", u, item[2], 1, item[3])] + 1))
                        act.activation(oq[:], PVT, ACT.Copy).then_inc(sem["pv_free"], 1)
                    elif kind == "woT":
                        small(item)
                        act.activation(oT[:], SM, ACT.Copy).then_inc(sem["small_free"], 1)
                    elif kind == "wo" and u == 2:
                        act.wait_ge(sem["small_free"], at(it, "small_free", now.small[item] + 1))
                        for t in range(TT):
                            last = act.activation(zb[:, t, 1:], za[:, t, 1:], ACT.Square, accum_out=st[:, 6, t:t + 1])
                        last.then_inc(sem["ssq"], 1)
                    elif kind == "wo" and u == 1:
                        act.wait_ge(sem["small_free"], at(it, "small_free", now.small[item] + 1))
                        for t in range(TT):
                            last = act.activation(za[:, t, :], x2[:, t, :], ACT.Square, accum_out=st[:, 6, t:t + 1])
                        last.then_inc(sem["ssq"], 1)
                        act.wait_ge(sem["rstd"], at(it, "rstd", 1))
                        by_token(za, x2, st[:, 7, :]).then_inc(sem["z2"], 1)
                    elif kind == "z2T":
                        small(item)
                        act.activation(z2T, SM, ACT.Copy, scale=norm2).then_inc(sem["small_free"], 1)
                    elif kind == "moe0" and item[1] % 2 == 0:
                        n, m = item[1], now.tiles[item]
                        act.wait_ge(sem["probs_used"], at(it, "probs_used", m - 3))
                        b, free = full(item)
                        for i in range(2):
                            act.activation(probs[:, m % 4, i, :], PS[:, b + i, :], ACT.Relu, bias=b1e[2 * n + i])\
                                .then_inc(free, 1)
                    elif kind == "y0":
                        act.wait_ge(sem["probs_used"], at(it, "probs_used", now.tiles[("moe0", HT // 2 - 1)] + 1))
                        act.activation(t2, ACC0, ACT.Copy).then_inc(sem["max_free%d" % (now.maxima["acc0"] % 2)], 1)
                    elif kind == "combT":
                        small(item)
                        act.activation(combS[0:E1], SM[0:E1], ACT.Copy).then_inc(sem["comb_hi"], 1)
                    elif kind == "moe1":
                        p = silu_place(item[1])
                        b, _ = full(item)
                        if p == 1:
                            act.wait_ge(sem["combS"], at(it, "combS", 1))
                        elif p == 2:
                            r = now.ring[("moe1", HT)]
                            act.wait_ge(sem[f"ring_free{r % 2}"], at(it, f"ring_free{r % 2}", 2 * (r // 2) + 2))
                        elif p >= 3:
                            c = now.maxima[("comb", p - 3)]
                            act.wait_ge(sem[f"max_free{c % 2}"], at(it, f"max_free{c % 2}", c // 2 + 1))
                        act.activation((t2, rq)[p % 2], PS[:, b, :], ACT.Silu).then_inc(sem["silu"], 1)
                    elif kind == "y1":
                        act.wait_ge(sem["probs_used"], at(it, "probs_used", now.tiles[("moe1", HT - 1)] + 1))
                        act.activation(t2, PVT, ACT.Copy).then_inc(sem["pv_free"], 1)

            attend(OPENING)
            with act.Fori(0, batches) as it:
                now = TURN
                attend(LAYER0)

                b, free = full("hT")
                act.activation(hT, PS[:, b, :], ACT.Copy).then_inc(free, 1)
                act.activation(hmT, PS[:, b, :], ACT.Identity, bias=mu0).then_inc(free, 1)
                small("gate1")
                act.activation(lg[:, 0].rearrange("p t e -> p (t e)"), SM[:, 0:TT * E1], ACT.Exp, scale=-1.0)\
                    .then_inc(sem["small_free"], 1)
                b, free = full("hid")
                for i in range(2):
                    act.activation(h1[:, i, :], PS[:, b + i, :], ACT.Tanh, bias=b1m[i]).then_inc(free, 1)
                b, free = full("met")
                act.activation(t1, PS[:, b, :], ACT.Tanh, bias=b2m).then_inc(free, 2)
                act.wait_ge(sem["logm"], at(it, "logm", 1))
                act.activation(st[:, 10, :], st[:, 9, :], ACT.Ln).then_inc(sem["lns"], 1)
                b, free = full("vT")
                act.activation(vT, PS[:, b, :], ACT.Copy).then_inc(free, 2)
                b, _ = full("qk2")
                act.wait_ge(sem["scr_w"], at(it, "scr_w", 0))
                act.activation(k3[:, 2, :], PS[:, b + 1, :], ACT.Copy).then_inc(sem["hi"], 1)
                act.wait_ge(sem["metric"], at(it, "metric", 1))
                act.activation(q3[:, 0, :], qf, ACT.Copy).then_inc(sem["hi"], 1)
                b, free = full("v2")
                act.activation(v_columns(vb), v_source(b), ACT.Copy).then_inc(free, 2)

                attend(LAYER1)
            act.wait_ge(sem["x_in"], batches * 16 + 16)

        @block.vector
        def _(dve):
            count = [0]
            tab = probs[:].rearrange("p a b t -> p (a b t)").rearrange("p (h c) -> p h c", h=H)
            dve.wait_ge(loads, N_LOADS)
            for n, (parts, mask) in enumerate(((biasT, h1[:, 0, 0:256]), (biasS, h1[:, 1, 0:256]))):
                dve.wait_ge(rel_in, 48 + 16 * n)
                base = n * (H + 5)
                for h in range(H):
                    dve.scalar_tensor_tensor(tab[:, h, :], tab[:, h, :], rel_far[h], mask,
                                             ALU.subtract, ALU.add).then_inc(bias, 1)
                dve.wait_ge(bias, base + H + 1)
                dve.tensor_tensor(tab, tab, parts[:, 0], ALU.subtract).then_inc(bias, 1)
                dve.wait_ge(bias, base + H + 2)
                if n == 0:
                    dve.tensor_copy(parts[:, 1], tab).then_inc(bias, 1)
                    dve.wait_ge(bias, base + H + 3)
                    dve.tensor_tensor(parts[:, 2], tab, parts[:, 1], ALU.subtract).then_inc(bias, 2)
                    dve.wait_ge(bias, base + H + 5)
                else:
                    dve.tensor_copy(parts[:, 1], tab).then_inc(bias, 1)
                    dve.wait_ge(bias, base + H + 3)

            now, it = BEFORE, None

            def step(instruction):
                count[0] += 1
                instruction.then_inc(sem["dve"], 1)
                dve.wait_ge(sem["dve"], at(it, "dve", count[0]))

            def full(key):
                dve.wait_ge(sem["ring_full"], at(it, "ring_full", now.ring[key] + 1))
                return 2 * (now.ring[key] % 2), sem[f"ring_free{now.ring[key] % 2}"]

            def small(key):
                dve.wait_ge(sem["small_full"], at(it, "small_full", now.small[key] + 1))

            def statistics(src, width=128):
                for t in range(TT):
                    last = dve.bn_stats(bst[:, t, :], src[:, t, 0:width])
                step(last)
                unfused(nc.vector)
                for t in range(TT):
                    last = dve.bn_aggr(mv[:, t, :], bst[:, t, :])
                last.then_inc(sem["stats"], 1)

            def normalise(dst, src, rstd):
                for t in range(TT):
                    last = dve.tensor_scalar(dst[:, t, :], src[:, t, :], mv[:, t, 0:1], rstd[:, t:t + 1],
                                             ALU.subtract, ALU.mult)
                return last

            def attend(items):
                for item in items:
                    kind, u = item[0], item[1]
                    if kind == "ln":
                        dve.wait_ge(sem["x_in"], at(it, "x_in", 16))
                        statistics(xt)
                    elif kind == "xn":
                        dve.wait_ge(sem["rstd"], at(it, "rstd", now.first["rstd"] + 1))
                        normalise(xn, xt, st[:, 0, :]).then_inc(sem["xn"], 1)
                    elif kind == "qk0":
                        b, free = full(item)
                        dve.wait_ge(sem["hi"], at(it, "hi", now.first["hi"] + 1))
                        dve.scalar_tensor_tensor(rq, PS[:, b, :], RSQ8, q3[:, 0, :], ALU.mult, ALU.subtract)\
                            .then_inc(free, 1)
                        dve.wait_ge(sem["hi"], at(it, "hi", now.first["hi"] + 2))
                        dve.tensor_tensor(rk, PS[:, b + 1, :], k3[:, 2, :], ALU.subtract).then_inc(free, 1)
                    elif kind == "latln":
                        r = now.ring[("v0", 0)]
                        dve.wait_ge(sem[f"ring_free{r % 2}"], at(it, f"ring_free{r % 2}", 2 * (r // 2) + 2))
                        statistics(lat, 64)
                    elif kind == "latn":
                        dve.wait_ge(sem["rstd"], at(it, "rstd", now.first["rstd"] + 2))
                        normalise(lat, lat, st[:, 5, :]).then_inc(sem["lat"], 1)
                    elif kind in ("q1", "k1"):
                        b, free = full(item)
                        if kind == "k1":
                            dve.wait_ge(sem["roped"], at(it, "roped", 1))
                        dve.tensor_tensor(t1, PS[:, b, :], cosT[:], ALU.mult).then_inc(free, 1)
                        dve.tensor_tensor(t2, PS[:, b + 1, :], sinT[:], ALU.mult).then_inc(free, 1)
                    elif kind == "mx":
                        _, _, hl, qt = item
                        a, n = UNITS[u][0], now.maxima[item]
                        keys = T if a == 2 else 128 * (qt + 1)
                        dve.wait_ge(sem["max_full"], at(it, "max_full", n + 1))
                        dve.tensor_reduce(nmax[:, u % 2, qt, hl:hl + 1], PS[:, 5 + n % 2, 0:keys], AX.X,
                                          ALU.max, negate=True).then_inc(sem[f"max_free{n % 2}"], 1)
                        if (hl, qt) == (7, TT - 1):
                            dve.wait_ge(sem[f"max_free{n % 2}"], at(it, f"max_free{n % 2}", n // 2 + 1))
                            dve.wait_ge(sem[f"max_free{(n - 1) % 2}"], at(it, f"max_free{(n - 1) % 2}", (n - 1) // 2 + 1))
                            step(dve.tensor_copy(nmp[:, u % 2, :, 0], nmax[:, u % 2]))
                            dve.tensor_tensor(nmp[:, u % 2, :, 1], nmax[:, u % 2], nmp[:, u % 2, :, 0],
                                              ALU.subtract).then_inc(sem["nmax_parts"], 1)
                    elif kind == "fin":
                        small(item)
                        ps = SM.rearrange("p (t j c) -> p t j c", t=TT, j=4)
                        step(dve.reciprocal(rcp[:].unsqueeze(3), ps[:, :, :, DH:DH + 1]))
                        c0 = 64 * UNITS[u][1] + 32 * item[2]
                        dve.tensor_tensor(token_outputs(UNITS[u][0])[:, :, c0:c0 + 32].rearrange("p t (j d) -> p t j d", d=DH),
                                          ps[:, :, :, 0:DH], rcp[:].unsqueeze(3).broadcast_to((128, TT, 4, DH)),
                                          ALU.mult).then_inc(sem["small_free"], 1)
                    elif kind == "wo":
                        small(item)
                        if u == 0:
                            dve.wait_ge(sem["acc"], at(it, "acc", 2))
                            dve.tensor_tensor(acc[:], acc[:], SM_rows, ALU.add).then_inc(sem["small_free"], 1)
                        elif u == 1:
                            dve.tensor_tensor(x2[:], xn[:], SM_rows, ALU.add).then_inc(sem["small_free"], 1)
                        else:
                            step(dve.tensor_scalar(za[:], SM_rows, 0.1, 8.0, ALU.mult, ALU.min))
                            dve.tensor_scalar(za[:], za[:], -8.0, None, ALU.max).then_inc(sem["small_free"], 1)
                    elif kind == "gate0":
                        small(item)
                        lg0 = SM[:, 0:TT * E0].rearrange("p (t e) -> p t e", t=TT)
                        dve.tensor_tensor(g0[:, 0], lg0, gate_b.unsqueeze(1).broadcast_to((128, TT, E0)), ALU.add)\
                            .then_inc(sem["small_free"], 1)
                        dve.wait_ge(sem["small_free"], at(it, "small_free", now.small[item] + 1))
                        step(dve.tensor_reduce(gm[:, 0], g0[:, 0], AX.X, ALU.max))
                        step(dve.tensor_tensor(g0[:, 1], g0[:, 0], gm[:, 0].unsqueeze(2).broadcast_to((128, TT, E0)),
                                               ALU.is_equal))
                        step(dve.tensor_tensor(g0[:, 0], g0[:, 1], tie_w.unsqueeze(1).broadcast_to((128, TT, E0)),
                                               ALU.mult))
                        step(dve.tensor_reduce(gm[:, 1], g0[:, 0], AX.X, ALU.max))
                        dve.tensor_tensor(g0[:, 2], g0[:, 0], gm[:, 1].unsqueeze(2).broadcast_to((128, TT, E0)),
                                          ALU.is_equal).then_inc(sem["onehot"], 1)
                    elif kind == "ohT":
                        small(item)
                        step(dve.tensor_copy(ohT[0:E0], SM[0:E0]))
                        dve.tensor_scalar(penT[0:E0], SM[0:E0], -MASKED, MASKED, ALU.mult, ALU.add)\
                            .then_inc(sem["small_free"], 1)
                    elif kind == "moe0" and item[1] % 2 == 1:
                        n, m = item[1], now.tiles[item]
                        dve.wait_ge(sem["probs_used"], at(it, "probs_used", m - 3))
                        b, free = full(item)
                        for i in range(2):
                            dve.tensor_scalar(probs[:, m % 4, i, :], PS[:, b + i, :], b1e[2 * n + i], 0.0,
                                              ALU.add, ALU.max).then_inc(free, 1)
                    elif kind == "y0":
                        small(item)
                        dve.wait_ge(sem["small_free"], at(it, "small_free", now.small[("wo", 0)] + 1))
                        dve.tensor_tensor(acc[:], acc[:], SM_rows, ALU.add).then_inc(sem["small_free"], 1)
                    elif kind == "combT":
                        dve.wait_ge(sem["comb_hi"], at(it, "comb_hi", 1))
                        dve.tensor_tensor(rq[0:E1], SM[0:E1], combS[0:E1], ALU.subtract).then_inc(sem["small_free"], 1)
                        dve.wait_ge(sem["small_free"], at(it, "small_free", now.small[item] + 1))
                        dve.tensor_copy(combS[32:64], rq[0:E1])
                        step(dve.tensor_copy(penT[0:E1], rq[0:E1]))
                        dve.tensor_tensor(combS[64:96], rq[0:E1], penT[0:E1], ALU.subtract).then_inc(sem["combS"], 1)
                    elif kind == "comb" or item == ("moe1", HT):
                        n = item[1]
                        key = ("moe1", n)
                        m, r, s = now.tiles[key], now.ring[key], (t2, rq)[silu_place(n) % 2]
                        dve.wait_ge(sem["silu"], at(it, "silu", silu_place(n) + 1))
                        b, free = full(key)
                        if n == HT:
                            dve.wait_ge(sem["probs_used"], at(it, "probs_used", m - 3))
                            dve.tensor_tensor(probs[:, m % 4, 0, :], s, PS[:, b + 1, :], ALU.mult).then_inc(free, 2)
                            continue
                        dve.tensor_tensor(s, s, PS[:, b + 1, :], ALU.mult).then_inc(free, 2)
                        dve.wait_ge(sem[f"ring_free{r % 2}"], at(it, f"ring_free{r % 2}", 2 * (r // 2) + 2))
                        c = now.maxima[item]
                        dve.wait_ge(sem["max_full"], at(it, "max_full", c + 1))
                        dve.wait_ge(sem["probs_used"], at(it, "probs_used", m - 3))
                        dve.tensor_tensor(probs[:, m % 4, 0, :], s, PS[:, 5 + c % 2, :], ALU.mult)\
                            .then_inc(sem[f"max_free{c % 2}"], 1)
                    elif kind == "y1":
                        small(item)
                        dve.tensor_tensor(acc[:], acc[:], SM_rows, ALU.add).then_inc(sem["small_free"], 1)

            attend(OPENING)
            counted_before["dve"], count[0] = count[0], 0
            with dve.Fori(0, batches) as it:
                now = TURN
                attend(LAYER0)

                dve.wait_ge(sem["small_free"], at(it, "small_free", now.small[("y0", 0)] + 1))
                statistics(acc)
                dve.wait_ge(sem["rstd"], at(it, "rstd", 2))
                normalise(xn, acc, st[:, 0, :]).then_inc(sem["xn"], 1)
                dve.wait_ge(sem["xn"], at(it, "xn", 1))
                step(dve.tensor_scalar(zb[:], xn[:], 8.0, -8.0, ALU.min, ALU.max))
                for t in range(TT):
                    last = dve.tensor_tensor_reduce(out=x2[:, t, 1:], in0=zb[:, t, 1:], in1=zb[:, t, 1:], scale=1.0,
                                                    scalar=0.0, op0=ALU.mult, op1=ALU.add,
                                                    accum_out=st[:, 8, t:t + 1])
                last.then_inc(sem["squares"], 1)
                dve.wait_ge(sem["small_free"], at(it, "small_free", now.small["gate1"] + 1))
                step(dve.tensor_scalar(lg[:, 0], lg[:, 0], 1.0, None, ALU.add))
                step(dve.reciprocal(lg[:, 0], lg[:, 0]))
                step(dve.tensor_tensor(lg[:, 1], lg[:, 0], gate_bias.unsqueeze(1).broadcast_to((128, TT, E1)),
                                       ALU.add))
                four = lg[:, 1].rearrange("p t (g e) -> p t g e", e=E1 // GROUPS)
                for n, (i, op) in enumerate(((0, ALU.max), (0, ALU.min), (2, ALU.max), (2, ALU.min))):
                    last = dve.tensor_tensor(gs[:, n].unsqueeze(3), four[:, :, :, i:i + 1], four[:, :, :, i + 1:i + 2], op)
                step(last)
                dve.tensor_tensor(gs[:, 4], gs[:, 0], gs[:, 2], ALU.max)
                dve.tensor_tensor(gs[:, 5], gs[:, 0], gs[:, 2], ALU.min)
                step(dve.tensor_tensor(gs[:, 6], gs[:, 1], gs[:, 3], ALU.max))
                step(dve.tensor_tensor(gs[:, 7], gs[:, 5], gs[:, 6], ALU.max))
                step(dve.tensor_tensor(gs[:, 8], gs[:, 4], gs[:, 7], ALU.add))
                mine = gs[:, 8].unsqueeze(3).broadcast_to((128, TT, GROUPS, GROUPS))
                other = gs[:, 8].unsqueeze(2).broadcast_to((128, TT, GROUPS, GROUPS))
                early = earlier.unsqueeze(1).broadcast_to((128, TT, GROUPS, GROUPS))
                dve.tensor_tensor(gg[:, 0], other, mine, ALU.is_gt)
                step(dve.tensor_tensor(gg[:, 1], other, mine, ALU.is_equal))
                step(dve.tensor_tensor(gg[:, 1], gg[:, 1], early, ALU.mult))
                step(dve.tensor_tensor(gg[:, 0], gg[:, 0], gg[:, 1], ALU.add))
                step(dve.tensor_reduce(gs[:, 9], gg[:, 0], AX.X, ALU.add))
                step(dve.tensor_scalar(gs[:, 9], gs[:, 9], float(TOPG), None, ALU.is_lt))
                step(dve.tensor_tensor(lg[:, 2].rearrange("p t (g e) -> p t g e", e=E1 // GROUPS), four,
                                       gs[:, 9].unsqueeze(3).broadcast_to((128, TT, GROUPS, E1 // GROUPS)), ALU.mult))
                unfused(nc.vector)
                for t in range(TT):
                    last = dve.max(top[:, t, :], lg[:, 2, t, :])
                step(last)
                unfused(nc.vector)
                for t in range(TT):
                    last = dve.match_replace(lg[:, 1, t, :], top[:, t, :], lg[:, 2, t, :], MASKED)
                step(last)
                step(dve.tensor_scalar(lg[:, 2], lg[:, 1], MASKED, None, ALU.is_equal))
                step(dve.tensor_tensor(lg[:, 2], lg[:, 2], lg[:, 0], ALU.mult))
                step(dve.tensor_reduce(gm[:, 0], lg[:, 2], AX.X, ALU.add))
                step(dve.tensor_scalar(gm[:, 0], gm[:, 0], 1e-20, None, ALU.add))
                step(dve.reciprocal(gm[:, 1], gm[:, 0]))
                step(dve.tensor_tensor(lg[:, 2], lg[:, 2], gm[:, 1].unsqueeze(2).broadcast_to((128, TT, E1)), ALU.mult))
                dve.tensor_scalar(lg[:, 3], lg[:, 2], 2.5, None, ALU.mult).then_inc(sem["comb"], 1)
                dve.wait_ge(sem["logm"], at(it, "logm", 2))
                step(dve.reciprocal(st[:, 12, :], st[:, 12, :]))
                step(dve.tensor_tensor(st[:, 13, :], st[:, 11, :], st[:, 12, :], ALU.mult))
                for t in range(TT):
                    last = dve.tensor_scalar(zb[:, t, :], zb[:, t, :], st[:, 13, t:t + 1], None, ALU.mult)
                step(last)
                dve.tensor_tensor(zb[:, :, 0:1], st[:, 13, :].unsqueeze(2), st[:, 14, :].unsqueeze(2), ALU.mult)\
                    .then_inc(sem["vrow"], 1)
                met = now.ring["met"]
                dve.wait_ge(sem[f"ring_free{met % 2}"], at(it, f"ring_free{met % 2}", 2 * (met // 2) + 2))
                step(dve.tensor_scalar(t1, t1, 0.1, eta, ALU.mult, ALU.add))
                b, free = full("qk2")
                dve.tensor_tensor(qf, PS[:, b, :], t1, ALU.mult).then_inc(sem["metric"], 1)
                dve.wait_ge(sem["hi"], at(it, "hi", 1))
                dve.tensor_tensor(rk, PS[:, b + 1, :], k3[:, 2, :], ALU.subtract).then_inc(free, 2)

                attend(LAYER1)
                dve.wait_ge(sem["x0"], at(it, "x0", 1))
                dve.tensor_tensor(acc[:, :, 1:], acc[:, :, 1:], za[:, :, 1:], ALU.add)
                dve.tensor_tensor(acc[:, :, 0:1], acc[:, :, 0:1], st[:, 9, :].unsqueeze(2), ALU.add)\
                    .then_inc(sem["x0"], 1)

            counted["dve"] = count[0]

        @block.gpsimd
        def _(pool):
            count = [0]
            pool.memset(qst[:], 0.0).then_inc(built, 1)
            pool.memset(kst[:], 0.0).then_inc(built, 1)
            pool.memset(b2row[:], 0.0).then_inc(built, 1)
            for n, c in enumerate(CONSTANTS):
                last = pool.memset(const[:, n, :], c)
            last.then_inc(built, 1)
            for t in (va, vb):
                pool.memset(t[:], 0.0)
            pool.memset(ohT[:], 0.0)
            pool.memset(penT[:], 0.0)
            pool.memset(combS[:], 0.0)
            pool.memset(st[:], 0.0).then_inc(built, 1)
            pool.wait_ge(built, 5)
            for t in (va, vb):
                last = pool.memset(t[:].rearrange("p t h c -> p (t h) c")[:, :, DH:DH + 1], 1.0)
            last.then_inc(built, 1)
            pool.wait_ge(built, 6)
            for name in PRIMED:
                pool.sem_inc(sem[name], 1)

            now, it = BEFORE, None

            def step(instruction):
                count[0] += 1
                instruction.then_inc(sem["pool"], 1)
                pool.wait_ge(sem["pool"], at(it, "pool", count[0]))

            def with_constant(dst, src, op, c):
                return pool.tensor_tensor(dst, src, const[:, CONSTANTS.index(c), :], op)

            def add(dst, src, c):
                return with_constant(dst, src, ALU.add, c)

            def at_least(dst, src, c):
                unfused(nc.gpsimd)
                return pool.tensor_scalar(dst, src, c, None, ALU.max)

            def power(dst, src, c):
                return with_constant(dst, src, ALU.pow, c)

            def sum_power(dst, src, c, exponent):
                step(add(dst, src, c))
                return power(dst, dst, exponent)

            def parts(dst, mid, lo, rest):
                unfused(nc.gpsimd)
                step(pool.tensor_copy(dst[:, mid, :], rest))
                pool.tensor_tensor(dst[:, lo, :], rest, dst[:, mid, :], ALU.subtract)\
                    .then_inc(sem["parts"], 1)

            S = [st[:, n, :] for n in range(16)]
            def first_stage():
                pool.wait_ge(sem["stats"], at(it, "stats", now.first["stats"] + 1))
                step(sum_power(S[0], mv[:, :, 1], 1e-5, -0.5))
                step(pool.tensor_tensor(S[2], S[0], S[0], ALU.mult))
                step(pool.tensor_tensor(S[3], S[2], mv[:, :, 1], ALU.mult))
                step(sum_power(S[4], S[3], 1e-5, -0.5))
                sum_power(S[2], S[3], 1e-6, -0.5).then_inc(sem["rstd"], 1)
                pool.wait_ge(sem["rstd"], at(it, "rstd", now.first["rstd"] + 1))
                pool.wait_ge(sem["xn"], at(it, "xn", now.first["xn"] + 1))
                unfused(nc.gpsimd)
                for t in range(TT):
                    last = pool.tensor_scalar(zb[:, t, :], xn[:, t, :], S[2][:, t:t + 1], None, ALU.mult)
                last.then_inc(sem["zb"], 1)
                qk0 = now.ring[("qk0", 0)]
                pool.wait_ge(sem[f"ring_free{qk0 % 2}"], at(it, f"ring_free{qk0 % 2}", 2 * (qk0 // 2) + 2))
                parts(q3, 1, 2, rq)
                parts(k3, 1, 0, rk)
                pool.wait_ge(sem["stats"], at(it, "stats", now.first["stats"] + 2))
                sum_power(S[5], mv[:, :, 1], 1e-5, -0.5).then_inc(sem["rstd"], 1)
                for n, (key, full, first, p3, mid, lo) in enumerate(((("q1", 0), qf, 0, q3, 1, 2), (("k1", 0), kf, 2, k3, 1, 0))):
                    r = now.ring[key]
                    pool.wait_ge(sem[f"ring_free{r % 2}"], at(it, f"ring_free{r % 2}", 2 * (r // 2) + 2))
                    pool.tensor_tensor(full, t1, t2, ALU.add).then_inc(sem["roped"], 1)
                for n, (full, first, p3, mid, lo) in enumerate(((qf, 0, q3, 1, 2), (kf, 2, k3, 1, 0))):
                    pool.wait_ge(sem["hi"], at(it, "hi", now.first["hi"] + 3 + n))
                    step(pool.tensor_tensor(full, full, p3[:, first, :], ALU.subtract))
                    parts(p3, mid, lo, full)

            first_stage()
            counted_before["pool"], count[0] = count[0], 0
            with pool.Fori(0, batches) as it:
                now = TURN
                pool.wait_ge(sem["xn"], at(it, "xn", 0))
                pool.tensor_tensor(acc[:], xt[:], xn[:], ALU.add).then_inc(sem["acc"], 1)
                pool.wait_ge(sem["ssq"], at(it, "ssq", 1))
                step(with_constant(S[7], S[6], ALU.mult, 1.0 / D))
                sum_power(S[7], S[7], 1e-6, -0.5).then_inc(sem["rstd"], 1)
                pool.tensor_tensor(acc[:], acc[:], x2[:], ALU.add).then_inc(sem["acc"], 1)
                pool.wait_ge(sem["stats"], at(it, "stats", 1))
                sum_power(S[0], mv[:, :, 1], 1e-5, -0.5).then_inc(sem["rstd"], 1)
                pool.wait_ge(sem["squares"], at(it, "squares", 1))
                step(add(S[9], S[8], 1.0))
                step(sum_power(S[9], S[9], 1e-6, 0.5))
                step(at_least(S[10], S[9], 1.0 + 1e-6))
                step(pool.tensor_tensor(S[14], S[9], S[10], ALU.subtract))
                add(S[11], S[10], -1.0)
                step(add(S[12], S[10], 1.0))
                step(pool.tensor_tensor(S[11], S[11], S[12], ALU.mult))
                step(power(S[11], S[11], 0.5))
                pool.tensor_tensor(S[9], S[11], S[10], ALU.add).then_inc(sem["logm"], 1)
                step(pool.tensor_tensor(S[12], S[14], S[14], ALU.mult))
                step(pool.tensor_tensor(S[12], S[8], S[12], ALU.subtract))
                step(at_least(S[12], S[12], 1e-6))
                step(power(S[12], S[12], 0.5))
                step(add(S[12], S[12], 1e-6))
                pool.wait_ge(sem["lns"], at(it, "lns", 1))
                at_least(S[11], S[10], 1e-3).then_inc(sem["logm"], 1)
                r = now.ring["qk2"]
                pool.wait_ge(sem[f"ring_free{r % 2}"], at(it, f"ring_free{r % 2}", 2 * (r // 2) + 2))
                parts(k3, 1, 0, rk)
                pool.wait_ge(sem["hi"], at(it, "hi", 2))
                step(pool.tensor_tensor(qf, qf, q3[:, 0, :], ALU.subtract))
                parts(q3, 1, 2, qf)
                first_stage()
                pool.wait_ge(sem["ssq"], at(it, "ssq", 2))
                step(add(S[9], S[6], 1.0))
                sum_power(S[9], S[9], 1e-6, 0.5).then_inc(sem["x0"], 1)
                pool.wait_ge(sem["x0"], at(it, "x0", 2))
                pool.dma_start(out[it].rearrange("(t p) c -> p t c", p=128), acc[:]).then_inc(sem["out_done"], 16)
                pool.wait_ge(sem["out_done"], at(it, "out_done", 16))
            counted["pool"] = count[0]
    return counted_before, counted


def _host(x):
    f, bf = np.float32, mybir.dt.np(BF16)
    con = np.ascontiguousarray
    i = {k: np.asarray(v) for k, v in x.items()}
    t = lambda w: w.T
    swap = np.array([h * DH + (d + DH // 2) % DH for h in range(H) for d in range(DH)])
    pad = lambda v, n=128: np.concatenate([v, np.zeros(n - v.shape[0], f)])
    mq = t(i["L0_ffn_Wq"])
    uk = t(i["L0_ffn_Wuk"])
    stack = lambda *w: con(np.stack(w, 1))
    tiles = lambda w: con(w.reshape(-1, 128, w.shape[-1]).transpose(1, 0, 2))
    w2 = t(i["L1_attn_W2"])
    w1 = t(i["L1_attn_W1"])
    rel = i["L0_attn_rel"]
    p = np.arange(128)[:, None]
    c = np.arange(256)[None, :]
    far = rel.shape[1] - 1
    eta = np.ones(D, f)
    eta[0] = -1
    mu = np.zeros(D, f)
    mu[0] = -1
    cols = [i["L0_attn_ln_gamma"], i["L0_attn_ln_beta"], i["L0_ffn_norm1_w"], i["L0_ffn_norm2_w"],
            pad(i["L0_ffn_ln_g"]), pad(i["L0_ffn_ln_b"]), i["L1_attn_b2"], eta, mu,
            i["L1_attn_b1"][:128], i["L1_attn_b1"][128:]]
    cols += [np.broadcast_to(rel[h, far], (128,)) for h in range(H)]
    cols += list(i["L0_ffn_b1"].reshape(HT, 128))
    tri = (np.arange(GROUPS)[None, :] < np.arange(GROUPS)[:, None]).astype(f).ravel()
    rows = np.concatenate([i["L0_ffn_gate_b"], np.arange(E0, 0, -1).astype(f), i["L1_ffn_gate_bias"], tri])
    half = DH // 2
    freq = (f(1.0) / f(10000.0) ** (np.arange(half, dtype=f) / f(half))).astype(f)
    ang = np.arange(T, dtype=f)[None, :] * freq[:, None]
    cos, sin = np.cos(ang).astype(f), np.sin(ang).astype(f)
    pick0 = np.zeros((128, E0, 128), f)
    for e in range(E0):
        pick0[e, e] = 1
    pick1 = np.zeros((128, HT, 128), f)
    for n in range(HT):
        for part in range(3):
            pick1[32 * part + 2 * n, n, :64] = 1
            pick1[32 * part + 2 * n + 1, n, 64:] = 1
    sq = np.arange(128)
    return dict(
        x=con(np.concatenate([i["L0_attn_x"], np.zeros((1, T, D), f)])),
        w0=stack(*(t(i["L0_attn_" + n]) for n in ("Wq", "Wk", "Wv", "Wo"))),
        w1=con(np.concatenate([mq, mq[:, swap], t(i["L0_ffn_Wdkv"]), t(i["L0_ffn_Wo"])], 1)),
        w1k=stack(uk, uk[:, swap], t(i["L0_ffn_Wuv"])),
        w2=stack(*(t(i["L1_attn_" + n]) for n in ("Wq", "Wk", "Wv", "Wo")), w1[:, :128], w1[:, 128:],
                 w2[:128], w2[128:]),
        m0_up=con(t(i["L0_ffn_W1"].reshape(HID0, D)).reshape(D, HT, 128)),
        m0_down=tiles(i["L0_ffn_W2"].transpose(0, 2, 1).reshape(HID0, D)),
        m0_b2=con(i["L0_ffn_b2"]), m0_gate=con(t(i["L0_ffn_gate_w"])),
        m1_gate_w=con(t(i["L1_ffn_w_gate"].reshape(HID0, D)).reshape(D, HT, 128)),
        m1_up_w=con(t(i["L1_ffn_w_up"].reshape(HID0, D)).reshape(D, HT, 128)),
        m1_down_w=tiles(i["L1_ffn_w_down"].transpose(0, 2, 1).reshape(HID0, D)),
        m1_shared=stack(*(t(i["L1_ffn_" + n]) for n in ("sh_gate", "sh_up", "sh_down"))),
        m1_router=con(t(i["L1_ffn_gate_w"])),
        cols=con(np.stack(cols, 1)), rows=con(np.broadcast_to(rows, (128, rows.shape[0]))),
        rel_t=con(rel[:, np.clip(c - p, 0, far)].transpose(1, 0, 2).reshape(128, -1)),
        rel_s=con(rel[:, np.clip(128 + p - c, 0, far)].transpose(1, 0, 2).reshape(128, -1)),
        mask_t=np.where(c < p, MASKED, 0).astype(f), mask_s=np.where(c > 128 + p, MASKED, 0).astype(f),
        causal_t=np.where(sq[None] < sq[:, None], MASKED, 0).astype(bf),
        causal_s=np.where(sq[None] > sq[:, None], MASKED, 0).astype(bf),
        rope_cos=con(np.tile(np.concatenate([cos, cos]), (H, 1))),
        rope_sin=con(np.tile(np.concatenate([-sin, sin]), (H, 1))),
        eye=np.eye(128, dtype=f), eye_b=np.eye(128).astype(bf), pick0=pick0.astype(bf), pick1=pick1.astype(bf),
        ones2=np.ones((2, 4, T), bf), zeros2=np.zeros((2, 4, T), bf),
    )


def kernel(**inputs):
    from concourse import bacc as _bacc
    from concourse.bass_utils import run_bass_kernel_spmd as _run

    nc = _bacc.Bacc("TRN2", target_bir_lowering=False, num_devices=1)
    arrays = _host(inputs)
    b = arrays["x"].shape[0] - 1
    args = {n: nc.dram_tensor(f"in_{n}", a.shape, mybir.dt.from_np(a.dtype), kind="ExternalInput").ap()
            for n, a in arrays.items()}
    out = nc.dram_tensor("out_0", (b, T, D), F32, kind="ExternalOutput").ap()
    layers_kernel(nc, b, out=out, before=BEFORE.raised, per=TURN.raised, **args)
    r = _run(nc, [{f"in_{n}": a for n, a in arrays.items()}], core_ids=[0])
    return r.results[0]["out_0"]
```

```python
import concourse.bass as bass
from concourse import mybir
from contextlib import ExitStack
import numpy as np

F32 = mybir.dt.float32
BF16 = mybir.dt.bfloat16
ALU = mybir.AluOpType
ACT = mybir.ActivationFunctionType
AX = mybir.AxisListType

T, D, H, DH = 512, 128, 16, 8
TT = T // 128
HID0, E0 = 2048, 4
E1, TOPK, GROUPS, TOPG = 32, 8, 8, 4
HT = HID0 // 128
MASKED = -1e30
CONSTANTS = [-0.5, 0.5, 1e-5, 1e-6, 1.0, -1.0, 1.0 / D]
RSQ8 = float(1.0 / np.sqrt(8.0))

UNITS = [(0, 0), (1, 0), (1, 1), (0, 1), (2, 0), (2, 1)]
CAUSAL_STEPS = [[(0, 0)], [(1, 0), (3, 384)], [(2, 0)]]
FULL_STEPS = [[(k, 0)] for k in range(4)]


def steps_of(a):
    return FULL_STEPS if a == 2 else CAUSAL_STEPS


def first_query(a, kt):
    return 0 if a == 2 else 128 * kt


def step_width(a, s):
    return sum(T - first_query(a, kt) for kt, _ in steps_of(a)[s])


def keys_of(a, qt):
    return T if a == 2 else 128 * (qt + 1)


def max_items(u):
    if UNITS[u][0] == 2:
        return [("mx", u, ((hl, qt),)) for hl in range(8) for qt in range(TT)]
    out = []
    for hl in range(0, 8, 2):
        out += [((hl, 3),), ((hl, 0), (hl, 2)), ((hl, 1), (hl + 1, 1)), ((hl + 1, 3),), ((hl + 1, 0), (hl + 1, 2))]
    return [("mx", u, tiles) for tiles in out]


def exp_items(u):
    s_n = len(steps_of(UNITS[u][0]))
    out = []
    for n in range(2 * s_n):
        out += [("st", u, n // s_n, pair, n % s_n) for pair in range(2)]
        if n >= 2 and (n - 1) % s_n == 0:
            out.append(("fin", u, (n - 2) // s_n))
        if n >= 1:
            out.append(("pv", u, (n - 1) // s_n, (n - 1) % s_n))
    return out + [("pv", u, 1, s_n - 1), ("fin", u, 1)]


def merged(exps, maxes, lead=0, tail=0):
    end = len(exps) - tail
    out, m = list(exps[:lead]), 0
    for n, item in enumerate(exps[lead:end]):
        out.append(item)
        upto = (n + 1) * len(maxes) // (end - lead)
        out += maxes[m:upto]
        m = upto
    return out, list(exps[end:])


def beside(u, maxes):
    out, rest = merged(exp_items(u), maxes, LEADS[u], TAILS[u])
    return out + [("mrow", (u + 1) % 6)] + rest


def experts0(lo, hi):
    chunks = [[("moe0", lo)]] + [[("moe0", n), ("down0", n - 1)] for n in range(lo + 1, hi)]
    return chunks + [[("down0", hi - 1)]]


def with_experts(exps, first, last):
    before, beside_pv, behind = experts0(0, first), experts0(first, last), experts0(last, HT // 2)
    out = sum(before[:-1], []) + exps[:2] + before[-1]
    for item in exps[2:]:
        out.append(item)
        if item[0] == "pv" and beside_pv:
            out += beside_pv.pop(0)
    return out + sum(behind, [])


def experts1(n, maxes):
    return [("moe1", n)] + maxes[:2] + [("down1", n - 1 if n else HT)] + maxes[2:] + [("comb", n)]


def later(items, *moves):
    out = list(items)
    for item, by in moves:
        n = out.index(item)
        out.insert(n + by, out.pop(n))
    return out


def spread(items, others, first, every):
    out, rest = [], list(others)
    for n, item in enumerate(items):
        out.append(item)
        if n >= first and (n - first) % every == 0 and rest:
            out.append(rest.pop(0))
    return out + rest


LEADS = {0: 3, 1: 3, 2: 4, 4: 0, 5: 3}
TAILS = {0: 8, 1: 8, 4: 8, 5: 7}
SPLIT = 3
MX0, MX3, MX4 = max_items(0), max_items(3), max_items(4)
NORM = [("ln", 0), ("xn", 0)]
PROJECT = [("zT", 0), ("qk0", 0), ("v0", 0), ("latln", 0), ("q1", 0), ("latn", 0), ("q1hi", 0), ("latT", 0),
           ("k1", 0), ("k1hi", 0)]
CHOICE = (MX3[9:11] + [("woT", 1)] + MX3[11:12] + [("wo", 1)] + MX3[12:16] + [("z2T", 0)] + MX3[16:17]
          + [("gate0", 0)] + MX3[17:19] + [("ohT", 0)] + MX3[19:] + [("mrow", 3)])
EARLY1, MX4_A_TILE = 4, 3
EXPERTS1 = [("combT", 0)]
for n in range(HT):
    EXPERTS1 += [NORM[0]] if n == HT - 5 else []
    EXPERTS1 += [NORM[1]] if n == HT - 2 else []
    EXPERTS1 += experts1(n, MX4[max(0, MX4_A_TILE * (n - EARLY1)):max(0, MX4_A_TILE * (n - EARLY1 + 1))])
EXPERTS1.insert(EXPERTS1.index(("moe1", HT - 1)) + 1, ("mrow", 4))
EXPERTS1 += [("down1", HT - 1), ("y1", 0)]
FIRST_STAGE, FIRST_MAXIMA = NORM + PROJECT, MX0 + [("mrow", 0), ("v1", 0)]
OPENING = FIRST_STAGE + FIRST_MAXIMA
LAYER0 = (beside(0, max_items(1)) + beside(1, max_items(2))
          + sum(merged(exp_items(2), MX3[:9], LEADS[2]), []) + CHOICE + with_experts(exp_items(3), 3, 6))
LAYER0 += [("wo", 0), ("y0", 0)]
LAYER0 = later(LAYER0, (("mrow", 1), 2), (("fin", 0, 1), 2), (("mrow", 2), 2), (("fin", 1, 1), 2), (("mrow", 3), 1),
               (("fin", 3, 1), 1))
LAYER0.insert(LAYER0.index(("fin", 1, 0)), ("x", 0))
LAYER0.insert(LAYER0.index(("down0", HT // 2 - 2)), ("woT", 0))
LAYER1 = (EXPERTS1 + spread(beside(4, max_items(5)), PROJECT[:SPLIT], 0, 4)
          + spread(beside(5, MX0), PROJECT[SPLIT:], 0, 4) + [("v1", 0), ("woT", 2), ("wo", 2)])
LAYER1 = later(LAYER1, (("mrow", 5), 2), (("fin", 4, 1), 2), (("mrow", 0), 2))
SHARED = ("moe1", HT)
HEAD1 = ["hT", "hid", "met", SHARED, "vT", "qk2", "v2"]
SMALLS = ["fin", "mrow", "woT", "wo", "z2T", "gate0", "ohT", "y0", "combT", "y1", "latT"]


def of(kinds, items):
    return [i for i in items if i[0] in kinds]


BLOCKS = ((0, 1, 2, 0, 1, 0), (0, 1, 2, 1, 2, 2))
PART_ROWS = 8 * len(BLOCKS[0])
STORED = 16 * 2 * len(BLOCKS[0])
LOADED = 16 * 4


def used_up_in_order():
    made = [i[:3] + i[4:] if i[0] == "st" else i for i in of(["st", "moe0", "moe1"], LAYER0 + [SHARED] + LAYER1)]
    used = []
    for kind, *rest in of(["pv", "down0", "down1"], LAYER0 + LAYER1):
        used += 2 * [("st", *rest)] if kind == "pv" else [("moe" + kind[-1], *rest)]
    return made == used


assert used_up_in_order()


class Uses:

    def __init__(self, ring, maxima, small, pv, tiles, **others):
        self.ring, self.maxima, self.small, self.pv, self.tiles = (
            {k: n for n, k in enumerate(x)} for x in (ring, maxima, small, pv, tiles))
        self.pv_order = pv
        self.raised = dict(
            ring_full=len(ring), ring_free0=2 * ((len(ring) + 1) // 2), ring_free1=2 * (len(ring) // 2),
            max_full=len(maxima), max_free0=(len(maxima) + 1) // 2, max_free1=len(maxima) // 2,
            small_full=len(small), small_free=len(small), pv_free=len(pv), probs_used=len(tiles), **others)


RINGS = ["zT", "qk0", "v0", "q1", "k1", "v1", "st", "moe0", "moe1"]
BEFORE = Uses(
    of(RINGS, OPENING), of(["mx"], OPENING), of(SMALLS, OPENING), [], [],
    x_in=16, out_done=0, stats=2, rstd=2, xn=1, za=1, zb=1, lat=1, hi=4, parts=4, scr_w=2 * STORED,
    stk0=LOADED, stk1=0, nmax0=64, nmax1=0, nmax_parts=1, roped=2, acc=0, ssq=0, z2=0, onehot=0, squares=0,
    vrow=0, logm=0, lns=0, metric=0, summed=0, comb=0, comb_hi=0, combS=0, silu=0, biased=0, dve=3, pool=14)
TURN = Uses(
    of(RINGS, LAYER0) + HEAD1 + of(RINGS, LAYER1),
    of(["mx"], LAYER0) + ["acc0"] + of(["mx", "comb"], LAYER1),
    of(SMALLS, LAYER0) + ["gate1"] + of(SMALLS, LAYER1),
    [("quad", u, g) for u in range(4) for g in range(2)] + ["acc1"] + [("quad", u, g) for u in (4, 5) for g in range(2)],
    of(["st", "moe0", "moe1"], LAYER0 + [SHARED] + LAYER1),
    x_in=16, out_done=16, stats=3, rstd=4, xn=2, za=1, zb=1, lat=1, hi=6, parts=6, scr_w=3 * STORED,
    stk0=3 * LOADED, stk1=3 * LOADED, nmax0=3 * 64, nmax1=3 * 64, nmax_parts=6, roped=2, acc=2, ssq=2, z2=1,
    onehot=1, squares=1, vrow=1, logm=2, lns=1, metric=1, summed=1, comb=1, comb_hi=1, combS=1, silu=HT + 1,
    biased=24, dve=55, pool=33)
BEFORE.first = dict(stats=0, rstd=0, xn=0, hi=0, parts=0, scr_w=0)
TURN.first = dict(stats=1, rstd=2, xn=1, hi=2, parts=2, scr_w=STORED)
BEFORE.nth, BEFORE.nth_stack = {0: 1}, {0: 1}
TURN.nth = {1: 1, 2: 2, 3: 3, 4: 4, 5: 5, 0: 6}
TURN.nth_stack = {2: 1, 4: 2, 0: 3, 1: 1, 3: 2, 5: 3}

PRIMED = ("ring_full", "ring_free0", "ring_free1", "max_free0", "max_free1", "small_free", "pv_free",
          "probs_used")


def layers_kernel(nc, batches, x, out, w0, w1, w1k, w2, m0_up, m0_down, m0_b2, m0_gate, m1_gate_w,
                  m1_up_w, m1_down_w, m1_shared, m1_router, cols, rows, rel_t, rel_s, mask_t, mask_s,
                  causal_t, causal_s, rope_cos, rope_sin, eye, eye_b, pick0, pick1, ones2, zeros2, before, per):
    counted, counted_before = {}, {}
    scr = nc.dram_tensor("scratch_parts", (3, 2, H, PART_ROWS + 2, T), BF16, kind="Internal").ap()
    ctx = ExitStack()
    with ctx:
        def sb(name, shape, dt=F32):
            return ctx.enter_context(nc.sbuf_tensor(name, shape, dt))

        W0 = sb("W0", [128, 4, 128])
        W1 = sb("W1", [128, 448])
        W1k = sb("W1k", [64, 3, 128])
        W2 = sb("W2", [128, 8, 128])
        up0 = sb("up0", [128, HT, 128])
        down0 = sb("down0", [128, HT, 128])
        b2row = sb("b2row", [128, 128])
        gate0 = sb("gate0", [128, E0])
        gw1 = sb("gw1", [128, HT, 128])
        uw1 = sb("uw1", [128, HT, 128])
        dw1 = sb("dw1", [128, HT, 128])
        shared = sb("shared", [128, 3, 128])
        router = sb("router", [128, E1])
        col = sb("col", [128, cols.shape[1]])
        rowc = sb("rowc", [128, rows.shape[1]])
        cosT = sb("cosT", [128, T])
        sinT = sb("sinT", [128, T])
        ident = sb("ident", [128, 128])
        identb = sb("identb", [128, 128], BF16)
        causT = sb("causT", [128, 128], BF16)
        causS = sb("causS", [128, 128], BF16)
        sel0 = sb("sel0", [128, E0, 128], BF16)
        sel1 = sb("sel1", [128, HT, 128], BF16)
        biasT = sb("biasT", [128, H, 256])
        biasS = sb("biasS", [128, H, 256], BF16)
        qst = sb("qst", [128, 2, 8, T], BF16)
        kst = sb("kst", [128, 2, 4, T], BF16)
        q3 = sb("q3", [128, 3, T], BF16)
        k3 = sb("k3", [128, 3, T], BF16)
        va = sb("va", [128, TT, H, 32])
        vb = sb("vb", [128, TT, H, 32])
        probs = sb("probs", [128, 4, 2, T])
        wk = [sb(f"wk{n}", [128, T]) for n in range(6)]
        h1 = sb("h1", [128, 2, T])
        xt, xn, acc = sb("xt", [128, TT, 128]), sb("xn", [128, TT, 128]), sb("acc", [128, TT, 128])
        za, zb = sb("za", [128, TT, 128]), sb("zb", [128, TT, 128])
        otok, oT, oq = sb("otok", [128, TT, 128]), sb("oT", [128, T]), sb("oq", [128, T])
        x2 = sb("x2", [128, TT, 128])
        ohT = sb("ohT", [128, T])
        penT = sb("penT", [128, T], BF16)
        combS = sb("combS", [128, T], BF16)
        lat = sb("lat", [128, TT, 64])
        zaT, zbT, rq, rk, t1, t2 = (w[:] for w in wk)
        qf, kf = h1[:, 0, :], h1[:, 1, :]
        bst = sb("bst", [128, TT, 6])
        mv = sb("mv", [128, TT, 2])
        st = sb("st", [128, 16, TT])
        const = sb("const", [128, len(CONSTANTS), TT])
        nmax = sb("nmax", [128, 2, TT, 8])
        nmp = sb("nmp", [128, 2, TT, 2, 8], BF16)
        nmrow = sb("nmrow", [16, T], BF16)
        spare = sb("spare", [128, 2])
        rcp = sb("rcp", [128, TT, 4])
        g0 = sb("g0", [128, 3, TT, E0])
        gm = sb("gm", [128, 2, TT])
        lg = oq[:].rearrange("p (n t e) -> p n t e", n=4, t=TT)
        gs = oT[:, 0:320].rearrange("p (n t g) -> p n t g", n=10, t=TT)
        top = oT[:, 320:352].rearrange("p (t g) -> p t g", t=TT)
        gg = otok[:].rearrange("p t (n g) -> p (t n) g", n=16).rearrange("p (n t g) h -> p n t g h", n=2, t=TT)

        PS = ctx.enter_context(nc.psum_tensor("PS", [128, 8, T], F32))
        PVB, SMB = 4, 7
        SM = PS[:, SMB, :]
        SM_rows = SM.rearrange("p (t c) -> p t c", t=TT)
        PVT = PS[:, PVB, :]
        ACC0 = PS[:, 5 + TURN.maxima["acc0"] % 2, :]
        z2T, hT, vT, hmT, latT = zaT, zaT, zbT, t1, rk

        sem = {n: ctx.enter_context(nc.semaphore(n)) for n in per}
        loads = ctx.enter_context(nc.semaphore("loads"))
        built = ctx.enter_context(nc.semaphore("built"))
        rel_in = ctx.enter_context(nc.semaphore("rel_in"))
        bias = ctx.enter_context(nc.semaphore("bias"))
        first_loads = ctx.enter_context(nc.semaphore("first_loads"))
        block = ctx.enter_context(nc.Block())

        gamma, beta, norm1, norm2, ln_g, ln_b, b2m, eta, mu0 = (col[:, n:n + 1] for n in range(9))
        b1m = [col[:, 9 + n:10 + n] for n in range(2)]
        rel_far = [col[:, 11 + n:12 + n] for n in range(H)]
        b1e = [col[:, 27 + n:28 + n] for n in range(HT)]
        gate_b, tie_w = rowc[:, 0:E0], rowc[:, E0:2 * E0]
        gate_bias = rowc[:, 8:8 + E1]
        earlier = rowc[:, 40:40 + GROUPS * GROUPS].rearrange("p (a b) -> p a b", a=GROUPS)
        FIRST = [(col, cols), (rowc, rows), (ident, eye), (W0, w0), (W1, w1), (W1k, w1k), (cosT, rope_cos),
                 (sinT, rope_sin), (identb, eye_b)]
        LOADS = [(causT, causal_t), (causS, causal_s), (up0, m0_up), (down0, m0_down), (gate0, m0_gate),
                 (sel0, pick0), (W2, w2), (gw1, m1_gate_w), (uw1, m1_up_w), (dw1, m1_down_w),
                 (shared, m1_shared), (router, m1_router), (sel1, pick1)]
        N_FIRST = 16 * (len(FIRST) + 3)
        N_LOADS = 16 * (len(LOADS) + 5)
        tab = probs[:].rearrange("p a b t -> p (a b t)")
        tab_heads = tab.rearrange("p (h c) -> p h c", h=H)
        masks = x2[:].rearrange("p t c -> p (t c)").rearrange("p (n c) -> p n c", n=2)
        BIAS_S = H + 1
        BIAS_T = BIAS_S + H

        def token_outputs(a):
            return zb if a == 0 else otok

        def rows_of(t, n):
            return t[:, n * 128:(n + 1) * 128]

        def at(it, name, n):
            n += name in PRIMED
            return n if it is None else it * per[name] + (before[name] + n)

        def stack_ready(it, now, u):
            name = f"stk{u % 2}"
            return sem[name], at(it, name, now.nth_stack[u] * LOADED)

        def nmax_ready(it, n, slot):
            name = f"nmax{slot}"
            return sem[name], at(it, name, 64 * n)

        def biased_place(item):
            return [i for i in of(["st"], LAYER0) if UNITS[i[1]][0] == 0].index(item) + 1

        def silu_place(n):
            return 0 if n == HT else n + 1

        def unfused(engine):
            n = 0 if engine is nc.vector else 1
            engine.tensor_tensor(spare[:, n:n + 1], const[:, 0, 0:1], const[:, 0, 0:1], ALU.mult)

        def stack_freed(now, u):
            if u == 1 or now is BEFORE:
                return 0
            had = 4 if u == 0 else u - 2
            return now.ring[("st", had, 1, 1, len(steps_of(UNITS[had][0])) - 1)] + 1

        @block.sync
        def _(sp):
            for t, d in FIRST:
                sp.dma_start(t[:], d).then_inc(first_loads, 16)
            for a in range(3):
                sp.dma_start(scr[a, 0, :, PART_ROWS:], zeros2).then_inc(first_loads, 16)
            for n, mask in enumerate((mask_t, mask_s)):
                sp.dma_start(masks[:, n, :], mask).then_inc(rel_in, 16)
            sp.dma_start(tab, rel_s).then_inc(rel_in, 16)
            sp.dma_start(biasT[:].rearrange("p h c -> p (h c)"), rel_t).then_inc(rel_in, 16)
            for t, d in LOADS:
                sp.dma_start(t[:], d).then_inc(loads, 16)
            sp.wait_ge(built, 4)
            sp.dma_start(b2row[0:E0, :], m0_b2).then_inc(loads, 16)
            for s in range(2):
                for g in range(2):
                    sp.dma_start(kst[64 * g + 48:64 * g + 50, s], ones2).then_inc(loads, 16)
            sp.wait_ge(first_loads, N_FIRST)

            now, it = BEFORE, None

            def store_parts(a):
                def blocks(n, parts):
                    for block, part in enumerate(BLOCKS[n]):
                        if part in parts:
                            sp.dma_start(scr[a, n, :, 8 * block:8 * block + 8], (q3, k3)[n][:, part, :])\
                                .then_inc(sem["scr_w"], 16)

                q, k = (0, (0,), (1, 2)), (1, (2,), (0, 1))
                order = (k, q) if a == 2 else (q, k)
                hi, parts = (0, 0) if a == 2 else (now.first["hi"] + 2 * a, now.first["parts"] + 2 * a)
                for count, (n, first, _) in enumerate(order):
                    sp.wait_ge(sem["hi"], at(it, "hi", hi + count + 1))
                    blocks(n, first)
                for count, (n, _, others) in enumerate(order):
                    sp.wait_ge(sem["parts"], at(it, "parts", parts + count + 1))
                    blocks(n, others)

            def load_stack(u):
                a, hf = UNITS[u]
                s = u % 2
                name = sem[f"stk{s}"]
                if now is BEFORE or u == 4:
                    sp.wait_ge(sem["scr_w"], at(it, "scr_w", STORED))
                elif u != 5:
                    sp.wait_ge(sem["ring_full"], at(it, "ring_full", stack_freed(now, u)))
                for n, (t, rows_n) in enumerate(((qst, PART_ROWS + 2), (kst, PART_ROWS))):
                    src = scr[a, n, 8 * hf:8 * hf + 8, 0:rows_n].rearrange("(p g) r t -> g r p t", g=2)
                    for g in range(2):
                        dst = t[:, s, g::2] if n == 0 else t[:, s]
                        sp.dma_start(dst[64 * g:64 * g + rows_n], src[g]).then_inc(name, 16)

            def load_nmax(u, stored=None):
                s = u % 2
                sp.wait_ge(sem["small_free"], at(it, "small_free", now.small[("mrow", u)] + 1))
                for g in range(2):
                    for part in range(2):
                        sp.dma_start(qst[64 * g + 48 + part:64 * g + 49 + part, s, g::2],
                                     nmrow[8 * part + g:8 * part + 8:2, :]).then_inc(sem[f"nmax{s}"], 16)
                    if stored is not None and g == 0:
                        sp.wait_ge(sem["scr_w"], at(it, "scr_w", stored))

            store_parts(0)
            load_stack(0)
            store_parts(1)
            load_nmax(0, stored=2 * STORED)
            with sp.Fori(0, batches) as it:
                now = TURN
                load_stack(1)
                load_nmax(1)
                load_stack(2)
                load_nmax(2)
                load_stack(3)
                load_nmax(3)
                store_parts(2)
                load_stack(4)
                load_stack(5)
                load_nmax(4)
                store_parts(0)
                load_nmax(5, stored=2 * STORED)
                load_stack(0)
                store_parts(1)
                load_nmax(0, stored=3 * STORED)
            sp.wait_ge(sem["nmax0"], before["nmax0"] + batches * per["nmax0"])
            sp.wait_ge(sem["scr_w"], before["scr_w"] + batches * per["scr_w"])

        @block.tensor
        def _(pe):
            pe.wait_ge(first_loads, N_FIRST)
            pe.wait_ge(built, 6)

            now, it = BEFORE, None

            def claim_ring(key):
                n = now.ring[key]
                pe.wait_ge(sem[f"ring_free{n % 2}"], at(it, f"ring_free{n % 2}", 2 * (n // 2)))
                return 2 * (n % 2)

            def claim_max(key):
                n = now.maxima[key]
                pe.wait_ge(sem[f"max_free{n % 2}"], at(it, f"max_free{n % 2}", n // 2))
                return 5 + n % 2

            def claim_small(key):
                pe.wait_ge(sem["small_free"], at(it, "small_free", now.small[key]))

            def drained(*keys):
                for slot in range(2):
                    last = max((now.ring[key] for key in keys if now.ring[key] % 2 == slot), default=None)
                    if last is not None:
                        pe.wait_ge(sem[f"ring_free{slot}"], at(it, f"ring_free{slot}", 2 * (last // 2) + 2))

            def transposes(dst, src, n=TT, width=128):
                for t in range(n):
                    mm = nc.tensor.transpose(dst[0:width, t * 128:(t + 1) * 128], src[:, t, :], ident[:])
                return mm

            def by_rows(dst, lhs, rhs, width=128, k=128):
                for t in range(TT):
                    mm = nc.tensor.matmul(dst[:, t * width:(t + 1) * width], rows_of(lhs, t)[0:k], rhs,
                                          start=True, stop=True)
                return mm

            def row_max(item):
                _, u, tiles = item
                a, hf = UNITS[u]
                s = u % 2
                bank = PS[:, claim_max(item), :]
                c = 0
                for hl, qt in tiles:
                    keys = keys_of(a, qt)
                    mm = nc.tensor.matmul(bank[:, c:c + keys], qst[:, s, hl, qt * 128:(qt + 1) * 128],
                                          kst[:, s, hl // 2, 0:keys], start=True, stop=(a == 2))
                    c += keys
                    if a == 0:
                        w = min(256, keys)
                        mm = nc.tensor.matmul(bank[:, c - w:c], identb[:], biasS[:, 8 * hf + hl, 256 - w:256],
                                              start=False, stop=True)
                    elif a == 1:
                        mm = nc.tensor.matmul(bank[:, c - 128:c], identb[:], causS[:], start=False, stop=True)
                mm.then_inc(sem["max_full"], 1)

            def scores_t(u, g, pair, s):
                a, hf = UNITS[u]
                b = claim_ring(("st", u, g, pair, s))
                for i in range(2):
                    hl = 4 * g + 2 * pair + i
                    for kt, c in steps_of(a)[s]:
                        q0 = first_query(a, kt)
                        n = T - q0
                        mm = nc.tensor.matmul(PS[:, b + i, c:c + n], kst[:, u % 2, 2 * g + pair, kt * 128:(kt + 1) * 128],
                                              qst[:, u % 2, hl, q0:T], start=True, stop=(a != 1))
                        if a == 1:
                            mm = nc.tensor.matmul(PS[:, b + i, c:c + 128], identb[:], causT[:],
                                                  start=False, stop=True)
                mm.then_inc(sem["ring_full"], 1)

            def values(u, g, s):
                a, hf = UNITS[u]
                v = va if a == 0 else vb
                if s == 0:
                    pe.wait_ge(sem["pv_free"], at(it, "pv_free", now.pv[("quad", u, g)]))
                drained(("st", u, g, 0, s), ("st", u, g, 1, s))
                last = steps_of(a)[-1][-1][0]
                for kt, c in steps_of(a)[s]:
                    q0 = first_query(a, kt)
                    n = T - q0
                    for j in range(4):
                        slot = now.tiles[("st", u, g, j // 2, s)] % 4
                        mm = nc.tensor.matmul(PVT[32 * j:32 * j + 32, q0:T], v[:, kt, 8 * hf + 4 * g + j, :],
                                              probs[:, slot, j % 2, c:c + n], start=(kt == 0),
                                              stop=(kt == last), tile_position=(0, 32 * j))
                mm.then_inc(sem["probs_used"], 2)

            def attend(items):
                for item in items:
                    kind, u = item[0], item[1]
                    if kind == "zT":
                        b = claim_ring(item)
                        pe.wait_ge(sem["za"], at(it, "za", 1))
                        transposes(PS[:, b, :], za)
                        pe.wait_ge(sem["zb"], at(it, "zb", 1))
                        transposes(PS[:, b + 1, :], zb).then_inc(sem["ring_full"], 1)
                    elif kind == "qk0":
                        b = claim_ring(item)
                        if (now.ring[item] - now.ring[("zT", 0)]) % 2:
                            drained(("zT", 0))
                        nc.tensor.matmul(PS[:, b, :], W0[:, 0, :], zaT, start=True, stop=True)
                        nc.tensor.matmul(PS[:, b + 1, :], W0[:, 1, :], zaT, start=True, stop=True)\
                            .then_inc(sem["ring_full"], 1)
                    elif kind == "v0":
                        b = claim_ring(item)
                        by_rows(PS[:, b + 1, :], zbT, W1[:, 256:320], width=64)
                        by_rows(PS[:, b, :], zaT, W0[:, 2, :]).then_inc(sem["ring_full"], 1)
                    elif kind == "q1":
                        b = claim_ring(item)
                        nc.tensor.matmul(PS[:, b, :], W1[:, 0:128], zbT, start=True, stop=True)
                        nc.tensor.matmul(PS[:, b + 1, :], W1[:, 128:256], zbT, start=True, stop=True)\
                            .then_inc(sem["ring_full"], 1)
                    elif kind == "latT":
                        claim_small(item)
                        pe.wait_ge(sem["lat"], at(it, "lat", 1))
                        for t in range(TT):
                            mm = nc.tensor.matmul(SM[0:64, t * 128:(t + 1) * 128], lat[:, t, :], ident[:],
                                                  start=True, stop=True)
                        mm.then_inc(sem["small_full"], 1)
                    elif kind == "k1":
                        pe.wait_ge(sem["small_free"], at(it, "small_free", now.small[("latT", 0)] + 1))
                        b = claim_ring(item)
                        nc.tensor.matmul(PS[:, b, :], W1k[:, 0, :], latT[0:64], start=True, stop=True)
                        nc.tensor.matmul(PS[:, b + 1, :], W1k[:, 1, :], latT[0:64], start=True, stop=True)\
                            .then_inc(sem["ring_full"], 1)
                    elif kind == "v1":
                        b = claim_ring(item)
                        by_rows(PS[:, b, :], latT, W1k[:, 2, :], k=64).then_inc(sem["ring_full"], 1)
                    elif kind == "mx":
                        if item == max_items(u)[0]:
                            pe.wait_ge(*stack_ready(it, now, u))
                        row_max(item)
                    elif kind == "mrow":
                        claim_small(item)
                        pe.wait_ge(sem["nmax_parts"], at(it, "nmax_parts", now.nth[u]))
                        for t in range(TT):
                            mm = nc.tensor.transpose(
                                PS[0:16, SMB, :].bitcast(BF16)[:, t * 128:(t + 1) * 128],
                                nmp[:, u % 2, t].rearrange("p a h -> p (a h)"), identb[:])
                        mm.then_inc(sem["small_full"], 1)
                    elif kind == "st":
                        if item[2:] == (0, 0, 0):
                            pe.wait_ge(*nmax_ready(it, now.nth_stack[u] if u else 0, u % 2))
                        scores_t(*item[1:])
                    elif kind == "pv":
                        values(*item[1:])
                    elif kind == "fin":
                        pe.wait_ge(sem["pv_free"], at(it, "pv_free", now.pv[("quad", u, item[2])] + 1))
                        claim_small(item)
                        for t in range(TT):
                            mm = nc.tensor.transpose(SM[:, t * 128:(t + 1) * 128], rows_of(oq, t), ident[:])
                        mm.then_inc(sem["small_full"], 1)
                    elif kind == "woT":
                        claim_small(item)
                        transposes(SM, token_outputs(u)).then_inc(sem["small_full"], 1)
                    elif kind == "wo":
                        claim_small(item)
                        wo = (W0[:, 3, :], W1[:, 320:448], W2[:, 3, :])[u]
                        by_rows(SM, oT, wo).then_inc(sem["small_full"], 1)
                    elif kind == "z2T":
                        claim_small(item)
                        pe.wait_ge(sem["z2"], at(it, "z2", 1))
                        transposes(SM, za).then_inc(sem["small_full"], 1)
                    elif kind == "gate0":
                        claim_small(item)
                        by_rows(SM, z2T, gate0[:], width=E0).then_inc(sem["small_full"], 1)
                    elif kind == "ohT":
                        claim_small(item)
                        pe.wait_ge(sem["onehot"], at(it, "onehot", 1))
                        for t in range(TT):
                            mm = nc.tensor.transpose(SM[0:E0, t * 128:(t + 1) * 128], g0[:, 2, t, :], ident[:])
                        mm.then_inc(sem["small_full"], 1)
                    elif kind == "moe0":
                        n = item[1]
                        if n == 0:
                            claim_max("acc0")
                            pe.wait_ge(sem["small_free"], at(it, "small_free", now.small[("ohT", 0)] + 1))
                            nc.tensor.matmul(ACC0, b2row[:], ohT[:], start=True, stop=False)\
                                .then_inc(sem["max_full"], 1)
                        b = claim_ring(item)
                        for i in range(2):
                            tile = 2 * n + i
                            nc.tensor.matmul(PS[:, b + i, :], sel0[:, tile // TT, :], penT[:], start=True, stop=False)
                            mm = nc.tensor.matmul(PS[:, b + i, :], up0[:, tile, :], z2T, start=False, stop=True)
                        mm.then_inc(sem["ring_full"], 1)
                    elif kind == "down0":
                        n = item[1]
                        drained(("moe0", n))
                        slot = now.tiles[("moe0", n)] % 4
                        for i in range(2):
                            mm = nc.tensor.matmul(ACC0, down0[:, 2 * n + i, :], probs[:, slot, i, :],
                                                  start=False, stop=(2 * n + i == HT - 1))
                        mm.then_inc(sem["probs_used"], 1)
                    elif kind in ("y0", "y1"):
                        if kind == "y0":
                            c = now.maxima["acc0"]
                            pe.wait_ge(sem[f"max_free{c % 2}"], at(it, f"max_free{c % 2}", c // 2 + 1))
                        else:
                            pe.wait_ge(sem["pv_free"], at(it, "pv_free", now.pv["acc1"] + 1))
                        claim_small(item)
                        for t in range(TT):
                            mm = nc.tensor.transpose(SM[:, t * 128:(t + 1) * 128], rows_of(t2, t), ident[:])
                        mm.then_inc(sem["small_full"], 1)
                    elif kind == "combT":
                        claim_small(item)
                        pe.wait_ge(sem["comb"], at(it, "comb", 1))
                        for t in range(TT):
                            mm = nc.tensor.transpose(SM[0:E1, t * 128:(t + 1) * 128], lg[:, 3, t, :], ident[:])
                        mm.then_inc(sem["small_full"], 1)
                    elif kind == "moe1":
                        n = item[1]
                        b = claim_ring(item)
                        gw, uw = (shared[:, 0, :], shared[:, 1, :]) if n == HT else (gw1[:, n, :], uw1[:, n, :])
                        nc.tensor.matmul(PS[:, b, :], gw, hT, start=True, stop=True)
                        nc.tensor.matmul(PS[:, b + 1, :], uw, hT, start=True, stop=True).then_inc(sem["ring_full"], 1)
                    elif kind == "comb":
                        if item[1] == 0:
                            pe.wait_ge(sem["combS"], at(it, "combS", 1))
                        b = claim_max(item)
                        nc.tensor.matmul(PS[:, b, :], sel1[:, item[1], :], combS[:], start=True, stop=True)\
                            .then_inc(sem["max_full"], 1)
                    elif kind == "down1":
                        n = item[1]
                        if n == HT:
                            drained(("moe1", n))
                            pe.wait_ge(sem["pv_free"], at(it, "pv_free", now.pv["acc1"]))
                        else:
                            c = now.maxima[("comb", n)]
                            pe.wait_ge(sem[f"max_free{c % 2}"], at(it, f"max_free{c % 2}", c // 2 + 1))
                        lhs = shared[:, 2, :] if n == HT else dw1[:, n, :]
                        nc.tensor.matmul(PVT, lhs, probs[:, now.tiles[("moe1", n)] % 4, 0, :], start=(n == HT),
                                         stop=(n == HT - 1))\
                            .then_inc(sem["probs_used"], 1)

            attend(FIRST_STAGE)
            pe.wait_ge(bias, BIAS_S)
            pe.wait_ge(loads, N_LOADS)
            attend(FIRST_MAXIMA)
            with pe.Fori(0, batches) as it:
                now = TURN
                attend(LAYER0)

                b = claim_ring("hT")
                pe.wait_ge(sem["xn"], at(it, "xn", 1))
                transposes(PS[:, b, :], xn).then_inc(sem["ring_full"], 1)
                r = now.ring["hT"]
                pe.wait_ge(sem[f"ring_free{r % 2}"], at(it, f"ring_free{r % 2}", 2 * (r // 2) + 1))
                claim_small("gate1")
                by_rows(SM, hT, router[:], width=E1).then_inc(sem["small_full"], 1)
                drained("hT")
                b = claim_ring("hid")
                for i in range(2):
                    mm = nc.tensor.matmul(PS[:, b + i, :], W2[:, 4 + i, :], hmT, start=True, stop=True)
                mm.then_inc(sem["ring_full"], 1)
                drained("hid")
                b = claim_ring("met")
                for i in range(2):
                    mm = nc.tensor.matmul(PS[:, b, :], W2[:, 6 + i, :], h1[:, i, :], start=(i == 0), stop=(i == 1))
                mm.then_inc(sem["ring_full"], 1)
                attend([SHARED])
                b = claim_ring("vT")
                pe.wait_ge(sem["vrow"], at(it, "vrow", 1))
                transposes(PS[:, b, :], zb).then_inc(sem["ring_full"], 1)
                drained("vT")
                b = claim_ring("qk2")
                nc.tensor.matmul(PS[:, b, :], W2[:, 0, :], vT, start=True, stop=True)
                nc.tensor.matmul(PS[:, b + 1, :], W2[:, 1, :], vT, start=True, stop=True)\
                    .then_inc(sem["ring_full"], 1)
                b = claim_ring("v2")
                by_rows(PS[:, b, :], vT, W2[:, 2, :]).then_inc(sem["ring_full"], 1)

                attend(LAYER1)

        @block.scalar
        def _(act):
            act.dma_start(xt[:], x[0].rearrange("(t p) c -> p t c", p=128)).then_inc(sem["x_in"], 16)
            act.wait_ge(first_loads, N_FIRST)
            act.wait_ge(built, 6)

            now, it = BEFORE, None

            def full(key):
                act.wait_ge(sem["ring_full"], at(it, "ring_full", now.ring[key] + 1))
                return 2 * (now.ring[key] % 2), sem[f"ring_free{now.ring[key] % 2}"]

            def small(key):
                act.wait_ge(sem["small_full"], at(it, "small_full", now.small[key] + 1))

            def by_token(dst, src, scale):
                for t in range(TT):
                    last = act.activation(dst[:, t, :], src[:, t, :], ACT.Copy, scale=scale[:, t:t + 1])
                return last

            def v_columns(v):
                return v[:].rearrange("p t h c -> p (t h) c")[:, :, 0:DH]

            def v_source(b):
                return PS[:, b, :].rearrange("p (n d) -> p n d", d=DH)

            def attend(items):
                for item in items:
                    kind, u = item[0], item[1]
                    if kind == "xn":
                        act.wait_ge(sem["rstd"], at(it, "rstd", now.first["rstd"] + 1))
                        act.wait_ge(sem["xn"], at(it, "xn", now.first["xn"] + 1))
                        by_token(za, xn, st[:, 4, :]).then_inc(sem["za"], 1)
                    elif kind == "zT":
                        b, free = full(item)
                        act.activation(zaT, PS[:, b, :], ACT.Identity, scale=gamma, bias=beta).then_inc(free, 1)
                        act.activation(zbT, PS[:, b + 1, :], ACT.Copy, scale=norm1).then_inc(free, 1)
                    elif kind == "qk0":
                        b, _ = full(item)
                        if now is TURN:
                            act.wait_ge(sem["scr_w"], at(it, "scr_w", now.first["scr_w"]))
                        act.activation(q3[:, 0, :], PS[:, b, :], ACT.Copy, scale=RSQ8).then_inc(sem["hi"], 1)
                        act.activation(k3[:, 2, :], PS[:, b + 1, :], ACT.Copy).then_inc(sem["hi"], 1)
                    elif kind == "v0":
                        b, free = full(item)
                        act.activation(lat[:].rearrange("p t c -> p (t c)"), PS[:, b + 1, 0:TT * 64], ACT.Copy)\
                            .then_inc(free, 1)
                        act.activation(v_columns(va), v_source(b), ACT.Copy).then_inc(free, 1)
                    elif kind == "latT":
                        small(item)
                        act.wait_ge(sem["parts"], at(it, "parts", now.first["parts"] + 2))
                        act.activation(latT[0:64], SM[0:64], ACT.Identity, scale=ln_g[0:64], bias=ln_b[0:64])\
                            .then_inc(sem["small_free"], 1)
                    elif kind == "q1hi":
                        act.wait_ge(sem["scr_w"], at(it, "scr_w", now.first["scr_w"] + STORED))
                        act.wait_ge(sem["roped"], at(it, "roped", 1))
                        act.activation(q3[:, 0, :], qf, ACT.Copy).then_inc(sem["hi"], 1)
                    elif kind == "k1hi":
                        act.wait_ge(sem["roped"], at(it, "roped", 2))
                        act.activation(k3[:, 2, :], kf, ACT.Copy).then_inc(sem["hi"], 1)
                    elif kind == "x":
                        act.wait_ge(sem["acc"], at(it, "acc", 1))
                        act.dma_start(xt[:], x[it + 1].rearrange("(t p) c -> p t c", p=128)).then_inc(sem["x_in"], 16)
                    elif kind == "v1":
                        b, free = full(item)
                        act.activation(v_columns(vb), v_source(b), ACT.Copy).then_inc(free, 2)
                    elif kind == "mrow":
                        small(item)
                        if u == 1:
                            act.wait_ge(*nmax_ready(it, 0, 0))
                        elif now is TURN:
                            had = (u - 1) % 6
                            act.wait_ge(*nmax_ready(it, now.nth_stack[had], had % 2))
                        act.activation(nmrow[:], PS[0:16, SMB, :].bitcast(BF16)[:, 0:T], ACT.Copy)\
                            .then_inc(sem["small_free"], 1)
                    elif kind == "st":
                        a = UNITS[u][0]
                        n, w = now.tiles[item], step_width(a, item[4])
                        act.wait_ge(sem["probs_used"], at(it, "probs_used", max(n - 3, 0)))
                        b, free = full(item)
                        if a == 0:
                            act.wait_ge(sem["biased"], at(it, "biased", biased_place(item)))
                        act.activation(probs[:, n % 4, :, 0:w], PS[:, b:b + 2, 0:w], ACT.Exp,
                                       scale=1.0 if a == 0 else RSQ8).then_inc(free, 2)
                    elif kind == "pv" and item[3] == len(steps_of(UNITS[u][0])) - 1:
                        q = now.pv[("quad", u, item[2])]
                        if q >= 1 and now.pv_order[q - 1] != "acc1":
                            act.wait_ge(sem["small_full"], at(it, "small_full", now.small[("fin",) + now.pv_order[q - 1][1:]] + 1))
                        act.wait_ge(sem["probs_used"], at(it, "probs_used", now.tiles[("st", u, item[2], 1, item[3])] + 1))
                        act.activation(oq[:], PVT, ACT.Copy).then_inc(sem["pv_free"], 1)
                    elif kind == "woT":
                        small(item)
                        act.activation(oT[:], SM, ACT.Copy).then_inc(sem["small_free"], 1)
                    elif kind == "wo" and u == 2:
                        act.wait_ge(sem["small_free"], at(it, "small_free", now.small[item] + 1))
                        for t in range(TT):
                            last = act.activation(zb[:, t, 1:], za[:, t, 1:], ACT.Square, accum_out=st[:, 6, t:t + 1])
                        last.then_inc(sem["ssq"], 1)
                    elif kind == "wo" and u == 1:
                        act.wait_ge(sem["small_free"], at(it, "small_free", now.small[item] + 1))
                        for t in range(TT):
                            last = act.activation(za[:, t, :], x2[:, t, :], ACT.Square, accum_out=st[:, 6, t:t + 1])
                        last.then_inc(sem["ssq"], 1)
                        act.wait_ge(sem["rstd"], at(it, "rstd", 1))
                        by_token(za, x2, st[:, 7, :]).then_inc(sem["z2"], 1)
                    elif kind == "z2T":
                        small(item)
                        act.activation(z2T, SM, ACT.Copy, scale=norm2).then_inc(sem["small_free"], 1)
                    elif kind == "moe0" and item[1] % 2 == 0:
                        n, m = item[1], now.tiles[item]
                        act.wait_ge(sem["probs_used"], at(it, "probs_used", m - 3))
                        b, free = full(item)
                        for i in range(2):
                            act.activation(probs[:, m % 4, i, :], PS[:, b + i, :], ACT.Relu, bias=b1e[2 * n + i])\
                                .then_inc(free, 1)
                    elif kind == "y0":
                        act.wait_ge(sem["probs_used"], at(it, "probs_used", now.tiles[("moe0", HT // 2 - 1)] + 1))
                        act.activation(t2, ACC0, ACT.Copy).then_inc(sem["max_free%d" % (now.maxima["acc0"] % 2)], 1)
                    elif kind == "combT":
                        small(item)
                        act.activation(combS[0:E1], SM[0:E1], ACT.Copy).then_inc(sem["comb_hi"], 1)
                    elif kind == "moe1":
                        p = silu_place(item[1])
                        b, _ = full(item)
                        if p == 1:
                            act.wait_ge(sem["combS"], at(it, "combS", 1))
                        elif p == 2:
                            r = now.ring[("moe1", HT)]
                            act.wait_ge(sem[f"ring_free{r % 2}"], at(it, f"ring_free{r % 2}", 2 * (r // 2) + 2))
                        elif p >= 3:
                            c = now.maxima[("comb", p - 3)]
                            act.wait_ge(sem[f"max_free{c % 2}"], at(it, f"max_free{c % 2}", c // 2 + 1))
                        act.activation((t2, rq)[p % 2], PS[:, b, :], ACT.Silu).then_inc(sem["silu"], 1)
                    elif kind == "y1":
                        act.wait_ge(sem["probs_used"], at(it, "probs_used", now.tiles[("moe1", HT - 1)] + 1))
                        act.activation(t2, PVT, ACT.Copy).then_inc(sem["pv_free"], 1)

            attend(FIRST_STAGE)
            act.wait_ge(bias, H)
            act.activation(biasS[:], tab_heads, ACT.Copy).then_inc(bias, 1)
            attend(FIRST_MAXIMA)
            with act.Fori(0, batches) as it:
                now = TURN
                attend(LAYER0)

                b, free = full("hT")
                act.activation(hT, PS[:, b, :], ACT.Copy).then_inc(free, 1)
                act.activation(hmT, PS[:, b, :], ACT.Identity, bias=mu0).then_inc(free, 1)
                small("gate1")
                act.activation(lg[:, 0].rearrange("p t e -> p (t e)"), SM[:, 0:TT * E1], ACT.Exp, scale=-1.0)\
                    .then_inc(sem["small_free"], 1)
                b, free = full("hid")
                for i in range(2):
                    act.activation(h1[:, i, :], PS[:, b + i, :], ACT.Tanh, bias=b1m[i]).then_inc(free, 1)
                b, free = full("met")
                act.activation(t1, PS[:, b, :], ACT.Tanh, bias=b2m).then_inc(free, 2)
                act.wait_ge(sem["logm"], at(it, "logm", 1))
                act.activation(st[:, 10, :], st[:, 9, :], ACT.Ln).then_inc(sem["lns"], 1)
                attend([SHARED])
                b, free = full("vT")
                act.activation(vT, PS[:, b, :], ACT.Copy).then_inc(free, 2)
                b, _ = full("qk2")
                act.wait_ge(sem["scr_w"], at(it, "scr_w", 0))
                act.activation(k3[:, 2, :], PS[:, b + 1, :], ACT.Copy).then_inc(sem["hi"], 1)
                act.wait_ge(sem["metric"], at(it, "metric", 1))
                act.activation(q3[:, 0, :], qf, ACT.Copy).then_inc(sem["hi"], 1)
                b, free = full("v2")
                act.activation(v_columns(vb), v_source(b), ACT.Copy).then_inc(free, 2)

                attend(LAYER1)
            act.wait_ge(sem["x_in"], batches * 16 + 16)

        @block.vector
        def _(dve):
            count = [0]
            dve.wait_ge(first_loads, N_FIRST)
            dve.wait_ge(built, 1)
            now, it = BEFORE, None

            def step(instruction):
                count[0] += 1
                instruction.then_inc(sem["dve"], 1)
                dve.wait_ge(sem["dve"], at(it, "dve", count[0]))

            def full(key):
                dve.wait_ge(sem["ring_full"], at(it, "ring_full", now.ring[key] + 1))
                return 2 * (now.ring[key] % 2), sem[f"ring_free{now.ring[key] % 2}"]

            def small(key):
                dve.wait_ge(sem["small_full"], at(it, "small_full", now.small[key] + 1))

            def statistics(src, width=128):
                for t in range(TT):
                    last = dve.bn_stats(bst[:, t, :], src[:, t, 0:width])
                step(last)
                unfused(nc.vector)
                for t in range(TT):
                    last = dve.bn_aggr(mv[:, t, :], bst[:, t, :])
                last.then_inc(sem["stats"], 1)

            def normalise(dst, src, rstd):
                for t in range(TT):
                    last = dve.tensor_scalar(dst[:, t, :], src[:, t, :], mv[:, t, 0:1], rstd[:, t:t + 1],
                                             ALU.subtract, ALU.mult)
                return last

            def attend(items):
                for item in items:
                    kind, u = item[0], item[1]
                    if kind == "ln":
                        dve.wait_ge(sem["x_in"], at(it, "x_in", 16))
                        statistics(xt)
                    elif kind == "xn":
                        dve.wait_ge(sem["rstd"], at(it, "rstd", now.first["rstd"] + 1))
                        normalise(xn, xt, st[:, 0, :]).then_inc(sem["xn"], 1)
                    elif kind == "qk0":
                        b, free = full(item)
                        dve.wait_ge(sem["hi"], at(it, "hi", now.first["hi"] + 1))
                        dve.scalar_tensor_tensor(rq, PS[:, b, :], RSQ8, q3[:, 0, :], ALU.mult, ALU.subtract)\
                            .then_inc(free, 1)
                        dve.wait_ge(sem["hi"], at(it, "hi", now.first["hi"] + 2))
                        dve.tensor_tensor(rk, PS[:, b + 1, :], k3[:, 2, :], ALU.subtract).then_inc(free, 1)
                    elif kind == "latln":
                        r = now.ring[("v0", 0)]
                        dve.wait_ge(sem[f"ring_free{r % 2}"], at(it, f"ring_free{r % 2}", 2 * (r // 2) + 2))
                        statistics(lat, 64)
                    elif kind == "latn":
                        dve.wait_ge(sem["rstd"], at(it, "rstd", now.first["rstd"] + 2))
                        normalise(lat, lat, st[:, 5, :]).then_inc(sem["lat"], 1)
                    elif kind in ("q1", "k1"):
                        b, free = full(item)
                        if kind == "k1":
                            dve.wait_ge(sem["roped"], at(it, "roped", 1))
                        dve.tensor_tensor(t1, PS[:, b, :], cosT[:], ALU.mult).then_inc(free, 1)
                        dve.tensor_tensor(t2, PS[:, b + 1, :], sinT[:], ALU.mult).then_inc(free, 1)
                    elif kind == "mx":
                        a, n = UNITS[u][0], now.maxima[item]
                        dve.wait_ge(sem["max_full"], at(it, "max_full", n + 1))
                        (hl, qt), (last_hl, last_qt) = item[2][0], item[2][-1]
                        c = 0
                        if qt == last_qt:
                            heads = last_hl - hl + 1
                            last = dve.tensor_reduce(
                                nmax[:, u % 2, qt, hl:hl + heads],
                                PS[:, 5 + n % 2, 0:heads * keys_of(a, qt)].rearrange("p (h k) -> p h k", h=heads),
                                AX.X, ALU.max, negate=True)
                        else:
                            for hl, qt in item[2]:
                                keys = keys_of(a, qt)
                                last = dve.tensor_reduce(nmax[:, u % 2, qt, hl:hl + 1], PS[:, 5 + n % 2, c:c + keys],
                                                         AX.X, ALU.max, negate=True)
                                c += keys
                        last.then_inc(sem[f"max_free{n % 2}"], 1)
                        if item == max_items(u)[-1]:
                            dve.wait_ge(sem[f"max_free{n % 2}"], at(it, f"max_free{n % 2}", n // 2 + 1))
                            dve.wait_ge(sem[f"max_free{(n - 1) % 2}"], at(it, f"max_free{(n - 1) % 2}", (n - 1) // 2 + 1))
                            step(dve.tensor_copy(nmp[:, u % 2, :, 0], nmax[:, u % 2]))
                            dve.tensor_tensor(nmp[:, u % 2, :, 1], nmax[:, u % 2], nmp[:, u % 2, :, 0],
                                              ALU.subtract).then_inc(sem["nmax_parts"], 1)
                    elif kind == "st" and UNITS[u][0] == 0:
                        b, _ = full(item)
                        h = 8 * UNITS[u][1] + 4 * item[2] + 2 * item[3]
                        for kt, c in steps_of(0)[item[4]]:
                            w = min(256, T - first_query(0, kt))
                            last = dve.tensor_tensor(PS[:, b:b + 2, c:c + w], PS[:, b:b + 2, c:c + w],
                                                     biasT[:, h:h + 2, 0:w], ALU.add)
                        last.then_inc(sem["biased"], 1)
                    elif kind == "fin":
                        small(item)
                        ps = SM.rearrange("p (t j c) -> p t j c", t=TT, j=4)
                        step(dve.reciprocal(rcp[:].unsqueeze(3), ps[:, :, :, DH:DH + 1]))
                        c0 = 64 * UNITS[u][1] + 32 * item[2]
                        dve.tensor_tensor(token_outputs(UNITS[u][0])[:, :, c0:c0 + 32].rearrange("p t (j d) -> p t j d", d=DH),
                                          ps[:, :, :, 0:DH], rcp[:].unsqueeze(3).broadcast_to((128, TT, 4, DH)),
                                          ALU.mult).then_inc(sem["small_free"], 1)
                    elif kind == "wo":
                        small(item)
                        if u == 0:
                            dve.wait_ge(sem["acc"], at(it, "acc", 2))
                            dve.tensor_tensor(acc[:], acc[:], SM_rows, ALU.add).then_inc(sem["small_free"], 1)
                        elif u == 1:
                            dve.tensor_tensor(x2[:], xn[:], SM_rows, ALU.add).then_inc(sem["small_free"], 1)
                        else:
                            step(dve.tensor_scalar(za[:], SM_rows, 0.1, 8.0, ALU.mult, ALU.min))
                            dve.tensor_scalar(za[:], za[:], -8.0, None, ALU.max).then_inc(sem["small_free"], 1)
                    elif kind == "gate0":
                        small(item)
                        lg0 = SM[:, 0:TT * E0].rearrange("p (t e) -> p t e", t=TT)
                        dve.tensor_tensor(g0[:, 0], lg0, gate_b.unsqueeze(1).broadcast_to((128, TT, E0)), ALU.add)\
                            .then_inc(sem["small_free"], 1)
                        dve.wait_ge(sem["small_free"], at(it, "small_free", now.small[item] + 1))
                        step(dve.tensor_reduce(gm[:, 0], g0[:, 0], AX.X, ALU.max))
                        step(dve.tensor_tensor(g0[:, 1], g0[:, 0], gm[:, 0].unsqueeze(2).broadcast_to((128, TT, E0)),
                                               ALU.is_equal))
                        step(dve.tensor_tensor(g0[:, 0], g0[:, 1], tie_w.unsqueeze(1).broadcast_to((128, TT, E0)),
                                               ALU.mult))
                        step(dve.tensor_reduce(gm[:, 1], g0[:, 0], AX.X, ALU.max))
                        dve.tensor_tensor(g0[:, 2], g0[:, 0], gm[:, 1].unsqueeze(2).broadcast_to((128, TT, E0)),
                                          ALU.is_equal).then_inc(sem["onehot"], 1)
                    elif kind == "ohT":
                        small(item)
                        step(dve.tensor_copy(ohT[0:E0], SM[0:E0]))
                        dve.tensor_scalar(penT[0:E0], SM[0:E0], -MASKED, MASKED, ALU.mult, ALU.add)\
                            .then_inc(sem["small_free"], 1)
                    elif kind == "moe0" and item[1] % 2 == 1:
                        n, m = item[1], now.tiles[item]
                        dve.wait_ge(sem["probs_used"], at(it, "probs_used", m - 3))
                        b, free = full(item)
                        for i in range(2):
                            dve.tensor_scalar(probs[:, m % 4, i, :], PS[:, b + i, :], b1e[2 * n + i], 0.0,
                                              ALU.add, ALU.max).then_inc(free, 1)
                    elif kind == "y0":
                        small(item)
                        dve.wait_ge(sem["small_free"], at(it, "small_free", now.small[("wo", 0)] + 1))
                        dve.tensor_tensor(acc[:], acc[:], SM_rows, ALU.add).then_inc(sem["small_free"], 1)
                    elif kind == "combT":
                        dve.wait_ge(sem["comb_hi"], at(it, "comb_hi", 1))
                        dve.tensor_tensor(rq[0:E1], SM[0:E1], combS[0:E1], ALU.subtract).then_inc(sem["small_free"], 1)
                        dve.wait_ge(sem["small_free"], at(it, "small_free", now.small[item] + 1))
                        dve.tensor_copy(combS[32:64], rq[0:E1])
                        step(dve.tensor_copy(penT[0:E1], rq[0:E1]))
                        dve.tensor_tensor(combS[64:96], rq[0:E1], penT[0:E1], ALU.subtract).then_inc(sem["combS"], 1)
                    elif kind == "comb" or item == ("moe1", HT):
                        n = item[1]
                        key = ("moe1", n)
                        m, r, s = now.tiles[key], now.ring[key], (t2, rq)[silu_place(n) % 2]
                        dve.wait_ge(sem["silu"], at(it, "silu", silu_place(n) + 1))
                        b, free = full(key)
                        if n == HT:
                            dve.wait_ge(sem["probs_used"], at(it, "probs_used", m - 3))
                            dve.tensor_tensor(probs[:, m % 4, 0, :], s, PS[:, b + 1, :], ALU.mult).then_inc(free, 2)
                            continue
                        dve.tensor_tensor(s, s, PS[:, b + 1, :], ALU.mult).then_inc(free, 2)
                        dve.wait_ge(sem[f"ring_free{r % 2}"], at(it, f"ring_free{r % 2}", 2 * (r // 2) + 2))
                        c = now.maxima[item]
                        dve.wait_ge(sem["max_full"], at(it, "max_full", c + 1))
                        dve.wait_ge(sem["probs_used"], at(it, "probs_used", m - 3))
                        dve.tensor_tensor(probs[:, m % 4, 0, :], s, PS[:, 5 + c % 2, :], ALU.mult)\
                            .then_inc(sem[f"max_free{c % 2}"], 1)
                    elif kind == "y1":
                        small(item)
                        dve.tensor_tensor(acc[:], acc[:], SM_rows, ALU.add).then_inc(sem["small_free"], 1)

            def above_far(table, mask):
                for h in range(H):
                    dve.scalar_tensor_tensor(table[:, h, :], table[:, h, :], rel_far[h], masks[:, mask, :],
                                             ALU.subtract, ALU.add).then_inc(bias, 1)

            attend(FIRST_STAGE)
            dve.wait_ge(rel_in, 48)
            above_far(tab_heads, 1)
            attend(FIRST_MAXIMA)
            dve.wait_ge(rel_in, 64)
            above_far(biasT, 0)
            dve.wait_ge(bias, BIAS_T)
            counted_before["dve"], count[0] = count[0], 0
            with dve.Fori(0, batches) as it:
                now = TURN
                attend(LAYER0)

                dve.wait_ge(sem["small_free"], at(it, "small_free", now.small[("y0", 0)] + 1))
                statistics(acc)
                dve.wait_ge(sem["rstd"], at(it, "rstd", 2))
                normalise(xn, acc, st[:, 0, :]).then_inc(sem["xn"], 1)
                dve.wait_ge(sem["xn"], at(it, "xn", 1))
                step(dve.tensor_scalar(zb[:], xn[:], 8.0, -8.0, ALU.min, ALU.max))
                for t in range(TT):
                    last = dve.tensor_tensor_reduce(out=x2[:, t, 1:], in0=zb[:, t, 1:], in1=zb[:, t, 1:], scale=1.0,
                                                    scalar=0.0, op0=ALU.mult, op1=ALU.add,
                                                    accum_out=st[:, 8, t:t + 1])
                step(last)
                dve.tensor_scalar(st[:, 9, :], st[:, 8, :], 1.0, 1e-6, ALU.add, ALU.add).then_inc(sem["squares"], 1)
                dve.wait_ge(sem["small_free"], at(it, "small_free", now.small["gate1"] + 1))
                step(dve.tensor_scalar(lg[:, 0], lg[:, 0], 1.0, None, ALU.add))
                step(dve.reciprocal(lg[:, 0], lg[:, 0]))
                step(dve.tensor_tensor(lg[:, 1], lg[:, 0], gate_bias.unsqueeze(1).broadcast_to((128, TT, E1)),
                                       ALU.add))
                four = lg[:, 1].rearrange("p t (g e) -> p t g e", e=E1 // GROUPS)
                for n, (i, op) in enumerate(((0, ALU.max), (0, ALU.min), (2, ALU.max), (2, ALU.min))):
                    last = dve.tensor_tensor(gs[:, n].unsqueeze(3), four[:, :, :, i:i + 1], four[:, :, :, i + 1:i + 2], op)
                step(last)
                dve.tensor_tensor(gs[:, 4], gs[:, 0], gs[:, 2], ALU.max)
                dve.tensor_tensor(gs[:, 5], gs[:, 0], gs[:, 2], ALU.min)
                step(dve.tensor_tensor(gs[:, 6], gs[:, 1], gs[:, 3], ALU.max))
                step(dve.tensor_tensor(gs[:, 7], gs[:, 5], gs[:, 6], ALU.max))
                step(dve.tensor_tensor(gs[:, 8], gs[:, 4], gs[:, 7], ALU.add))
                mine = gs[:, 8].unsqueeze(3).broadcast_to((128, TT, GROUPS, GROUPS))
                other = gs[:, 8].unsqueeze(2).broadcast_to((128, TT, GROUPS, GROUPS))
                early = earlier.unsqueeze(1).broadcast_to((128, TT, GROUPS, GROUPS))
                dve.tensor_tensor(gg[:, 0], other, mine, ALU.is_gt)
                step(dve.tensor_tensor(gg[:, 1], other, mine, ALU.is_equal))
                step(dve.tensor_tensor(gg[:, 1], gg[:, 1], early, ALU.mult))
                step(dve.tensor_tensor(gg[:, 0], gg[:, 0], gg[:, 1], ALU.add))
                step(dve.tensor_reduce(gs[:, 9], gg[:, 0], AX.X, ALU.add))
                step(dve.tensor_scalar(gs[:, 9], gs[:, 9], float(TOPG), None, ALU.is_lt))
                step(dve.tensor_tensor(lg[:, 2].rearrange("p t (g e) -> p t g e", e=E1 // GROUPS), four,
                                       gs[:, 9].unsqueeze(3).broadcast_to((128, TT, GROUPS, E1 // GROUPS)), ALU.mult))
                dve.wait_ge(sem["logm"], at(it, "logm", 2))
                step(dve.reciprocal(st[:, 12, :], st[:, 12, :]))
                step(dve.tensor_tensor(st[:, 13, :], st[:, 11, :], st[:, 12, :], ALU.mult))
                for t in range(TT):
                    last = dve.tensor_scalar(zb[:, t, :], zb[:, t, :], st[:, 13, t:t + 1], None, ALU.mult)
                step(last)
                dve.tensor_tensor(zb[:, :, 0:1], st[:, 13, :].unsqueeze(2), st[:, 14, :].unsqueeze(2), ALU.mult)\
                    .then_inc(sem["vrow"], 1)
                attend([SHARED])
                unfused(nc.vector)
                for t in range(TT):
                    last = dve.max(top[:, t, :], lg[:, 2, t, :])
                step(last)
                unfused(nc.vector)
                for t in range(TT):
                    last = dve.match_replace(lg[:, 1, t, :], top[:, t, :], lg[:, 2, t, :], MASKED)
                step(last)
                step(dve.tensor_scalar(lg[:, 2], lg[:, 1], MASKED, None, ALU.is_equal))
                step(dve.tensor_tensor(lg[:, 2], lg[:, 2], lg[:, 0], ALU.mult))
                step(dve.tensor_reduce(gm[:, 0], lg[:, 2], AX.X, ALU.add))
                step(dve.tensor_scalar(gm[:, 0], gm[:, 0], 1e-20, None, ALU.add))
                step(dve.reciprocal(gm[:, 1], gm[:, 0]))
                step(dve.tensor_tensor(lg[:, 2], lg[:, 2], gm[:, 1].unsqueeze(2).broadcast_to((128, TT, E1)), ALU.mult))
                dve.tensor_scalar(lg[:, 3], lg[:, 2], 2.5, None, ALU.mult).then_inc(sem["comb"], 1)
                met = now.ring["met"]
                dve.wait_ge(sem[f"ring_free{met % 2}"], at(it, f"ring_free{met % 2}", 2 * (met // 2) + 2))
                step(dve.tensor_scalar(t1, t1, 0.1, eta, ALU.mult, ALU.add))
                b, free = full("qk2")
                dve.tensor_tensor(qf, PS[:, b, :], t1, ALU.mult).then_inc(sem["metric"], 1)
                dve.wait_ge(sem["hi"], at(it, "hi", 1))
                dve.tensor_tensor(rk, PS[:, b + 1, :], k3[:, 2, :], ALU.subtract).then_inc(free, 2)

                attend(LAYER1)
            counted["dve"] = count[0]

        @block.gpsimd
        def _(pool):
            count = [0]
            for n, c in enumerate(CONSTANTS):
                last = pool.memset(const[:, n, :], c)
            last.then_inc(built, 1)
            pool.memset(qst[:], 0.0).then_inc(built, 1)
            pool.memset(kst[:], 0.0).then_inc(built, 1)
            pool.memset(b2row[:], 0.0).then_inc(built, 1)
            for t in (va, vb):
                pool.memset(t[:], 0.0)
            pool.memset(ohT[:], 0.0)
            pool.memset(penT[:], 0.0)
            pool.memset(combS[:], 0.0)
            pool.memset(st[:], 0.0).then_inc(built, 1)
            pool.wait_ge(built, 5)
            for t in (va, vb):
                last = pool.memset(t[:].rearrange("p t h c -> p (t h) c")[:, :, DH:DH + 1], 1.0)
            last.then_inc(built, 1)
            pool.wait_ge(built, 6)
            for name in PRIMED:
                pool.sem_inc(sem[name], 1)

            now, it = BEFORE, None

            def step(instruction):
                count[0] += 1
                instruction.then_inc(sem["pool"], 1)
                pool.wait_ge(sem["pool"], at(it, "pool", count[0]))

            def with_constant(dst, src, op, c):
                return pool.tensor_tensor(dst, src, const[:, CONSTANTS.index(c), :], op)

            def add(dst, src, c):
                return with_constant(dst, src, ALU.add, c)

            def at_least(dst, src, c):
                unfused(nc.gpsimd)
                return pool.tensor_scalar(dst, src, c, None, ALU.max)

            def power(dst, src, c):
                return with_constant(dst, src, ALU.pow, c)

            def sum_power(dst, src, c, exponent):
                step(add(dst, src, c))
                return power(dst, dst, exponent)

            def parts(dst, mid, lo, rest):
                unfused(nc.gpsimd)
                step(pool.tensor_copy(dst[:, mid, :], rest))
                pool.tensor_tensor(dst[:, lo, :], rest, dst[:, mid, :], ALU.subtract)\
                    .then_inc(sem["parts"], 1)

            S = [st[:, n, :] for n in range(16)]
            def first_stage():
                pool.wait_ge(sem["stats"], at(it, "stats", now.first["stats"] + 1))
                step(sum_power(S[0], mv[:, :, 1], 1e-5, -0.5))
                step(pool.tensor_tensor(S[2], S[0], S[0], ALU.mult))
                step(pool.tensor_tensor(S[3], S[2], mv[:, :, 1], ALU.mult))
                step(sum_power(S[4], S[3], 1e-5, -0.5))
                sum_power(S[2], S[3], 1e-6, -0.5).then_inc(sem["rstd"], 1)
                pool.wait_ge(sem["rstd"], at(it, "rstd", now.first["rstd"] + 1))
                pool.wait_ge(sem["xn"], at(it, "xn", now.first["xn"] + 1))
                unfused(nc.gpsimd)
                for t in range(TT):
                    last = pool.tensor_scalar(zb[:, t, :], xn[:, t, :], S[2][:, t:t + 1], None, ALU.mult)
                last.then_inc(sem["zb"], 1)
                qk0 = now.ring[("qk0", 0)]
                pool.wait_ge(sem[f"ring_free{qk0 % 2}"], at(it, f"ring_free{qk0 % 2}", 2 * (qk0 // 2) + 2))
                parts(q3, 1, 2, rq)
                parts(k3, 1, 0, rk)
                pool.wait_ge(sem["stats"], at(it, "stats", now.first["stats"] + 2))
                sum_power(S[5], mv[:, :, 1], 1e-5, -0.5).then_inc(sem["rstd"], 1)
                for n, (key, full, first, p3, mid, lo) in enumerate(((("q1", 0), qf, 0, q3, 1, 2), (("k1", 0), kf, 2, k3, 1, 0))):
                    r = now.ring[key]
                    pool.wait_ge(sem[f"ring_free{r % 2}"], at(it, f"ring_free{r % 2}", 2 * (r // 2) + 2))
                    pool.tensor_tensor(full, t1, t2, ALU.add).then_inc(sem["roped"], 1)
                for n, (full, first, p3, mid, lo) in enumerate(((qf, 0, q3, 1, 2), (kf, 2, k3, 1, 0))):
                    pool.wait_ge(sem["hi"], at(it, "hi", now.first["hi"] + 3 + n))
                    step(pool.tensor_tensor(full, full, p3[:, first, :], ALU.subtract))
                    parts(p3, mid, lo, full)

            first_stage()
            counted_before["pool"], count[0] = count[0], 0
            with pool.Fori(0, batches) as it:
                now = TURN
                pool.wait_ge(sem["xn"], at(it, "xn", 0))
                pool.tensor_tensor(acc[:], xt[:], xn[:], ALU.add).then_inc(sem["acc"], 1)
                pool.wait_ge(sem["ssq"], at(it, "ssq", 1))
                step(with_constant(S[7], S[6], ALU.mult, 1.0 / D))
                sum_power(S[7], S[7], 1e-6, -0.5).then_inc(sem["rstd"], 1)
                pool.tensor_tensor(acc[:], acc[:], x2[:], ALU.add).then_inc(sem["acc"], 1)
                pool.wait_ge(sem["stats"], at(it, "stats", 1))
                sum_power(S[0], mv[:, :, 1], 1e-5, -0.5).then_inc(sem["rstd"], 1)
                pool.wait_ge(sem["squares"], at(it, "squares", 1))
                step(power(S[9], S[9], 0.5))
                step(at_least(S[10], S[9], 1.0 + 1e-6))
                pool.tensor_tensor(S[14], S[9], S[10], ALU.subtract)
                add(S[11], S[10], -1.0)
                step(add(S[12], S[10], 1.0))
                step(pool.tensor_tensor(S[11], S[11], S[12], ALU.mult))
                step(power(S[11], S[11], 0.5))
                pool.tensor_tensor(S[9], S[11], S[10], ALU.add).then_inc(sem["logm"], 1)
                step(pool.tensor_tensor(S[12], S[14], S[14], ALU.mult))
                step(pool.tensor_tensor(S[12], S[8], S[12], ALU.subtract))
                step(at_least(S[12], S[12], 1e-6))
                step(power(S[12], S[12], 0.5))
                step(add(S[12], S[12], 1e-6))
                pool.wait_ge(sem["lns"], at(it, "lns", 1))
                at_least(S[11], S[10], 1e-3).then_inc(sem["logm"], 1)
                r = now.ring["qk2"]
                pool.wait_ge(sem[f"ring_free{r % 2}"], at(it, f"ring_free{r % 2}", 2 * (r // 2) + 2))
                parts(k3, 1, 0, rk)
                pool.wait_ge(sem["hi"], at(it, "hi", 2))
                step(pool.tensor_tensor(qf, qf, q3[:, 0, :], ALU.subtract))
                parts(q3, 1, 2, qf)
                first_stage()
                pool.wait_ge(sem["ssq"], at(it, "ssq", 2))
                step(add(S[9], S[6], 1.0))
                step(sum_power(S[9], S[9], 1e-6, 0.5))
                pool.tensor_tensor(acc[:, :, 1:], acc[:, :, 1:], za[:, :, 1:], ALU.add)
                pool.tensor_tensor(acc[:, :, 0:1], acc[:, :, 0:1], S[9].unsqueeze(2), ALU.add).then_inc(sem["summed"], 1)
                pool.wait_ge(sem["summed"], at(it, "summed", 1))
                pool.dma_start(out[it].rearrange("(t p) c -> p t c", p=128), acc[:]).then_inc(sem["out_done"], 16)
                pool.wait_ge(sem["out_done"], at(it, "out_done", 16))
            counted["pool"] = count[0]
    return counted_before, counted


def _host(x):
    f, bf = np.float32, mybir.dt.np(BF16)
    con = np.ascontiguousarray
    i = {k: np.asarray(v) for k, v in x.items()}
    t = lambda w: w.T
    swap = np.array([h * DH + (d + DH // 2) % DH for h in range(H) for d in range(DH)])
    pad = lambda v, n=128: np.concatenate([v, np.zeros(n - v.shape[0], f)])
    mq = t(i["L0_ffn_Wq"])
    uk = t(i["L0_ffn_Wuk"])
    stack = lambda *w: con(np.stack(w, 1))
    tiles = lambda w: con(w.reshape(-1, 128, w.shape[-1]).transpose(1, 0, 2))
    w2 = t(i["L1_attn_W2"])
    w1 = t(i["L1_attn_W1"])
    rel = i["L0_attn_rel"]
    p = np.arange(128)[:, None]
    c = np.arange(256)[None, :]
    far = rel.shape[1] - 1
    eta = np.ones(D, f)
    eta[0] = -1
    mu = np.zeros(D, f)
    mu[0] = -1
    cols = [i["L0_attn_ln_gamma"], i["L0_attn_ln_beta"], i["L0_ffn_norm1_w"], i["L0_ffn_norm2_w"],
            pad(i["L0_ffn_ln_g"]), pad(i["L0_ffn_ln_b"]), i["L1_attn_b2"], eta, mu,
            i["L1_attn_b1"][:128], i["L1_attn_b1"][128:]]
    cols += [np.broadcast_to(rel[h, far], (128,)) for h in range(H)]
    cols += list(i["L0_ffn_b1"].reshape(HT, 128))
    tri = (np.arange(GROUPS)[None, :] < np.arange(GROUPS)[:, None]).astype(f).ravel()
    rows = np.concatenate([i["L0_ffn_gate_b"], np.arange(E0, 0, -1).astype(f), i["L1_ffn_gate_bias"], tri])
    half = DH // 2
    freq = (f(1.0) / f(10000.0) ** (np.arange(half, dtype=f) / f(half))).astype(f)
    ang = np.arange(T, dtype=f)[None, :] * freq[:, None]
    cos, sin = np.cos(ang).astype(f), np.sin(ang).astype(f)
    pick0 = np.zeros((128, E0, 128), f)
    for e in range(E0):
        pick0[e, e] = 1
    pick1 = np.zeros((128, HT, 128), f)
    for n in range(HT):
        for part in range(3):
            pick1[32 * part + 2 * n, n, :64] = 1
            pick1[32 * part + 2 * n + 1, n, 64:] = 1
    sq = np.arange(128)
    return dict(
        x=con(np.concatenate([i["L0_attn_x"], np.zeros((1, T, D), f)])),
        w0=stack(*(t(i["L0_attn_" + n]) for n in ("Wq", "Wk", "Wv", "Wo"))),
        w1=con(np.concatenate([mq, mq[:, swap], t(i["L0_ffn_Wdkv"]), t(i["L0_ffn_Wo"])], 1)),
        w1k=stack(uk, uk[:, swap], t(i["L0_ffn_Wuv"])),
        w2=stack(*(t(i["L1_attn_" + n]) for n in ("Wq", "Wk", "Wv", "Wo")), w1[:, :128], w1[:, 128:],
                 w2[:128], w2[128:]),
        m0_up=con(t(i["L0_ffn_W1"].reshape(HID0, D)).reshape(D, HT, 128)),
        m0_down=tiles(i["L0_ffn_W2"].transpose(0, 2, 1).reshape(HID0, D)),
        m0_b2=con(i["L0_ffn_b2"]), m0_gate=con(t(i["L0_ffn_gate_w"])),
        m1_gate_w=con(t(i["L1_ffn_w_gate"].reshape(HID0, D)).reshape(D, HT, 128)),
        m1_up_w=con(t(i["L1_ffn_w_up"].reshape(HID0, D)).reshape(D, HT, 128)),
        m1_down_w=tiles(i["L1_ffn_w_down"].transpose(0, 2, 1).reshape(HID0, D)),
        m1_shared=stack(*(t(i["L1_ffn_" + n]) for n in ("sh_gate", "sh_up", "sh_down"))),
        m1_router=con(t(i["L1_ffn_gate_w"])),
        cols=con(np.stack(cols, 1)), rows=con(np.broadcast_to(rows, (128, rows.shape[0]))),
        rel_t=con(rel[:, np.clip(c - p, 0, far)].transpose(1, 0, 2).reshape(128, -1)),
        rel_s=con(rel[:, np.clip(128 + p - c, 0, far)].transpose(1, 0, 2).reshape(128, -1)),
        mask_t=np.where(c < p, MASKED, 0).astype(f), mask_s=np.where(c > 128 + p, MASKED, 0).astype(f),
        causal_t=np.where(sq[None] < sq[:, None], MASKED, 0).astype(bf),
        causal_s=np.where(sq[None] > sq[:, None], MASKED, 0).astype(bf),
        rope_cos=con(np.tile(np.concatenate([cos, cos]), (H, 1))),
        rope_sin=con(np.tile(np.concatenate([-sin, sin]), (H, 1))),
        eye=np.eye(128, dtype=f), eye_b=np.eye(128).astype(bf), pick0=pick0.astype(bf), pick1=pick1.astype(bf),
        ones2=np.ones((2, 4, T), bf), zeros2=np.zeros((H, 2, T), bf),
    )


def kernel(**inputs):
    from concourse import bacc as _bacc
    from concourse.bass_utils import run_bass_kernel_spmd as _run

    nc = _bacc.Bacc("TRN2", target_bir_lowering=False, num_devices=1)
    arrays = _host(inputs)
    b = arrays["x"].shape[0] - 1
    args = {n: nc.dram_tensor(f"in_{n}", a.shape, mybir.dt.from_np(a.dtype), kind="ExternalInput").ap()
            for n, a in arrays.items()}
    out = nc.dram_tensor("out_0", (b, T, D), F32, kind="ExternalOutput").ap()
    layers_kernel(nc, b, out=out, before=BEFORE.raised, per=TURN.raised, **args)
    r = _run(nc, [{f"in_{n}": a for n, a in arrays.items()}], core_ids=[0])
    return r.results[0]["out_0"]
```
